# Optimizing a Trainium2 kernel written in Bass

```python
import numpy as np
import jax
import jax.numpy as jnp

def _softmax(x, axis=-1):
    return jax.nn.softmax(x, axis=axis)

def _gelu(x):
    return jax.nn.gelu(x, approximate=True)

def _silu(x):
    return jax.nn.silu(x)

def _sigmoid(x):
    return jax.nn.sigmoid(x)

def _layernorm(x, axis=-1, eps=1e-05):
    m = jnp.mean(x, axis=axis, keepdims=True)
    v = jnp.var(x, axis=axis, keepdims=True)
    return (x - m) / jnp.sqrt(v + eps)

def _scatter_add(tgt, idx, src, axis=0):
    return tgt.at[idx].add(src)

def _segment_sum(src, seg, n):
    return jax.ops.segment_sum(src, seg, n)
kernel_name = 'mk_decoder_postln_d1_seqx_r8_2ad802'

def setup_inputs(seed: int=0):
    np.random.seed(seed)
    _w = jnp.asarray

    def _rec_inputs():
        import jax
        import jax.numpy as jnp
        _rk = jax.random.key(seed)
        x = 7.22e-05 + 1 * jax.random.normal(jax.random.fold_in(_rk, 1), (32, 128, 128), jnp.float32)
        _lenS = 128 - jax.random.randint(jax.random.fold_in(_rk, 7), (32,), 0, max(1, 128 // 4) + 1, jnp.int32)
        _lenS2 = 77 - jax.random.randint(jax.random.fold_in(_rk, 8), (32,), 0, max(1, 77 // 4) + 1, jnp.int32)
        _ctx_1024P = jax.random.normal(jax.random.fold_in(_rk, 11), (32, 16, 128), jnp.float32)
        _ctx_1024c = jax.random.dirichlet(jax.random.fold_in(_rk, 511), 0.3 * jnp.ones((16,), jnp.float32), (32, 77))
        _ctx_1024t = jnp.einsum('bsk,bkd->bsd', _ctx_1024c, _ctx_1024P)
        _ctx_1024t = _ctx_1024t * jax.lax.rsqrt(jnp.mean(jnp.square(_ctx_1024t)) + 1e-12) * 0.953939
        ctx_1024 = 4.13588e-05 + 0.999923 * (_ctx_1024t + 0.3 * jax.random.normal(jax.random.fold_in(_rk, 611), (32, 77, 128), jnp.float32))
        return (x, ctx_1024)
    x, ctx_1024 = _rec_inputs()

    def _L0_attn_setup():
        import jax, jax.numpy as jnp
        import numpy as np
        E = 128
        D = 64
        H = E // D
        EPS = 1e-05
        key = jax.random.key(seed)
        ks = jax.random.split(key, 8)
        std = 0.02
        x = jax.random.normal(ks[0], (2, 128, E), jnp.float32)
        Wq = jax.random.normal(ks[1], (E, E), jnp.float32) * std
        Wk = jax.random.normal(ks[2], (E, E), jnp.float32) * std
        Wv = jax.random.normal(ks[3], (E, E), jnp.float32) * std
        Wo = jax.random.normal(ks[4], (E, E), jnp.float32) * std
        delta = jnp.full((E,), float(np.log(0.99 / 0.01)), jnp.float32)
        G1 = jax.random.normal(ks[5], (E, D), jnp.float32) * std
        G2 = jax.random.normal(ks[6], (D, E), jnp.float32) * std
        norm_w = jnp.ones((E,), jnp.float32)
        return {'x': x, 'Wq': Wq, 'Wk': Wk, 'Wv': Wv, 'Wo': Wo, 'delta': delta, 'G1': G1, 'G2': G2, 'norm_w': norm_w}
    _L0_attn_all = _L0_attn_setup()
    _L0_attn_in = {k: v for k, v in _L0_attn_all.items() if k in ('Wq', 'Wk', 'Wv', 'Wo', 'delta', 'G1', 'G2', 'norm_w')}
    del _L0_attn_all

    def _L0_xattn_setup():
        import jax, jax.numpy as jnp
        import numpy as np
        N_HEAD = 16
        key = jax.random.key(seed)
        ks = jax.random.split(key, 5)
        b, l, d = (4, 256, 128)
        dh = d // N_HEAD
        return {'q': jax.random.normal(ks[0], (b, l, d), dtype=jnp.float32), 'kv': jax.random.normal(ks[1], (b, l, d), dtype=jnp.float32), 'Wq': jax.random.normal(ks[2], (d, d), dtype=jnp.float32) * 0.02, 'Wkv': jax.random.normal(ks[3], (2 * dh, d), dtype=jnp.float32) * 0.02, 'Wc': jax.random.normal(ks[4], (d, d), dtype=jnp.float32) * 0.02}
    _L0_xattn_all = _L0_xattn_setup()
    _L0_xattn_in = {k: v for k, v in _L0_xattn_all.items() if k in ('Wq', 'Wkv', 'Wc')}
    del _L0_xattn_all

    def _L0_ffn_setup():
        import jax, jax.numpy as jnp
        import numpy as np
        E = 16
        K = 4
        B, S, H, I = (4, 128, 128, 256)
        key = jax.random.key(seed)
        k0, k1, k2, k3 = jax.random.split(key, 4)
        scale = 0.02
        return {'hidden_states': jax.random.normal(k0, (B, S, H), jnp.float32), 'router_w': jax.random.normal(k1, (H, E), jnp.float32) * scale, 'router_b': jnp.zeros((E,), jnp.float32), 'w1': jax.random.normal(k2, (E, H, I), jnp.float32) * scale, 'b1': jnp.zeros((E, I), jnp.float32), 'w2': jax.random.normal(k3, (E, I, H), jnp.float32) * scale, 'b2': jnp.zeros((E, H), jnp.float32)}
    _L0_ffn_all = _L0_ffn_setup()
    _L0_ffn_in = {k: v for k, v in _L0_ffn_all.items() if k in ('router_w', 'router_b', 'w1', 'b1', 'w2', 'b2')}
    del _L0_ffn_all
    return {'x': x, 'ctx_1024': ctx_1024, 'L0_attn_Wq': _L0_attn_in['Wq'], 'L0_attn_Wk': _L0_attn_in['Wk'], 'L0_attn_Wv': _L0_attn_in['Wv'], 'L0_attn_Wo': _L0_attn_in['Wo'], 'L0_attn_delta': _L0_attn_in['delta'], 'L0_attn_G1': _L0_attn_in['G1'], 'L0_attn_G2': _L0_attn_in['G2'], 'L0_attn_norm_w': _L0_attn_in['norm_w'], 'L0_xattn_Wq': _L0_xattn_in['Wq'], 'L0_xattn_Wkv': _L0_xattn_in['Wkv'], 'L0_xattn_Wc': _L0_xattn_in['Wc'], 'L0_ffn_router_w': _L0_ffn_in['router_w'], 'L0_ffn_router_b': _L0_ffn_in['router_b'], 'L0_ffn_w1': _L0_ffn_in['w1'], 'L0_ffn_b1': _L0_ffn_in['b1'], 'L0_ffn_w2': _L0_ffn_in['w2'], 'L0_ffn_b2': _L0_ffn_in['b2']}

def reference(x, ctx_1024, L0_attn_Wq, L0_attn_Wk, L0_attn_Wv, L0_attn_Wo, L0_attn_delta, L0_attn_G1, L0_attn_G2, L0_attn_norm_w, L0_xattn_Wq, L0_xattn_Wkv, L0_xattn_Wc, L0_ffn_router_w, L0_ffn_router_b, L0_ffn_w1, L0_ffn_b1, L0_ffn_w2, L0_ffn_b2):
    import jax
    import jax.numpy as jnp

    def _L0_attn_ref(x, Wq, Wk, Wv, Wo, delta, G1, G2, norm_w):
        import jax, jax.numpy as jnp
        import numpy as np
        E = 128
        D = 64
        H = E // D
        EPS = 1e-05
        B, T, _ = x.shape
        q = jax.nn.silu(x @ Wq)
        v = x @ Wv
        log_f = jax.nn.log_sigmoid(x @ Wk + delta)
        k = -jnp.expm1(log_f)

        def to_tbhd(a):
            return a.reshape(B, T, H, D).transpose(1, 0, 2, 3)
        qh, kh, vh, gh = map(to_tbhd, (q, k, v, log_f))
        S0 = jnp.zeros((B, H, D, D), x.dtype)

        def step(S, inp):
            q_t, k_t, v_t, g_t = inp
            S = S * jnp.exp(g_t)[..., None] + k_t[..., None] * v_t[..., None, :]
            o_t = jnp.einsum('bhk,bhkv->bhv', q_t, S)
            return (S, o_t)
        _, o = jax.lax.scan(step, S0, (qh, kh, vh, gh))
        o = o.transpose(1, 0, 2, 3).reshape(B, T, E)
        gate = x @ G1 @ G2
        o = o * jax.nn.sigmoid(gate)
        og = o.reshape(B, T, H, D)
        og = og * jax.lax.rsqrt(jnp.mean(og * og, axis=-1, keepdims=True) + EPS)
        o = og.reshape(B, T, E) * norm_w
        return o @ Wo

    def _L0_xattn_ref(q, kv, Wq, Wkv, Wc):
        import jax, jax.numpy as jnp
        import numpy as np
        N_HEAD = 16
        b, l, d = q.shape
        h = N_HEAD
        dh = d // h
        qp = jnp.einsum('bld,ed->ble', q, Wq)
        scores = jnp.einsum('bld,bmd->blm', qp, kv)
        idx = jnp.argmax(scores, axis=-1)
        mem = jnp.take_along_axis(kv, idx[..., None], axis=1)
        mkv = jnp.einsum('bld,ed->ble', mem, Wkv)
        mk, mv = jnp.split(mkv, 2, axis=-1)
        qh = qp.reshape(b, l, h, dh).transpose(0, 2, 1, 3)
        scale = 1.0 / np.sqrt(dh).astype(np.float32)
        logits = jnp.einsum('bhld,bmd->bhlm', qh, mk) * scale
        attn = jax.nn.softmax(logits, axis=-1)
        out = jnp.einsum('bhlm,bmd->bhld', attn, mv)
        out = out.transpose(0, 2, 1, 3).reshape(b, l, d)
        return jnp.einsum('bld,ed->ble', out, Wc)

    def _L0_ffn_ref(hidden_states, router_w, router_b, w1, b1, w2, b2):
        import jax, jax.numpy as jnp
        import numpy as np
        E = 16
        K = 4
        B, S, H, I = (4, 128, 128, 256)
        b, s, h = hidden_states.shape
        logits = hidden_states @ router_w + router_b
        probs = jax.nn.softmax(logits, axis=-1)
        topw, topi = jax.lax.top_k(probs, K)
        topw = topw / jnp.sum(topw, axis=-1, keepdims=True)
        combine = jnp.sum(jax.nn.one_hot(topi, E, dtype=hidden_states.dtype) * topw[..., None], axis=2)
        x = hidden_states.reshape(b * s, h)
        c = combine.reshape(b * s, E)

        def body(acc, expert):
            w1e, b1e, w2e, b2e, ce = expert
            hmid = jax.nn.gelu(x @ w1e + b1e, approximate=False)
            return (acc + (hmid @ w2e + b2e) * ce[:, None], None)
        out, _ = jax.lax.scan(body, jnp.zeros_like(x), (w1, b1, w2, b2, c.T))
        return out.reshape(b, s, h)
    x = _layernorm(x + _L0_attn_ref(x, L0_attn_Wq, L0_attn_Wk, L0_attn_Wv, L0_attn_Wo, L0_attn_delta, L0_attn_G1, L0_attn_G2, L0_attn_norm_w), axis=-1)
    x = _layernorm(x + _L0_xattn_ref(x, ctx_1024, L0_xattn_Wq, L0_xattn_Wkv, L0_xattn_Wc), axis=-1)
    x = _layernorm(x + _L0_ffn_ref(x, L0_ffn_router_w, L0_ffn_router_b, L0_ffn_w1, L0_ffn_b1, L0_ffn_w2, L0_ffn_b2), axis=-1)
    return x

_drawn_inputs = setup_inputs


def setup_inputs(seed=0):
    import zlib

    import numpy as np

    out = dict(_drawn_inputs(seed))
    spreads = {'L0_attn_delta': (4.595119953155518, 0.2),
     'L0_attn_norm_w': (1.0, 0.2),
     'L0_ffn_router_b': (0.0, 0.1),
     'L0_ffn_b1': (0.0, 0.8),
     'L0_ffn_b2': (0.0, 0.1)}
    factors = {'L0_attn_G1': 8.0,
     'L0_attn_G2': 8.0,
     'L0_xattn_Wq': 7.953,
     'L0_ffn_w1': 3.013,
     'L0_ffn_w2': 2.714}
    for name, (base, spread) in spreads.items():
        noise = np.random.default_rng([zlib.crc32(name.encode()), seed]).standard_normal(out[name].shape)
        drawn = base * np.exp(spread * noise) if base else spread * noise
        out[name] = jnp.asarray(drawn.astype(out[name].dtype))
    for name, factor in factors.items():
        out[name] = (out[name] * factor).astype(out[name].dtype)
    return out
```

```python
from contextlib import ExitStack

import concourse.bacc as _bacc
import concourse.mybir as _mybir
import numpy as np
from concourse.bass_utils import run_bass_kernel_spmd as _run


def build(nc, A, out):
    import concourse.bass as bass
    from concourse import mybir

    ALU = mybir.AluOpType
    ACT = mybir.ActivationFunctionType
    AX = mybir.AxisListType
    F32 = mybir.dt.float32
    U32 = mybir.dt.uint32
    F16 = mybir.dt.float16

    P = 128
    E = 128
    B = A["x"].shape[1]
    T = 128
    GB = 4
    GC = GB * T
    NG = B // GB
    H = 2
    DH = E // H
    HALVES = [64, 32, 16, 8]
    NL = len(HALVES)
    LEAF = 8
    FLOOR = 20.0
    EPS = 1e-5

    with ExitStack() as ctx:
        def sb(name, shape, dt=F32):
            return ctx.enter_context(nc.sbuf_tensor(name, shape, dt))

        def sem(name):
            return ctx.enter_context(nc.semaphore(name))

        banks = [ctx.enter_context(nc.psum_tensor(f"bank{i}", [P, 512], F32)) for i in range(8)]

        X = sb("X", [P, B, E])
        wk, wq, wv, wo = (sb(n, [P, E]) for n in ("wk", "wq", "wv", "wo"))
        g1 = sb("g1", [P, DH])
        g2 = sb("g2", [DH, E])
        delta = sb("delta", [P, 1])
        norm_w = sb("norm_w", [P, 1])
        won = sb("won", [P, E])
        ident = sb("ident", [P, P])
        restart = sb("restart", [P, GC])
        lmask = [sb(f"lmask{h}", [P, 64]) for h in HALVES]
        leafmask = sb("leafmask", [P, P])

        xTg = [sb(f"xTg{p}", [P, GC]) for p in range(2)]
        uS, soft, kk, k, qc, sq_, q, N, gc, sg_ = (sb(n, [P, GC]) for n in ("uS", "soft", "kk", "k", "qc", "sigq", "q", "N", "gc", "lgate"))
        gate = [sb(f"gate{p}", [P, GC]) for p in range(2)]
        v = [sb(f"v{p}", [P, GC]) for p in range(2)]
        zT = sb("zT", [DH, GC])
        dec = [sb(f"dec{l}", [P, GC]) for l in range(NL + 1)]
        decK = sb("decK", [P, GC])
        Lk = [sb(f"Lk{l}", [P, GC]) for l in range(NL + 1)]
        Rq = [sb(f"Rq{l}", [P, GB, H, T // 2]) for l in range(NL)]
        Rleaf = sb("Rleaf", [P, GB, H, T])
        AT = sb("AT", [P, GB, H, T])
        og, osq, on, oT, r1 = (sb(n, [P, GC]) for n in ("og", "osq", "on", "oT", "r1"))
        ss, lss, rss = (sb(n, [P, GB * H]) for n in ("ss", "lss", "rss"))
        st1 = sb("st1", [P, GB, 6])
        mv1 = sb("mv1", [P, GB, 2])
        ln1, rs1, nm1 = (sb(n, [P, GB]) for n in ("ln1", "rs1", "nm1"))

        C = A["ctxT"].shape[2]
        NH = 16
        DX = E // NH
        QD = 4
        NQ = NH // QD
        KV = DX + 1
        cwq = sb("cwq", [P, E])
        cwqT = sb("cwqT", [P, E])
        cwkvT = sb("cwkvT", [P, 2 * DX])
        cwcT = sb("cwcT", [P, E])
        wqs = sb("wqs", [P, NQ, 3, QD * DX])
        wks = sb("wks", [P, P // DX, DX])
        ident16, ones16 = sb("ident16", [P, P], F16), sb("ones16", [P, P], F16)
        iotaC = sb("iotaC", [P, C])
        thr, mult = sb("thr", [P, 1]), sb("mult", [P, 1])
        bmask = sb("bmask", [P, QD], F16)
        x1s = [sb(f"x1s{p}", [P, E]) for p in range(2)]
        ctxs = [sb(f"ctxs{p}", [P, C]) for p in range(2)]
        FW = E + 2 * C
        Fs = [sb(f"Fs{p}", [P, FW]) for p in range(2)]
        mv9 = [sb(f"mv9{p}", [C, KV]) for p in range(2)]
        qs = [sb(f"qs{p}", [P, NQ, T], F16) for p in range(2)]
        scr = sb("scr", [P, C])
        top8 = sb("top8", [P, 8])
        idx8 = sb("idx8", [P, 8], U32)
        idxf = sb("idxf", [P, 1])
        onehot = sb("onehot", [P, C], F16)
        src = [sb(f"src{p}", [P, C], F16) for p in range(2)]
        bd = [sb(f"bd{p}", [P, QD, C], F16) for p in range(2)]
        w9 = sb("w9", [C, KV])
        w18 = [sb(f"w18{p}", [C, 2, KV], F16) for p in range(2)]
        mx16 = sb("mx16", [P, NH], F16)
        E32 = sb("E32", [C, NQ, QD * T])
        Ehi = [sb(f"Ehi{p}", [C, NQ, QD * T], F16) for p in range(2)]
        Elo = [sb(f"Elo{p}", [C, NQ, QD * T], F16) for p in range(2)]
        osb = sb("osb", [P, NH, 2, KV])
        osum = sb("osum", [P, NH, KV])
        rden = sb("rden", [P, NH])
        at, aT, r2 = sb("at", [P, E]), sb("aT", [P, E]), sb("r2", [P, E])
        st2, mv2 = sb("st2", [P, 6]), sb("mv2", [P, 2])
        ln2, rs2 = sb("ln2", [P, 1]), sb("rs2", [P, 1])

        NE = A["rw"].shape[1]
        TOP = 4
        I = A["w1"].shape[2]
        NI = I // P
        rw = sb("rw", [P, NE])
        rb = sb("rb", [P, NE])
        b1T = sb("b1T", [P, NE * NI])
        b2 = sb("b2", [NE, E])
        x2s = [sb(f"x2s{p}", [P, E]) for p in range(2)]
        x2Tb = [sb(f"x2Tb{p}", [P, T]) for p in range(2)]
        lgs = sb("lgs", [P, NE])
        rtop = sb("rtop", [P, 8])
        ridx = sb("ridx", [P, 8], U32)
        topl, topi, gates = (sb(n, [P, B, TOP]) for n in ("topl", "topi", "gates"))
        gsum, grec = sb("gsum", [P, B]), sb("grec", [P, B])
        iotaE = sb("iotaE", [P, NE])
        x2T = sb("x2T", [P, B * T])
        oh, comb = sb("oh", [P, B, NE]), sb("comb", [P, B, NE])
        w1s = [sb(f"w1s{p}", [P, I]) for p in range(2)]
        w2s = [sb(f"w2s{p}", [P, NI, E]) for p in range(2)]
        hs = [sb(f"hs{p}", [P, NI, GC]) for p in range(2)]
        cT = [sb(f"cT{p}", [NE, P]) for p in range(2)]
        acc = sb("acc", [P, B * E])
        st3, mv3 = sb("st3", [P, B, 6]), sb("mv3", [P, B, 2])
        ln3, rs3 = sb("ln3", [P, B]), sb("rs3", [P, B])

        S = {}

        def s(name):
            if name not in S:
                S[name] = sem(name)
            return S[name]

        def pause(eng):
            eng.sem_inc(s("waits_over"), 1)

        block = ctx.enter_context(nc.Block())

        weights_dma = ["wk", "wq", "wv", "wo", "g1", "g2", "delta", "norm_w", "cwq", "cwqT", "cwkvT", "cwcT", "rw", "rb", "b1T", "b2"]
        WN = 16 * len(weights_dma)
        MASKED = -30000.0
        SCALE = float(1.0 / np.sqrt(np.float32(DX)))

        def steps(eng, step, first, last):
            first()
            step(0, 0, 0, True, False, False)
            step(1, 0, 1, True, True, False)
            with eng.Fori(0, B // 2 - 2) as i:
                for d in range(2):
                    step(2 * i + 2 + d, i + 1, d, True, True, True)
            step(B - 2, B // 2 - 1, 0, True, True, True)
            step(B - 1, B // 2 - 1, 1, False, True, False)
            if last:
                last()

        setup_steps = {}

        @block.sync
        def _(sp):
            for name, t in zip(weights_dma, (wk, wq, wv, wo, g1, g2, delta, norm_w, cwq, cwqT, cwkvT, cwcT, rw, rb, b1T, b2)):
                sp.dma_start(t[:, :], A[name]).then_inc(s("weights_in"), 16)
            for g in range(2):
                sp.dma_start(xTg[g][:, :], A["xT"][:, g * GC:(g + 1) * GC]).then_inc(s(f"xT_in{g}"), 16)
            sp.dma_start(X[:, :, :], A["x"]).then_inc(s("x_in"), 16)
            with sp.Fori(0, NG // 2 - 1) as i:
                for p in range(2):
                    g = 2 * i + p
                    sp.wait_ge(s("v_ps"), g + 1)
                    sp.dma_start(xTg[p][:, :], A["xT"][:, bass.ds((g + 2) * GC, GC)]).then_inc(s(f"xT_in{p}"), 16)
            sp.wait_ge(s("x1_ready"), NG)

            def fetch(b, p):
                sp.dma_start(x1s[p][:, :], X[:, :, :].rearrange("p b e -> p (b e)")[:, bass.ds(b * E, E)]).then_inc(s(f"cross_in{p}"), 16)
                sp.dma_start(ctxs[p][:, :], A["ctxT"].rearrange("b p c -> p b c")[:, bass.ds(b, 1), :]).then_inc(s(f"cross_in{p}"), 16)

            fetch(0, 0)
            fetch(1, 1)
            def save(b, p):
                sp.wait_ge(s("x2_ready"), b + 1)
                sp.dma_start(X[:, :, :].rearrange("p b e -> p (b e)")[:, bass.ds(b * E, E)], x2s[p][:, :]).then_inc(s(f"x2_saved{p}"), 16)

            def save_T(b, p):
                sp.wait_ge(s("x2T_ready"), b + 1)
                pause(sp)
                sp.dma_start(x2T[:, bass.ds(b * T, T)], x2Tb[p][:, :]).then_inc(s(f"x2T_saved{p}"), 16)

            def refetch(b, p):
                sp.wait_ge(s("F_ps"), b + 1)
                fetch(b + 2, p)

            for p in range(2):
                sp.sem_inc(s(f"x2_saved{p}"), 16)
                sp.sem_inc(s(f"x2T_saved{p}"), 16)
            for b in range(4):
                refetch(b, b % 2)
            with sp.Fori(0, B // 2 - 3) as i:
                for p in range(2):
                    b = 2 * i + p
                    refetch(b + 4, p)
                    save(b, p)
                    save_T(b, p)
            for b in range(B - 6, B):
                save(b, b % 2)
                save_T(b, b % 2)
            def weights(e, p):
                sp.dma_start(w1s[p][:, :], A["w1"].rearrange("e p i -> p e i")[:, bass.ds(e, 1), :]).then_inc(s(f"w_in{p}"), 16)
                sp.dma_start(w2s[p][:, :, :], A["w2"].rearrange("e (c p) d -> p e c d", p=P)[:, bass.ds(e, 1), :, :]).then_inc(s(f"w_in{p}"), 16)
            weights(0, 0)
            weights(1, 1)
            with sp.Fori(0, NE // 2 - 1) as i:
                for p in range(2):
                    sp.wait_ge(s("y_units"), NG * (2 * i + p + 1))
                    weights(2 * i + p + 2, p)
            sp.wait_ge(s("x3_ready"), 1)
            sp.dma_start(out, X[:, :, :]).then_inc(s("out"), 16)
            sp.wait_ge(s("out"), 16)

        @block.gpsimd
        def _(pool):
            n = 0

            def done(ins):
                nonlocal n
                n += 1
                ins.then_inc(s("pool_setup"), 1)
                pool.wait_ge(s("pool_setup"), n)

            def keep(v, pattern, base, channel, fill=0.0, op=ALU.is_ge):
                done(pool.affine_select(out=v, in_=v, compare_op=op, fill=fill, base=base, pattern=pattern, channel_multiplier=channel))

            done(pool.memset(ident[:, :], 0.0))
            keep(ident[:, :], [[-1, P]], 0, 1, fill=1.0, op=ALU.not_equal)
            for m, h in zip(lmask, HALVES):
                v3 = m[:, :].rearrange("p (b r) -> p b r", r=h)
                nb = 64 // h
                done(pool.memset(m[:, :], 1.0))
                keep(v3, [[-2 * h, nb], [0, h]], 0, 1)
                keep(v3, [[2 * h, nb], [0, h]], h - 1, -1)
            v3 = leafmask[:, :].rearrange("p (b r) -> p b r", r=LEAF)
            nb = T // LEAF
            done(pool.memset(leafmask[:, :], 1.0))
            keep(v3, [[-LEAF, nb], [0, LEAF]], 0, 1)
            keep(v3, [[LEAF, nb], [1, LEAF]], 0, -1)
            setup_steps["masks"] = n

            done(pool.memset(ones16[:, :], 1.0))
            done(pool.memset(ident16[:, :], 0.0))
            keep(ident16[:, :], [[-1, P]], 0, 1, fill=1.0, op=ALU.not_equal)
            done(pool.memset(thr[:, :], 0.5))
            done(pool.memset(thr[96:96 + QD, :], 1e9))
            done(pool.memset(mult[:, :], MASKED / (P - 96 - QD)))
            done(pool.memset(mult[96:96 + QD, :], -1.0))
            done(pool.memset(bmask[:, :], 1.0))
            keep(bmask[96:96 + QD, :], [[-1, QD]], 0, 1, op=ALU.is_equal)
            for blk in range(3):
                rows = bmask[32 * blk:32 * blk + 32, :]
                keep(rows, [[-DX, QD]], 0, 1)
                keep(rows, [[DX, QD]], DX - 1, -1)
            done(pool.iota(iotaC[:, :], pattern=[[1, C]], base=0, channel_multiplier=0, allow_small_or_imprecise_dtypes=True))
            done(pool.iota(iotaE[:, :], pattern=[[1, NE]], base=0, channel_multiplier=0, allow_small_or_imprecise_dtypes=True))
            for p in range(2):
                done(pool.memset(qs[p][96:128, :, :], 1.0))
                done(pool.memset(mv9[p][:, DX:KV], 1.0))
            setup_steps["cross"] = n

            def front(b, p):
                mk = Fs[p][:, E + C:E + 2 * C]
                if not (isinstance(b, int) and b <= 1):
                    pool.wait_ge(s("Elo_pool"), b - 1)
                pool.wait_ge(s("F_ready"), b + 1)
                pause(pool)
                pool.memset(qs[p][96:96 + QD, :, :], 0.0).then_inc(s("qzero"), 1)
                pool.wait_ge(s("qzero"), b + 1)
                pause(pool)
                pool.tensor_copy(src[p][0:96, :], mk[0:96, :]).then_inc(s("src_hi"), 1)
                pool.wait_ge(s("src_hi"), b + 1)
                pool.tensor_tensor(src[p][32:64, :], mk[32:64, :], src[p][32:64, :], ALU.subtract).then_inc(s("src_lo"), 1)
                pool.wait_ge(s("src_lo"), b + 1)
                pool.wait_ge(s("w9_ready"), b + 1)
                pause(pool)
                pool.tensor_copy(w18[p][:, 0, :], w9[:, :]).then_inc(s("w9_hi"), 1)
                pool.wait_ge(s("w9_hi"), b + 1)
                pool.tensor_tensor(w18[p][:, 1, :], w9[:, :], w18[p][:, 0, :], ALU.subtract).then_inc(s("w18_ready"), 1)
                pool.wait_ge(s("src_aux"), b + 1)
                pool.wait_ge(s("w18_ready"), b + 1)
                pool.tensor_tensor(bd[p][:, :, :], src[p][:, :].unsqueeze(1).to_broadcast([P, QD, C]),
                                   bmask[:, :].unsqueeze(2).to_broadcast([P, QD, C]), ALU.mult).then_inc(s("bd_ready"), 1)

            def split(b, p):
                j = NQ - 1
                if not (isinstance(b, int) and b == B - 1):
                    pool.wait_ge(s("bd_ready"), b + 2)
                pool.wait_ge(s("Ehi_dve"), 2 * b + 2)
                pool.tensor_tensor(Elo[p][:, j, :], E32[:, j, :], Ehi[p][:, j, :], ALU.subtract).then_inc(s("Elo_pool"), 1)

            steps(pool, lambda t, h, p, fr, tl, rt: ((front(t + 1, 1 - p) if fr else None), split(t, p)), lambda: front(0, 0), None)

        @block.tensor
        def _(pe):
            psU, psQ, psV, psG = banks[0], banks[1], banks[2], banks[3]
            psZ = banks[3]
            psA = banks[4:6]
            psO, psT, psY = banks[6], banks[7], banks[7]

            def project(g, p, n16, first=False):
                pe.wait_ge(s(f"xT_in{p}"), n16)
                if not first:
                    pe.wait_ge(s("u_ready"), g)
                pe.matmul(psU[:, :], wk[:, :], xTg[p][:, :], start=True, stop=True).then_inc(s("u_ps"), 1)
                if not first:
                    pe.wait_ge(s("qc_ready"), g)
                pe.matmul(psQ[:, :], wq[:, :], xTg[p][:, :], start=True, stop=True).then_inc(s("q_ps"), 1)
                if not first:
                    pe.wait_ge(s("gc_ready"), g)
                pe.matmul(psZ[0:DH, :], g1[:, :], xTg[p][:, :], start=True, stop=True).then_inc(s("z_ps"), 1)
                if not first:
                    pe.wait_ge(s("v_ready"), g)
                for b in range(GB):
                    mm = pe.matmul(psV[:, b * E:(b + 1) * E], xTg[p][:, b * T:(b + 1) * T], wv[:, :], start=True, stop=True)
                mm.then_inc(s("v_ps"), 1)
                pe.wait_ge(s("zT_ready"), g + 1)
                for b in range(GB):
                    mm = pe.matmul(psG[:, b * E:(b + 1) * E], zT[:, b * T:(b + 1) * T], g2[:, :], start=True, stop=True)
                mm.then_inc(s("g_ps"), 1)

            def attend(g, p):
                for l in range(NL):
                    pe.wait_ge(s("LR_ready"), (NL + 1) * g + l + 1)
                    if l >= 2:
                        pe.wait_ge(s("A_taken"), (NL + 2) * g + l - 1)
                    for b in range(GB):
                        mm = pe.matmul(psA[l % 2][:, b * T:(b + 1) * T], Lk[l][:, b * T:(b + 1) * T], Rq[l][:, b, :, :], start=True, stop=True)
                    mm.then_inc(s("A_ps"), 1)
                pe.wait_ge(s("LR_ready"), (NL + 1) * g + NL + 1)
                for j in range(2):
                    pe.wait_ge(s("A_taken"), (NL + 2) * g + NL + j - 1)
                    for b in range(2):
                        bb = 2 * j + b
                        mm = pe.matmul(psA[j][:, b * 2 * T:(b + 1) * 2 * T], Lk[NL][:, bb * T:(bb + 1) * T], Rleaf[:, bb, :, :], start=True, stop=True)
                    mm.then_inc(s("A_ps"), 1)
                pe.wait_ge(s("A_taken"), (NL + 2) * (g + 1))
                for b in range(GB):
                    for h in range(H):
                        c = b * E + h * DH
                        mm = pe.matmul(psO[:, c:c + DH], AT[:, b, h, :], v[p][:, c:c + DH], start=True, stop=True)
                mm.then_inc(s("o_ps"), 1)
                pe.wait_ge(s("on_ready"), g + 1)
                for b in range(GB):
                    mm = pe.transpose(psT[:, b * T:(b + 1) * T], on[:, b * E:(b + 1) * E], ident[:, :])
                mm.then_inc(s("oT_ps"), 1)
                pe.wait_ge(s("oT_ready"), g + 1)
                for b in range(GB):
                    mm = pe.matmul(psY[:, b * E:(b + 1) * E], oT[:, b * T:(b + 1) * T], won[:, :], start=True, stop=True)
                mm.then_inc(s("y_ps"), 1)

            pe.wait_ge(s("weights_in"), WN)
            pe.wait_ge(s("pool_setup"), setup_steps["masks"])
            pe.wait_ge(s("won_ready"), 1)
            project(0, 0, 16, first=True)

            def step(i, last=False):
                project(2 * i + 1, 1, 16 * i + 16)
                attend(2 * i, 0)
                if not last:
                    project(2 * i + 2, 0, 16 * i + 32)
                attend(2 * i + 1, 1)

            with pe.Fori(0, NG // 2 - 1) as i:
                step(i)
            step(NG // 2 - 1, last=True)

            psF, psQx, psS, psL1, psL2, psR = banks[0], banks[1], banks[2], banks[3:5], banks[5:7], banks[7]
            pe.wait_ge(s("pool_setup"), setup_steps["cross"])
            pe.wait_ge(s("wqs_ready"), 2)
            pe.wait_ge(s("x1_ready"), NG)

            def front_f(b, p, n32):
                pe.wait_ge(s(f"cross_in{p}"), n32)
                if not (isinstance(b, int) and b == 0):
                    pe.wait_ge(s("F_ready"), b)
                    pe.wait_ge(s("mv9_ready"), b)
                pe.transpose(psF[:, 0:E], x1s[p][:, :], ident[:, :])
                pe.matmul(psF[:, E:E + C], cwq[:, :], ctxs[p][:, :], start=True, stop=True)
                pe.matmul(psF[:, E + C:E + 2 * C], wks[:, :, :].rearrange("p r d -> p (r d)"), ctxs[p][:, :], start=True, stop=True)
                pe.matmul(psF[0:C, FW:FW + DX], ctxs[p][:, :], cwkvT[:, DX:2 * DX], start=True, stop=True).then_inc(s("F_ps"), 1)

            pe.sem_inc(s("x2T_ps"), 2)

            def route_turn(b, p):
                pe.wait_ge(s("x2_ready"), b + 1)
                if not (isinstance(b, int) and b == 0):
                    pe.wait_ge(s("lgs_ready"), b)
                pe.transpose(psS[:, 384:384 + T], x2s[p][:, :], ident[:, :]).then_inc(s("x2T_ps"), 1)

            def route_logits(b, p):
                pe.wait_ge(s("x2T_ready"), b + 1)
                pe.matmul(psS[:, 320:320 + NE], x2Tb[p][:, :], rw[:, :], start=True, stop=True).then_inc(s("lg_ps"), 1)

            def front_q(b, p, rt=False):
                pe.wait_ge(s("F_ready"), b + 1)
                if not (isinstance(b, int) and b == 0):
                    pe.wait_ge(s("qlo_ready"), b)
                for j in range(NQ):
                    mm = pe.matmul(psQx[0:96, j * T:(j + 1) * T], wqs[:, j, :, :].rearrange("p r d -> p (r d)"), Fs[p][:, 0:E], start=True, stop=True)
                mm.then_inc(s("Qx_ps"), 1)
                if not (isinstance(b, int) and b == 0):
                    pe.wait_ge(s("w9_ready"), b)
                    pe.wait_ge(s("src_aux"), b)
                if rt:
                    route_turn(b - 3, 1 - p)
                pe.matmul(psS[:, 0:C], Fs[p][:, 0:E], Fs[p][:, E:E + C], start=True, stop=True).then_inc(s("S_ps"), 1)

            def front_c(b):
                pe.wait_ge(s("onehot_ready"), b + 1)
                pe.matmul(psS[:, 128:128 + C], ones16[:, :], onehot[:, :], start=True, stop=True)
                pe.matmul(psS[0:C, 256:257], onehot[:, :], ones16[:, 0:1], start=True, stop=True).then_inc(s("cnt_ps"), 1)

            def pass1(t, p, half):
                if half == 0:
                    pe.wait_ge(s("bd_ready"), t + 1)
                    pe.wait_ge(s("qzero"), t + 1)
                    pe.wait_ge(s("qhi_ready"), t + 1)
                    pe.wait_ge(s("qlo_ready"), t + 1)
                    if not (isinstance(t, int) and t == 0):
                        pe.wait_ge(s("mx_ready"), 2 * t)
                else:
                    pe.wait_ge(s("mx_ready"), 2 * t + 1)
                for j in range(2):
                    mm = pe.matmul(psL1[j][:, 0:QD * C], qs[p][:, 2 * half + j, :], bd[p][:, :, :].rearrange("p h c -> p (h c)"), start=True, stop=True)
                mm.then_inc(s("L1_ps"), 1)

            def maxrows(t):
                pe.wait_ge(s("mx_ready"), 2 * t + 2)
                if not (isinstance(t, int) and t == 0):
                    pe.wait_ge(s("E_ready"), NQ * t - 1)
                for j in range(NQ):
                    mm = pe.matmul(psL2[0][96:96 + QD, j * T:(j + 1) * T], mx16[:, QD * j:QD * j + QD], ident16[:, :], start=True, stop=True)
                mm.then_inc(s("M_ps"), 1)

            def pass2(t, p, j):
                if j == 0:
                    pe.wait_ge(s("qmax_ready"), t + 1)
                elif j > 1 or not (isinstance(t, int) and t == 0):
                    pe.wait_ge(s("E_ready"), NQ * t + j - 1)
                for h in range(QD):
                    mm = pe.matmul(psL2[j % 2][0:C, h * T:(h + 1) * T], bd[p][:, h, :], qs[p][:, j, :], start=True, stop=True)
                mm.then_inc(s("L2_ps"), 1)

            def values(b, p):
                if not (isinstance(b, int) and b == 0):
                    pe.wait_ge(s("r2_ready"), b)
                pe.wait_ge(s("w18_ready"), b + 1)
                pe.wait_ge(s("Ehi_act"), 2 * b + 2)
                pe.wait_ge(s("Elo_dve"), 3 * b + 3)
                pe.wait_ge(s("Elo_pool"), b + 1)
                for h in range(NH):
                    o = psR[:, h * 2 * KV:(h + 1) * 2 * KV]
                    cols = slice((h % QD) * T, (h % QD + 1) * T)
                    pe.matmul(o, Ehi[p][:, h // QD, cols], w18[p][:, :, :].rearrange("p s v -> p (s v)"), start=True, stop=False, skip_group_check=True)
                    mm = pe.matmul(o[:, 0:KV], Elo[p][:, h // QD, cols], w18[p][:, 0, :], start=False, stop=True, skip_group_check=True)
                mm.then_inc(s("O_ps"), 1)

            def turn(b):
                pe.wait_ge(s("at_ready"), b + 1)
                pe.transpose(psR[:, 384:384 + E], at[:, :], ident[:, :]).then_inc(s("aT_ps"), 1)

            def project_out(b):
                pe.wait_ge(s("aT_ready"), b + 1)
                pe.matmul(psR[:, 0:E], aT[:, :], cwcT[:, :], start=True, stop=True).then_inc(s("Y2_ps"), 1)

            def step(t, h, p, fr, tl, rt):
                pass1(t, p, 0)
                if fr:
                    front_f(t + 1, 1 - p, 16 * (t + 1 + p) + 16)
                pass1(t, p, 1)
                if tl:
                    values(t - 1, 1 - p)
                if fr:
                    front_q(t + 1, 1 - p, rt)
                maxrows(t)
                if tl:
                    turn(t - 1)
                pass2(t, p, 0)
                pass2(t, p, 1)
                if tl:
                    project_out(t - 1)
                pass2(t, p, 2)
                if rt:
                    route_logits(t - 2, p)
                if fr:
                    front_c(t + 1)
                pass2(t, p, 3)

            def first():
                front_f(0, 0, 32)
                front_q(0, 0)
                front_c(0)

            def last():
                values(B - 1, 1)
                turn(B - 1)
                project_out(B - 1)
                for b in range(B - 3, B):
                    route_turn(b, b % 2)
                    route_logits(b, b % 2)

            steps(pe, step, first, last)

            psH, psY3 = banks[0:4], banks[4:6]
            psC, psB = banks[6], banks[7]
            pe.wait_ge(s("comb_ready"), 1)
            pe.wait_ge(s("E_ready"), NQ * B)
            pe.wait_ge(s("r2_ready"), B)
            for t in range(B):
                if t:
                    pe.wait_ge(s("cT_ready"), t)
                pe.transpose(psC[0:NE, 0:P], comb[:, t, :], ident[:, :]).then_inc(s("cT_ps"), 1)
                pe.wait_ge(s("cT_ready"), t + 1)
                if t:
                    pe.wait_ge(s("acc_init"), t)
                pe.matmul(psB[:, 0:E], cT[t % 2][:, :], b2[:, :], start=True, stop=True).then_inc(s("b_ps"), 1)
            for p in range(2):
                pe.wait_ge(s(f"x2T_saved{p}"), 16 * (B // 2) + 16)

            def hidden(u, g, p, pw):
                pe.wait_ge(s("h_ready"), 2 * u + 1)
                for c in range(NI):
                    mm = pe.matmul(psH[2 * p + c][:, :], w1s[pw][:, c * P:(c + 1) * P], x2T[:, bass.ds(g * GC, GC)], start=True, stop=True)
                mm.then_inc(s("h_ps"), 1)

            def outputs(u, p, pw):
                pe.wait_ge(s("h_ready"), 2 * u + 2 + 4)
                pe.wait_ge(s("acc_ready"), u + 1)
                for j in range(GB):
                    for c in range(NI):
                        mm = pe.matmul(psY3[p][:, j * E:(j + 1) * E], hs[p][:, c, j * T:(j + 1) * T], w2s[pw][:, c, :], start=(c == 0), stop=(c == NI - 1), skip_group_check=True)
                mm.then_inc(s("y_units"), 1)

            with pe.Fori(0, NE // 2) as i:
                for pw in range(2):
                    e = 2 * i + pw
                    pe.wait_ge(s(f"w_in{pw}"), 32 * i + 32)
                    for g in range(NG):
                        hidden(e * NG + g, g, g % 2, pw)
                        outputs(e * NG + g, g % 2, pw)

        @block.scalar
        def _(act):
            psQ, psV, psG, psZ, psT = banks[1], banks[2], banks[3], banks[3], banks[7]
            act.preload_act_table_set("natural_log_exp_and_others")
            act.wait_ge(s("weights_in"), WN)

            def project(g, p):
                act.wait_ge(s("z_ps"), g + 1)
                act.activation(zT[:, :], psZ[0:DH, :], ACT.Copy).then_inc(s("zT_ready"), 1)
                act.wait_ge(s("u_ready"), g + 1)
                act.activation(soft[:, :], uS[:, :], ACT.Exp, scale=-1.0).then_inc(s("act_chain"), 1)
                act.wait_ge(s("act_chain"), 6 * g + 1)
                act.activation(soft[:, :], soft[:, :], ACT.Ln, bias=1.0).then_inc(s("soft_ready"), 1)
                act.wait_ge(s("v_ps"), g + 1)
                act.activation(v[p][:, :], psV[:, :], ACT.Copy).then_inc(s("v_ready"), 1)
                act.wait_ge(s("kk_ready"), g + 1)
                act.activation(k[:, :], kk[:, :], ACT.Exp, scale=-1.0).then_inc(s("k_ready"), 1)
                for src, dst, ready, done, n in ((qc, sq_, "qc_ready", "sigq_ready", 0), (gc, sg_, "gc_ready", "gate_ready", 2)):
                    act.wait_ge(s(ready), g + 1)
                    act.activation(dst[:, :], src[:, :], ACT.Exp, scale=-1.0).then_inc(s("act_chain"), 1)
                    act.wait_ge(s("act_chain"), 6 * g + n + 2)
                    act.activation(dst[:, :], dst[:, :], ACT.Ln, bias=1.0).then_inc(s("act_chain"), 1)
                    act.wait_ge(s("act_chain"), 6 * g + n + 3)
                    o = gate[p] if n else dst
                    act.activation(o[:, :], dst[:, :], ACT.Exp, scale=-1.0).then_inc(s(done), 1)
                act.sem_inc(s("act_chain"), 1)

            def decays(g):
                for l in range(NL + 1):
                    act.wait_ge(s("dec_ready"), (NL + 1) * g + l + 1)
                    if l == NL:
                        act.activation(decK[:, :], dec[l][:, :], ACT.Exp).then_inc(s("decK_exp"), 1)
                    act.activation(dec[l][:, :], dec[l][:, :], ACT.Exp, scale=-1.0).then_inc(s("dec_exp"), 1)

            def finish(g, p):
                act.wait_ge(s("og_ready"), g + 1)
                act.activation(osq[:, :], og[:, :], ACT.Square).then_inc(s("osq_ready"), 1)
                act.wait_ge(s("ss_ready"), g + 1)
                act.activation(lss[:, :], ss[:, :], ACT.Ln, bias=EPS, scale=1.0 / DH).then_inc(s("lss_ready"), 1)
                act.wait_ge(s("lss_ready"), g + 1)
                act.activation(rss[:, :], lss[:, :], ACT.Exp, scale=-0.5).then_inc(s("rss_ready"), 1)
                act.wait_ge(s("oT_ps"), g + 1)
                act.activation(oT[:, :], psT[:, :], ACT.Copy).then_inc(s("oT_ready"), 1)
                act.wait_ge(s("mv1_ready"), g + 1)
                act.activation(ln1[:, :], mv1[:, :, 1], ACT.Ln, bias=EPS).then_inc(s("ln1_ready"), 1)
                act.wait_ge(s("ln1_ready"), g + 1)
                act.activation(rs1[:, :], ln1[:, :], ACT.Exp, scale=-0.5).then_inc(s("rs1_ready"), 1)

            project(0, 0)

            def step(i, last=False):
                decays(2 * i)
                project(2 * i + 1, 1)
                finish(2 * i, 0)
                decays(2 * i + 1)
                if not last:
                    project(2 * i + 2, 0)
                finish(2 * i + 1, 1)

            with act.Fori(0, NG // 2 - 1) as i:
                step(i)
            step(NG // 2 - 1, last=True)

            psF, psQx, psS, psL2, psR = banks[0], banks[1], banks[2], banks[5:7], banks[7]

            def route(b, p, hb):
                act.wait_ge(s("x2T_ps"), b + 3)
                act.wait_ge(s(f"x2T_saved{p}"), 16 * hb + 16)
                act.activation(x2Tb[p][:, :], psS[:, 384:384 + T], ACT.Copy).then_inc(s("x2T_ready"), 1)

            def front(b, p, rt=None):
                act.wait_ge(s("F_ps"), b + 1)
                act.activation(Fs[p][:, :], psF[:, 0:FW], ACT.Copy).then_inc(s("F_ready"), 1)
                act.activation(mv9[p][:, 0:DX], psF[0:C, FW:FW + DX], ACT.Copy).then_inc(s("mv9_ready"), 1)
                act.wait_ge(s("Qx_ps"), b + 1)
                act.activation(qs[p][0:96, :, :].rearrange("p j t -> p (j t)"), psQx[0:96, :], ACT.Copy).then_inc(s("qhi_ready"), 1)
                act.wait_ge(s("S_ps"), b + 1)
                act.activation(scr[:, :], psS[:, 0:C], ACT.Copy).then_inc(s("scr_ready"), 1)
                if rt is not None:
                    route(b - 3, 1 - p, rt)

            def expo(t, p):
                act.wait_ge(s("M_ps"), t + 1)
                act.activation(qs[p][96:96 + QD, :, :].rearrange("p j t -> p (j t)"), psL2[0][96:96 + QD, :], ACT.Copy).then_inc(s("qmax_ready"), 1)
                for j in range(NQ):
                    act.wait_ge(s("L2_ps"), NQ * t + j + 1)
                    if not (isinstance(t, int) and t == 0):
                        if j < 3:
                            act.wait_ge(s("Elo_dve"), 3 * t + j - 2)
                        else:
                            act.wait_ge(s("Elo_pool"), t)
                    act.activation(E32[:, j, :], psL2[j % 2][0:C, :], ACT.Exp).then_inc(s("E_ready"), 1)
                    if 1 <= j <= 2:
                        act.wait_ge(s("E_ready"), NQ * t + j)
                        act.activation(Ehi[p][:, j - 1, :], E32[:, j - 1, :], ACT.Copy).then_inc(s("Ehi_act"), 1)

            def tail_o(b):
                act.wait_ge(s("O_ps"), b + 1)
                act.activation(osb[:, :, :, :].rearrange("p h s v -> p (h s v)"), psR[:, 0:NH * 2 * KV], ACT.Copy).then_inc(s("osb_ready"), 1)

            def tail_t(b):
                act.wait_ge(s("aT_ps"), b + 1)
                act.activation(aT[:, :], psR[:, 384:384 + E], ACT.Copy).then_inc(s("aT_ready"), 1)

            def tail_n(b):
                act.wait_ge(s("mv2_ready"), b + 1)
                act.activation(ln2[:, :], mv2[:, 1:2], ACT.Ln, bias=EPS).then_inc(s("ln2_ready"), 1)
                act.wait_ge(s("ln2_ready"), b + 1)
                act.activation(rs2[:, :], ln2[:, :], ACT.Exp, scale=-0.5).then_inc(s("rs2_ready"), 1)

            def step(t, h, p, fr, tl, rt):
                if tl:
                    tail_o(t - 1)
                if fr:
                    front(t + 1, 1 - p, h - 1 if rt else None)
                if tl:
                    tail_t(t - 1)
                expo(t, p)
                if tl:
                    tail_n(t - 1)

            def last():
                tail_o(B - 1)
                tail_t(B - 1)
                tail_n(B - 1)
                for b in range(B - 3, B):
                    route(b, b % 2, b // 2)

            steps(act, step, lambda: front(0, 0), last)

            psH, psC = banks[0:4], banks[6]
            act.wait_ge(s("gates0"), 1)
            act.activation(gates[:, :, :].rearrange("p b k -> p (b k)"), gates[:, :, :].rearrange("p b k -> p (b k)"), ACT.Exp).then_inc(s("gates1"), 1)
            for t in range(B):
                act.wait_ge(s("cT_ps"), t + 1)
                if t > 1:
                    act.wait_ge(s("b_ps"), t - 1)
                act.activation(cT[t % 2][:, :], psC[0:NE, 0:P], ACT.Copy).then_inc(s("cT_ready"), 1)
            act.preload_act_table_set("gelu_and_others")
            act.sem_inc(s("h_ready"), 4)
            with act.Fori(0, NE) as e:
                for g in range(NG):
                    u = e * NG + g
                    act.wait_ge(s("h_ps"), u + 1)
                    act.wait_ge(s("y_credit"), u + 1)
                    pause(act)
                    for c in range(NI):
                        act.activation(hs[g % 2][:, c, :], psH[2 * (g % 2) + c][:, :], ACT.Gelu, bias=b1T[:, bass.ds(e * NI + c, 1)]).then_inc(s("h_ready"), 1)
            act.preload_act_table_set("natural_log_exp_and_others")
            act.wait_ge(s("mv3_ready"), 1)
            act.activation(ln3[:, :], mv3[:, :, 1], ACT.Ln, bias=EPS).then_inc(s("ln3_ready"), 1)
            act.wait_ge(s("ln3_ready"), 1)
            act.activation(rs3[:, :], ln3[:, :], ACT.Exp, scale=-0.5).then_inc(s("rs3_ready"), 1)

        @block.vector
        def _(dve):
            psU, psQ, psG = banks[0], banks[1], banks[3]
            psA = banks[4:6]
            psO, psY = banks[6], banks[7]
            dve.memset(restart[:, :], 1.0).then_inc(s("dve_init"), 1)
            dve.memset(AT[:, :, :, :], 0.0).then_inc(s("dve_init"), 1)
            n = 2
            for t in Lk:
                dve.memset(t[:, :], 0.0).then_inc(s("dve_init"), 1)
                n += 1
            for t in [*Rq, Rleaf]:
                dve.memset(t[:, :, :, :], 0.0).then_inc(s("dve_init"), 1)
                n += 1
            dve.wait_ge(s("dve_init"), n)
            dve.memset(restart[:, :].rearrange("p (b t) -> p b t", t=T)[:, :, 0:1], 0.0).then_inc(s("dve_init"), 1)
            dve.wait_ge(s("weights_in"), WN)
            dve.tensor_scalar(won[:, :], wo[:, :], norm_w[:, 0:1], None, ALU.mult).then_inc(s("won_ready"), 1)
            dve.wait_ge(s("dve_init"), n + 1)
            dve.wait_ge(s("pool_setup"), setup_steps["masks"])
            dve.wait_ge(s("x_in"), 16)

            def project(g, p):
                dve.wait_ge(s("u_ps"), g + 1)
                dve.tensor_scalar(uS[:, :], psU[:, :], delta[:, 0:1], -FLOOR, ALU.add, ALU.max).then_inc(s("u_ready"), 1)
                dve.wait_ge(s("q_ps"), g + 1)
                dve.tensor_scalar(qc[:, :], psQ[:, :], -40.0, None, ALU.max).then_inc(s("qc_ready"), 1)
                dve.wait_ge(s("g_ps"), g + 1)
                dve.tensor_scalar(gc[:, :], psG[:, :], -40.0, None, ALU.max).then_inc(s("gc_ready"), 1)
                dve.wait_ge(s("soft_ready"), g + 1)
                dve.tensor_tensor(kk[:, :], uS[:, :], soft[:, :], ALU.add).then_inc(s("kk_ready"), 1)
                dve.tensor_tensor_scan(N[:, :], restart[:, :], soft[:, :], 0.0, ALU.mult, ALU.add).then_inc(s("N_ready"), 1)
                dve.wait_ge(s("sigq_ready"), g + 1)
                dve.tensor_tensor(q[:, :], qc[:, :], sq_[:, :], ALU.mult).then_inc(s("q_ready"), 1)

            def attend(g):
                dve.wait_ge(s("N_ready"), g + 1)
                for l, h in enumerate(HALVES):
                    nb = GC // (2 * h)
                    n4 = N[:, :].rearrange("p (b s r) -> p b s r", s=2, r=h)
                    d4 = dec[l][:, :].rearrange("p (b s r) -> p b s r", s=2, r=h)
                    anchor = n4[:, :, 0, h - 1:h].to_broadcast([P, nb, h])
                    dve.tensor_tensor(d4[:, :, 1, :], n4[:, :, 1, :], anchor, ALU.subtract)
                    dve.tensor_tensor(d4[:, :, 0, :], anchor, n4[:, :, 0, :], ALU.subtract).then_inc(s("dec_ready"), 1)
                n3 = N[:, :].rearrange("p (b r) -> p b r", r=LEAF)
                mid = n3[:, :, LEAF // 2 - 1:LEAF // 2].to_broadcast([P, GC // LEAF, LEAF])
                dve.tensor_tensor(dec[NL][:, :].rearrange("p (b r) -> p b r", r=LEAF), n3, mid, ALU.subtract).then_inc(s("dec_ready"), 1)
                dve.wait_ge(s("k_ready"), g + 1)
                dve.wait_ge(s("q_ready"), g + 1)
                for l, h in enumerate(HALVES):
                    dve.wait_ge(s("dec_exp"), (NL + 1) * g + l + 1)
                    k4, q4, d4, L4 = (t[:, :].rearrange("p (b s r) -> p b s r", s=2, r=h) for t in (k, q, dec[l], Lk[l]))
                    dve.tensor_tensor(L4[:, :, 0, :], k4[:, :, 0, :], d4[:, :, 0, :], ALU.mult)
                    for hd in range(H):
                        hp = slice(hd * DH, (hd + 1) * DH)
                        out_ = Rq[l][hp, :, hd, :].rearrange("p b (n r) -> p b n r", r=h)
                        qv, dv = (t[hp, :].rearrange("p (b n s r) -> p b n s r", b=GB, s=2, r=h)[:, :, :, 1, :] for t in (q, dec[l]))
                        ins = dve.tensor_tensor(out_, qv, dv, ALU.mult)
                    ins.then_inc(s("LR_ready"), 1)
                dve.wait_ge(s("decK_exp"), g + 1)
                dve.wait_ge(s("dec_exp"), (NL + 1) * (g + 1))
                dve.tensor_tensor(Lk[NL][:, :], k[:, :], decK[:, :], ALU.mult)
                for hd in range(H):
                    hp = slice(hd * DH, (hd + 1) * DH)
                    qv, dv = (t[hp, :].rearrange("p (b t) -> p b t", b=GB) for t in (q, dec[NL]))
                    ins = dve.tensor_tensor(Rleaf[hp, :, hd, :], qv, dv, ALU.mult)
                ins.then_inc(s("LR_ready"), 1)
                for l, h in enumerate(HALVES):
                    nb = T // (2 * h)
                    dve.wait_ge(s("A_ps"), (NL + 2) * g + l + 1)
                    if l:
                        dve.wait_ge(s("A_taken"), (NL + 2) * g + l)
                    dst = AT[:, :, :, :].rearrange("p b d (n s r) -> p (b d) n s r", s=2, r=h)[:, :, :, 1, :]
                    src = psA[l % 2][:, :].rearrange("p (m n r) -> p m n r", n=nb, r=h)
                    msk = lmask[l][:, :].bitcast(U32).rearrange("p (n r) -> p n r", r=h).unsqueeze(1).to_broadcast([P, GB * H, nb, h])
                    pause(dve)
                    dve.copy_predicated(dst, msk, src).then_inc(s("A_taken"), 1)
                for j in range(2):
                    dve.wait_ge(s("A_ps"), (NL + 2) * g + NL + j + 1)
                    dve.wait_ge(s("A_taken"), (NL + 2) * g + NL + j)
                    dst = AT[:, 2 * j:2 * j + 2, :, :].rearrange("p b d t -> p (b d) t")
                    src = psA[j][:, :].rearrange("p (m t) -> p m t", t=T)
                    msk = leafmask[:, :].bitcast(U32).unsqueeze(1).to_broadcast([P, 4, T])
                    pause(dve)
                    dve.copy_predicated(dst, msk, src).then_inc(s("A_taken"), 1)

            def finish(g, p):
                dve.wait_ge(s("o_ps"), g + 1)
                dve.wait_ge(s("gate_ready"), g + 1)
                dve.tensor_tensor(og[:, :], psO[:, :], gate[p][:, :], ALU.mult).then_inc(s("og_ready"), 1)
                dve.wait_ge(s("osq_ready"), g + 1)
                dve.tensor_reduce(ss[:, :], osq[:, :].rearrange("p (m d) -> p m d", d=DH), AX.X, ALU.add).then_inc(s("ss_ready"), 1)
                dve.wait_ge(s("rss_ready"), g + 1)
                dve.tensor_tensor(on[:, :].rearrange("p (m d) -> p m d", d=DH), og[:, :].rearrange("p (m d) -> p m d", d=DH),
                                  rss[:, :].unsqueeze(2).to_broadcast([P, GB * H, DH]), ALU.mult).then_inc(s("on_ready"), 1)
                dve.wait_ge(s("y_ps"), g + 1)
                xg = X[:, :, :].rearrange("p b e -> p (b e)")[:, bass.ds(g * GC, GC)]
                dve.tensor_tensor(r1[:, :], psY[:, :], xg, ALU.add).then_inc(s("r1_ready"), 1)
                dve.wait_ge(s("r1_ready"), g + 1)
                for b in range(GB):
                    ins = dve.bn_stats(st1[:, b, :], r1[:, b * E:(b + 1) * E])
                ins.then_inc(s("st1_ready"), 1)
                dve.wait_ge(s("st1_ready"), g + 1)
                pause(dve)
                for b in range(GB):
                    ins = dve.bn_aggr(mv1[:, b, :], st1[:, b, :])
                ins.then_inc(s("mv1_ready"), 1)
                dve.wait_ge(s("rs1_ready"), g + 1)
                for b in range(GB):
                    dst = X[:, :, :].rearrange("p b e -> p (b e)")[:, bass.ds(g * GC + b * E, E)]
                    ins = dve.tensor_scalar(dst, r1[:, b * E:(b + 1) * E], mv1[:, b, 0:1], rs1[:, b:b + 1], ALU.subtract, ALU.mult)
                ins.then_inc(s("x1_ready"), 1)

            project(0, 0)

            def step(i, last=False):
                attend(2 * i)
                project(2 * i + 1, 1)
                finish(2 * i, 0)
                attend(2 * i + 1)
                if not last:
                    project(2 * i + 2, 0)
                finish(2 * i + 1, 1)

            with dve.Fori(0, NG // 2 - 1) as i:
                step(i)
            step(NG // 2 - 1, last=True)


            psQx, psS, psR = banks[1], banks[2], banks[7]
            for r in range(3):
                ins = dve.tensor_copy(wqs[:, :, r, :], cwqT[:, :].rearrange("p (j d) -> p j d", j=NQ))
            ins.then_inc(s("wqs_ready"), 1)
            dve.tensor_scalar(wks[:, :, :], cwkvT[:, 0:DX].unsqueeze(1).to_broadcast([P, P // DX, DX]), SCALE, None, ALU.mult).then_inc(s("wqs_ready"), 1)
            dve.wait_ge(s("pool_setup"), setup_steps["cross"])

            def front_q(b, p):
                dve.wait_ge(s("qhi_ready"), b + 1)
                lo = qs[p][64:96, :, :].rearrange("p j t -> p (j t)")
                dve.tensor_tensor(lo, psQx[64:96, :], lo, ALU.subtract).then_inc(s("qlo_ready"), 1)

            def front_s(b):
                dve.wait_ge(s("scr_ready"), b + 1)
                pause(dve)
                dve.max(top8[:, :], scr[:, :]).then_inc(s("top8_ready"), 1)
                dve.wait_ge(s("top8_ready"), b + 1)
                pause(dve)
                dve.max_index(idx8[:, :], top8[:, :], scr[:, :]).then_inc(s("idx8_ready"), 1)
                dve.wait_ge(s("idx8_ready"), b + 1)
                dve.tensor_copy(idxf[:, :], idx8[:, 0:1]).then_inc(s("idxf_ready"), 1)
                dve.wait_ge(s("idxf_ready"), b + 1)
                dve.tensor_scalar(onehot[:, :], iotaC[:, :], idxf[:, 0:1], None, ALU.is_equal).then_inc(s("onehot_ready"), 1)

            def front_c(b, p):
                dve.wait_ge(s("cnt_ps"), b + 1)
                dve.wait_ge(s("mv9_ready"), b + 1)
                if not (isinstance(b, int) and b == 0):
                    dve.wait_ge(s("w18_ready"), b)
                dve.tensor_scalar(src[p][96:128, :], psS[96:128, 128:128 + C], thr[96:128, 0:1], mult[96:128, 0:1], ALU.is_le, ALU.mult).then_inc(s("src_aux"), 1)
                dve.tensor_scalar(w9[:, :], mv9[p][:, :], psS[0:C, 256:257], None, ALU.mult).then_inc(s("w9_ready"), 1)

            def maxima(t, half):
                dve.wait_ge(s("L1_ps"), 2 * t + half + 1)
                for j in range(2):
                    q0 = QD * (2 * half + j)
                    ins = dve.tensor_reduce(mx16[:, q0:q0 + QD], banks[3 + j][:, 0:QD * C].rearrange("p (h c) -> p h c", c=C), AX.X, ALU.max)
                ins.then_inc(s("mx_ready"), 1)

            def split(t, p, j):
                if j < 2:
                    dve.wait_ge(s("Ehi_act"), 2 * t + j + 1)
                else:
                    dve.wait_ge(s("E_ready"), NQ * t + j + 1)
                    dve.tensor_copy(Ehi[p][:, j, :], E32[:, j, :]).then_inc(s("Ehi_dve"), 1)
                    if j == 2:
                        dve.wait_ge(s("Ehi_dve"), 2 * t + 1)
                if j < 3:
                    dve.tensor_tensor(Elo[p][:, j, :], E32[:, j, :], Ehi[p][:, j, :], ALU.subtract).then_inc(s("Elo_dve"), 1)

            def tail_o(b):
                dve.wait_ge(s("osb_ready"), b + 1)
                dve.tensor_tensor(osum[:, :, :], osb[:, :, 0, :], osb[:, :, 1, :], ALU.add).then_inc(s("osum_ready"), 1)
                dve.wait_ge(s("osum_ready"), b + 1)
                dve.reciprocal(rden[:, :], osum[:, :, DX]).then_inc(s("rden_ready"), 1)
                dve.wait_ge(s("rden_ready"), b + 1)
                dve.tensor_tensor(at[:, :].rearrange("p (h d) -> p h d", d=DX), osum[:, :, 0:DX], rden[:, :].unsqueeze(2).to_broadcast([P, NH, DX]),
                                  ALU.mult).then_inc(s("at_ready"), 1)

            def tail_r(b):
                dve.wait_ge(s("Y2_ps"), b + 1)
                xb = X[:, :, :].rearrange("p b e -> p (b e)")[:, bass.ds(b * E, E)]
                dve.tensor_tensor(r2[:, :], psR[:, 0:E], xb, ALU.add).then_inc(s("r2_ready"), 1)
                dve.wait_ge(s("r2_ready"), b + 1)
                dve.bn_stats(st2[:, :], r2[:, :]).then_inc(s("st2_ready"), 1)
                dve.wait_ge(s("st2_ready"), b + 1)
                pause(dve)
                dve.bn_aggr(mv2[:, :], st2[:, :]).then_inc(s("mv2_ready"), 1)

            def tail_n(b, p, hb):
                dve.wait_ge(s("rs2_ready"), b + 1)
                dve.wait_ge(s("x2T_ps"), b + 1)
                dve.wait_ge(s(f"x2_saved{p}"), 16 * hb + 16)
                dve.tensor_scalar(x2s[p][:, :], r2[:, :], mv2[:, 0:1], rs2[:, 0:1], ALU.subtract, ALU.mult).then_inc(s("x2_ready"), 1)

            def route(b):
                dve.wait_ge(s("lg_ps"), b + 1)
                dve.tensor_tensor(lgs[:, :], psS[:, 320:320 + NE], rb[:, :], ALU.add).then_inc(s("lgs_ready"), 1)
                dve.wait_ge(s("lgs_ready"), b + 1)
                pause(dve)
                dve.max(rtop[:, :], lgs[:, :]).then_inc(s("rtop_ready"), 1)
                dve.wait_ge(s("rtop_ready"), b + 1)
                pause(dve)
                dve.max_index(ridx[:, :], rtop[:, :], lgs[:, :]).then_inc(s("ridx_ready"), 1)
                dve.tensor_copy(topl[:, bass.ds(b, 1), :], rtop[:, 0:TOP].unsqueeze(1)).then_inc(s("top_saved"), 1)
                dve.wait_ge(s("ridx_ready"), b + 1)
                dve.tensor_copy(topi[:, bass.ds(b, 1), :], ridx[:, 0:TOP].unsqueeze(1)).then_inc(s("top_saved"), 1)

            def step(t, h, p, fr, tl, rt):
                maxima(t, 0)
                if tl:
                    tail_o(t - 1)
                maxima(t, 1)
                if fr:
                    front_q(t + 1, 1 - p)
                    front_s(t + 1)
                split(t, p, 0)
                if tl:
                    tail_r(t - 1)
                split(t, p, 1)
                split(t, p, 2)
                if fr:
                    front_c(t + 1, 1 - p)
                split(t, p, 3)
                if tl:
                    tail_n(t - 1, 1 - p, h - 1 + p)
                if rt:
                    route(t - 2)

            def first():
                front_q(0, 0)
                front_s(0)
                front_c(0, 0)

            def last():
                tail_o(B - 1)
                tail_r(B - 1)
                tail_n(B - 1, 1, B // 2 - 1)
                for b in range(B - 3, B):
                    route(b)

            steps(dve, step, first, last)

            psB, psY3 = banks[7], banks[4:6]
            dve.wait_ge(s("top_saved"), 2 * B)
            dve.tensor_tensor(gates[:, :, :], topl[:, :, :], topl[:, :, 0:1].to_broadcast([P, B, TOP]), ALU.subtract).then_inc(s("gates0"), 1)
            dve.wait_ge(s("gates1"), 1)
            dve.tensor_reduce(gsum[:, :], gates[:, :, :], AX.X, ALU.add).then_inc(s("gsum"), 1)
            dve.wait_ge(s("gsum"), 1)
            dve.reciprocal(grec[:, :], gsum[:, :]).then_inc(s("gsum"), 1)
            dve.wait_ge(s("gsum"), 2)
            dve.tensor_tensor(gates[:, :, :], gates[:, :, :], grec[:, :].unsqueeze(2).to_broadcast([P, B, TOP]), ALU.mult).then_inc(s("gsum"), 1)
            dve.wait_ge(s("gsum"), 3)
            for r in range(TOP):
                dst = oh if r else comb
                if r > 1:
                    dve.wait_ge(s("oh_used"), r - 1)
                dve.tensor_tensor(dst[:, :, :], iotaE[:, :].unsqueeze(1).to_broadcast([P, B, NE]), topi[:, :, r:r + 1].to_broadcast([P, B, NE]), ALU.is_equal).then_inc(s("oh_a"), 1)
                dve.wait_ge(s("oh_a"), r + 1)
                dve.tensor_tensor(dst[:, :, :], dst[:, :, :], gates[:, :, r:r + 1].to_broadcast([P, B, NE]), ALU.mult).then_inc(s("oh_b"), 1)
                dve.wait_ge(s("oh_b"), r + 1)
                if r:
                    dve.tensor_tensor(comb[:, :, :], comb[:, :, :], oh[:, :, :], ALU.add).then_inc(s("oh_used"), 1)
            dve.wait_ge(s("oh_used"), 3)
            dve.sem_inc(s("comb_ready"), 1)
            for t in range(B):
                dve.wait_ge(s("b_ps"), t + 1)
                dve.tensor_copy(acc[:, t * E:(t + 1) * E], psB[:, 0:E]).then_inc(s("acc_init"), 1)
            dve.sem_inc(s("acc_ready"), 2)
            dve.wait_ge(s("acc_init"), B)
            dve.sem_inc(s("y_credit"), 2)
            with dve.Fori(0, NE) as e:
                for g in range(NG):
                    u = e * NG + g
                    dve.wait_ge(s("y_units"), u + 1)
                    dve.wait_ge(s("acc_ready"), u + 2)
                    dve.sem_inc(s("y_credit"), 1)
                    for j in range(GB):
                        t = g * GB + j
                        a = acc[:, t * E:(t + 1) * E]
                        cc = comb[:, :, :].rearrange("p b e -> p (b e)")[:, bass.ds(e + t * NE, 1)]
                        ins = dve.scalar_tensor_tensor(a, psY3[g % 2][:, j * E:(j + 1) * E], cc, a, ALU.mult, ALU.add)
                    ins.then_inc(s("acc_ready"), 1)
            dve.wait_ge(s("acc_ready"), NG * NE + 2)
            for p in range(2):
                dve.wait_ge(s(f"x2_saved{p}"), 16 * (B // 2) + 16)
            Xf = X[:, :, :].rearrange("p b e -> p (b e)")
            dve.tensor_tensor(acc[:, :], acc[:, :], Xf, ALU.add).then_inc(s("r3"), 1)
            dve.wait_ge(s("r3"), 1)
            for t in range(B):
                ins = dve.bn_stats(st3[:, t, :], acc[:, t * E:(t + 1) * E])
            ins.then_inc(s("r3"), 1)
            dve.wait_ge(s("r3"), 2)
            for t in range(B):
                ins = dve.bn_aggr(mv3[:, t, :], st3[:, t, :])
            ins.then_inc(s("mv3_ready"), 1)
            dve.wait_ge(s("rs3_ready"), 1)
            for t in range(B):
                ins = dve.tensor_scalar(Xf[:, t * E:(t + 1) * E], acc[:, t * E:(t + 1) * E], mv3[:, t, 0:1], rs3[:, t:t + 1], ALU.subtract, ALU.mult)
            ins.then_inc(s("x3_ready"), 1)


def layout(I):
    f = lambda a: np.ascontiguousarray(a)
    x = np.asarray(I["x"])
    B, T, E = x.shape
    return {
        "x": f(x.transpose(1, 0, 2)),
        "xT": f(x.reshape(B * T, E).T),
        "wk": f(I["L0_attn_Wk"]), "wq": f(I["L0_attn_Wq"]), "wv": f(I["L0_attn_Wv"]), "wo": f(I["L0_attn_Wo"]),
        "g1": f(I["L0_attn_G1"]), "g2": f(I["L0_attn_G2"]),
        "ctxT": f(np.asarray(I["ctx_1024"]).transpose(0, 2, 1)),
        "cwq": f(I["L0_xattn_Wq"]), "cwqT": f(np.asarray(I["L0_xattn_Wq"]).T), "cwkvT": f(np.asarray(I["L0_xattn_Wkv"]).T), "cwcT": f(np.asarray(I["L0_xattn_Wc"]).T),
        "rw": f(I["L0_ffn_router_w"]), "rb": f(np.broadcast_to(np.asarray(I["L0_ffn_router_b"]), (T, I["L0_ffn_router_b"].shape[0]))),
        "b1T": f(np.asarray(I["L0_ffn_b1"]).reshape(-1, E).T), "b2": f(I["L0_ffn_b2"]),
        "w1": f(I["L0_ffn_w1"]), "w2": f(I["L0_ffn_w2"]),
        "delta": f(I["L0_attn_delta"]).reshape(E, 1), "norm_w": f(I["L0_attn_norm_w"]).reshape(E, 1),
    }


def kernel(**inputs):
    laid = layout(inputs)
    B, T, E = np.asarray(inputs["x"]).shape
    nc = _bacc.Bacc("TRN2", target_bir_lowering=False, num_devices=1)
    A = {name: nc.dram_tensor(name + "_dram", a.shape, _mybir.dt.from_np(a.dtype), kind="ExternalInput").ap() for name, a in laid.items()}
    out = nc.dram_tensor("out_dram", (T, B, E), _mybir.dt.float32, kind="ExternalOutput").ap()
    build(nc, A, out)
    nc.compile()
    r = _run(nc, [{name + "_dram": a for name, a in laid.items()}], core_ids=[0])
    return np.ascontiguousarray(np.asarray(r.results[0]["out_dram"]).transpose(1, 0, 2))
```

```python
from contextlib import ExitStack

import concourse.bacc as _bacc
import concourse.mybir as _mybir
import numpy as np
from concourse.bass_utils import run_bass_kernel_spmd as _run


def build(nc, A, out):
    import concourse.bass as bass
    from concourse import mybir

    ALU = mybir.AluOpType
    ACT = mybir.ActivationFunctionType
    AX = mybir.AxisListType
    F32 = mybir.dt.float32
    U32 = mybir.dt.uint32
    F16 = mybir.dt.float16

    P = 128
    E = 128
    B = A["x"].shape[1]
    T = 128
    GB = 4
    GC = GB * T
    NG = B // GB
    H = 2
    DH = E // H
    HALVES = [64, 32, 16, 8]
    NL = len(HALVES)
    LEAF = 8
    FLOOR = 20.0
    EPS = 1e-5

    with ExitStack() as ctx:
        def sb(name, shape, dt=F32):
            return ctx.enter_context(nc.sbuf_tensor(name, shape, dt))

        def sem(name):
            return ctx.enter_context(nc.semaphore(name))

        banks = [ctx.enter_context(nc.psum_tensor(f"bank{i}", [P, 512], F32)) for i in range(8)]

        X = sb("X", [P, B, E])
        wk, wq, wv, wo = (sb(n, [P, E]) for n in ("wk", "wq", "wv", "wo"))
        g1 = sb("g1", [P, DH])
        g2 = sb("g2", [DH, E])
        delta = sb("delta", [P, 1])
        norm_w = sb("norm_w", [P, 1])
        won = sb("won", [P, E])
        ident = sb("ident", [P, P])
        restart = sb("restart", [P, GC])
        lmask = [sb(f"lmask{h}", [P, 64]) for h in HALVES]
        leafmask = sb("leafmask", [P, P])

        C = A["ctxT"].shape[2]
        NH = 16
        DX = E // NH
        QD = 4
        NQ = NH // QD
        KV = DX + 1
        cwq = sb("cwq", [P, E])
        cwqT = sb("cwqT", [P, E])
        cwkvT = sb("cwkvT", [P, 2 * DX])
        cwcT = sb("cwcT", [P, E])
        wqs = sb("wqs", [P, NQ, 3, QD * DX])
        wks = sb("wks", [P, P // DX, DX])
        ident16, ones16 = sb("ident16", [P, P], F16), sb("ones16", [P, P], F16)
        iotaC = sb("iotaC", [P, C])
        thr, mult = sb("thr", [P, 1]), sb("mult", [P, 1])
        bmask = sb("bmask", [P, QD], F16)
        x1s = [sb(f"x1s{p}", [P, E]) for p in range(4)]
        ctxs = [sb(f"ctxs{p}", [P, C]) for p in range(4)]
        FW = E + 2 * C
        Fs = [sb(f"Fs{p}", [P, FW]) for p in range(4)]
        mv9 = [sb(f"mv9{p}", [C, KV]) for p in range(4)]
        qs = [sb(f"qs{p}", [P, NQ, T], F16) for p in range(4)]
        top8 = sb("top8", [P, 8])
        idx8 = sb("idx8", [P, 8], U32)
        idxf = sb("idxf", [P, 1])
        onehot = [sb(f"onehot{p}", [P, C], F16) for p in range(2)]
        src = [sb(f"src{p}", [P, C], F16) for p in range(2)]
        bd = [sb(f"bd{p}", [P, QD, C], F16) for p in range(4)]
        w9 = [sb(f"w9{p}", [C, 32]) for p in range(4)]
        picks = sb("picks", [P, NQ, KV])
        outT = sb("outT", [P, QD * T])
        mx16 = [sb(f"mx16{p}", [P, NH], F16) for p in range(2)]
        Ex = [sb(f"Ex{p}", [C, NQ, QD * T]) for p in range(2)]
        rden = sb("rden", [P, NH])
        at = [sb(f"at{p}", [P, E]) for p in range(2)]
        aT = sb("aT", [P, E])
        r2 = [sb(f"r2{p}", [P, E]) for p in range(2)]
        st2 = sb("st2", [P, 6])
        mv2 = [sb(f"mv2{p}", [P, 2]) for p in range(2)]
        ln2 = sb("ln2", [P, 1])
        rs2 = [sb(f"rs2{p}", [P, 1]) for p in range(2)]
        c_av, c_y2, c_s, c_n, c_n1, c_lg, c_rk = 0, 144, 272, 352, 430, 432, 448

        NE = A["rw"].shape[1]
        TOP = 4
        I = A["w1"].shape[2]
        NI = I // P
        N_TOK = B * T
        CAP = N_TOK + P
        LAST = NE * CAP
        NT = N_TOK * TOP // P + NE
        UNROLL = 12
        QUAD = 4
        LEAD_T, LEAD_H = 3, 2
        NL_ = NT + UNROLL
        ROW = 192
        RW = E + 1
        NOWHERE = 1 << 20
        WROW = I + NI * E + NI + E
        xs = nc.dram_tensor("xs", [LAST + P, ROW], F32).ap()
        ys = nc.dram_tensor("ys", [N_TOK * TOP, E], F32).ap()
        rw = sb("rw", [P, NE])
        rb = sb("rb", [P, NE])
        xrow = [sb(f"xrow{p}", [P, TOP, E + 4]) for p in range(4)]
        x2Tb = sb("x2Tb", [P, T])
        lgs = sb("lgs", [P, NE])
        rtop = sb("rtop", [P, 8])
        ridx = sb("ridx", [P, 8], U32)
        topi = sb("topi", [P, TOP])
        onehots = sb("onehots", [P, TOP, NE])
        slotsel = sb("slotsel", [P, TOP, NE])
        chosen = sb("chosen", [P, NE], F16)
        before = sb("before", [P, NE], F16)
        slot_e = sb("slot_e", [P, NE])
        slotf = sb("slotf", [P, TOP])
        slots = [sb(f"slots{p}", [P, TOP], U32) for p in range(4)]
        results = sb("results", [P, B, TOP], U32)
        topl, gates = (sb(n, [P, B, TOP]) for n in ("topl", "gates"))
        gsum, grec = sb("gsum", [P, B]), sb("grec", [P, B])
        iotaE, baseE = sb("iotaE", [P, NE]), sb("baseE", [P, NE])
        upper16 = sb("upper16", [P, P], F16)
        pad = sb("pad", [P, RW])
        JT = N_TOK // P + 1
        steps128 = sb("steps128", [1, JT])
        tile_no = sb("tile_no", [1, NL_])
        ones_e, capE = sb("ones_e", [1, NE]), sb("capE", [P, NE])
        first_part = ExitStack()

        def passing(name, shape, dt=F32):
            return first_part.enter_context(nc.sbuf_tensor(name, shape, dt))

        xTg = [passing(f"xTg{p}", [P, GC]) for p in range(2)]
        uS, soft, kk, k, qc, sq_, q, N, gc, sg_ = (passing(n, [P, GC]) for n in ("uS", "soft", "kk", "k", "qc", "sigq", "q", "N", "gc", "lgate"))
        gate = [passing(f"gate{p}", [P, GC]) for p in range(2)]
        v = [passing(f"v{p}", [P, GC]) for p in range(2)]
        zT = passing("zT", [DH, GC])
        dec = [passing(f"dec{l}", [P, GC]) for l in range(NL + 1)]
        decK = passing("decK", [P, GC])
        Lk = [passing(f"Lk{l}", [P, GC]) for l in range(NL + 1)]
        Rq = [passing(f"Rq{l}", [P, GB, H, T // 2]) for l in range(NL)]
        Rleaf = passing("Rleaf", [P, GB, H, T])
        AT = passing("AT", [P, GB, H, T])
        og, osq, on, oT, r1 = (passing(n, [P, GC]) for n in ("og", "osq", "on", "oT", "r1"))
        ss, lss, rss = (passing(n, [P, GB * H]) for n in ("ss", "lss", "rss"))
        st1 = passing("st1", [P, GB, 6])
        mv1 = passing("mv1", [P, GB, 2])
        ln1, rs1, nm1 = (passing(n, [P, GB]) for n in ("ln1", "rs1", "nm1"))
        first_part.close()

        count = sb("count", [1, NE])
        over = sb("over", [1, NE, JT])
        ntile, last_tile = sb("ntile", [1, NE]), sb("last_tile", [1, NE])
        padf, pad_at = sb("padf", [1, NE]), sb("pad_at", [1, NE], U32)
        past = sb("past", [1, NL_, NE])
        expert, done_t, rowf, colf = (sb(n, [1, NL_]) for n in ("expert", "done_t", "rowf", "colf"))
        tile_row, tile_col = sb("tile_row", [1, NL_], U32), sb("tile_col", [1, NL_], U32)
        wall = sb("wall", [P, NE, WROW])
        wcur = [sb(f"wcur{p}", [P, WROW]) for p in range(QUAD)]
        xin = [sb(f"xin{p}", [P, RW]) for p in range(UNROLL)]
        xinT = [sb(f"xinT{p}", [P, P]) for p in range(4)]
        hid = [sb(f"hid{p}", [P, NI, P]) for p in range(3)]
        yout = [sb(f"yout{p}", [P, E]) for p in range(UNROLL)]
        yin = [sb(f"yin{p}", [P, TOP, E]) for p in range(4)]
        r3 = [sb(f"r3{p}", [P, E]) for p in range(2)]
        o3 = [sb(f"o3{p}", [P, E]) for p in range(2)]
        st3 = [sb(f"st3{p}", [P, 6]) for p in range(2)]
        mv3 = [sb(f"mv3{p}", [P, 2]) for p in range(2)]
        ln3 = sb("ln3", [P, 1])
        rs3 = [sb(f"rs3{p}", [P, 1]) for p in range(2)]

        S = {}

        def s(name):
            if name not in S:
                S[name] = sem(name)
            return S[name]

        def pause(eng):
            eng.sem_inc(s("waits_over"), 1)

        block = ctx.enter_context(nc.Block())

        weights_dma = ["wk", "wq", "wv", "wo", "g1", "g2", "delta", "norm_w", "cwq", "cwqT", "cwkvT", "cwcT", "rw", "rb"]
        WN = 16 * len(weights_dma)
        MASKED = -30000.0
        SCALE = float(1.0 / np.sqrt(np.float32(DX)))

        FIRST, FULL, REST = -3, 9, B - 3

        def steps(eng, step):
            for c in range(FIRST, FULL):
                step(0, c)
            with eng.Fori(0, (REST - FULL) // 4) as i:
                for d in range(4):
                    step(i, FULL + d)
            for c in range(REST, B + 5):
                step(0, c)

        def there(i, c):
            return not isinstance(i, int) or 0 <= c < B

        def free(eng, name, n):
            if not (isinstance(n, int) and n < 1):
                eng.wait_ge(s(name), n)

        setup_steps = {}

        def pad_rows(eng, half):
            with ExitStack() as regs:
                at = [regs.enter_context(eng.register(f"pad_at{half}_{j}")) for j in range(4)]
                for e in range(half * NE // 2, (half + 1) * NE // 2):
                    if e % 4 == 0:
                        eng.reg_load(at, pad_at[0:1, e:e + 4])
                    eng.dma_start(xs[bass.ds(eng.snap(at[e % 4], min_val=0, max_val=LAST - P), P), 0:RW], pad[:, :]).then_inc(s(f"pads{half}"), 16)

        @block.sync
        def _(sp):
            for name, t in zip(weights_dma, (wk, wq, wv, wo, g1, g2, delta, norm_w, cwq, cwqT, cwkvT, cwcT, rw, rb)):
                sp.dma_start(t[:, :], A[name]).then_inc(s("weights_in"), 16)
            for g in range(2):
                sp.dma_start(xTg[g][:, :], A["xT"][:, g * GC:(g + 1) * GC]).then_inc(s(f"xT_in{g}"), 16)
            sp.dma_start(X[:, :, :], A["x"]).then_inc(s("x_in"), 16)
            with sp.Fori(0, NG // 2 - 1) as i:
                for p in range(2):
                    g = 2 * i + p
                    sp.wait_ge(s("v_ps"), g + 1)
                    sp.dma_start(xTg[p][:, :], A["xT"][:, bass.ds((g + 2) * GC, GC)]).then_inc(s(f"xT_in{p}"), 16)
            sp.wait_ge(s("x1_ready"), NG)

            def fetch(b, p):
                sp.dma_start(x1s[p][:, :], X[:, :, :].rearrange("p b e -> p (b e)")[:, bass.ds(b * E, E)]).then_inc(s(f"cross_in{p}"), 16)
                sp.dma_start(ctxs[p][:, :], A["ctxT"].rearrange("b p c -> p b c")[:, bass.ds(b, 1), :]).then_inc(s(f"cross_in{p}"), 16)

            def refetch(b, p):
                sp.wait_ge(s("F_ps"), b + 1)
                pause(sp)
                fetch(b + 4, p)

            def save(b, p):
                sp.wait_ge(s("x2_ready"), b + 1)
                pause(sp)
                sp.dma_start(X[:, :, :].rearrange("p b e -> p (b e)")[:, bass.ds(b * E, E)], xrow[p][:, 0, 0:E]).then_inc(s(f"x2_saved{p}"), 16)

            for b in range(4):
                fetch(b, b)
            sp.dma_start(wall[:, :, 0:I], A["w1"].rearrange("e p i -> p e i")).then_inc(s("wall_in"), 16)
            for c in range(NI):
                sp.dma_start(wall[:, :, I + c * E:I + (c + 1) * E], A["w2"].rearrange("e (c p) d -> c p e d", p=P)[c]).then_inc(s("wall_in"), 16)
            sp.dma_start(wall[:, :, 2 * I:2 * I + NI], A["b1T"]).then_inc(s("wall_in"), 16)
            sp.dma_start(wall[:, :, 2 * I + NI:WROW], A["b2rep"]).then_inc(s("wall_in"), 16)
            for b in range(8):
                refetch(b, b % 4)
            with sp.Fori(0, B // 4 - 3) as i:
                for p in range(4):
                    refetch(4 * i + 8 + p, p)
                    save(4 * i + p, p)
            for b in range(B - 12, B):
                save(b, b % 4)
            sp.wait_ge(s("tables"), 1)
            pad_rows(sp, 0)
            sp.dma_start(xs[LAST:LAST + P, 0:RW], pad[:, :]).then_inc(s("pads0"), 16)
            sp.wait_ge(s("pads0"), 16 * (NE // 2 + 1))
            sp.wait_ge(s("pads1"), 16 * (NE // 2))
            for p in range(4):
                sp.wait_ge(s(f"scattered{p}"), 16 * TOP * (B // 4))
            with ExitStack() as regs:
                row = [regs.enter_context(sp.register(f"row{j}")) for j in range(QUAD)]

                def load(i, written):
                    for p in range(UNROLL):
                        if p % QUAD == 0:
                            sp.reg_load(row, tile_row[0:1, bass.ds(i + p, QUAD)])
                        if written is not None:
                            sp.wait_ge(s(f"y_out{p}"), written)
                            pause(sp)
                        sp.dma_start(xin[p][:, :], xs[bass.ds(sp.snap(row[p % QUAD], min_val=0, max_val=LAST), P), 0:RW]).then_inc(s(f"x_row_in{p}"), 16)

                load(0, None)
                with sp.Fori(0, NT // UNROLL) as i:
                    load(i * UNROLL + UNROLL, 16 * i + 16)
            for p in range(UNROLL):
                sp.wait_ge(s(f"y_out{p}"), 16 * (NT // UNROLL))
            y4 = ys.rearrange("(b p k) e -> p b (k e)", p=P, k=TOP)

            def load_y(b, p):
                if not (isinstance(b, int) and b < 4):
                    sp.wait_ge(s("r3_ready"), b - 3)
                    pause(sp)
                sp.dma_start(yin[p][:, :, :].rearrange("p k e -> p (k e)").unsqueeze(1), y4[:, bass.ds(b, 1), :]).then_inc(s(f"y_in{p}"), 16)

            def store(b, p):
                sp.wait_ge(s("x3_ready"), b + 1)
                pause(sp)
                sp.dma_start(out[:, bass.ds(b, 1), :], o3[p][:, :].unsqueeze(1)).then_inc(s(f"out{p}"), 16)

            for b in range(4):
                load_y(b, b)
            with sp.Fori(0, B // 4 - 1) as i:
                for p in range(4):
                    load_y(4 * i + 4 + p, p)
                    store(4 * i + p, p % 2)
            for b in range(B - 4, B):
                store(b, b % 2)
            for p in range(2):
                sp.wait_ge(s(f"out{p}"), 16 * (B // 2))

        @block.gpsimd
        def _(pool):
            n = 0

            def done(ins):
                nonlocal n
                n += 1
                ins.then_inc(s("pool_setup"), 1)
                pool.wait_ge(s("pool_setup"), n)

            def keep(v, pattern, base, channel, fill=0.0, op=ALU.is_ge):
                done(pool.affine_select(out=v, in_=v, compare_op=op, fill=fill, base=base, pattern=pattern, channel_multiplier=channel))

            done(pool.memset(ident[:, :], 0.0))
            keep(ident[:, :], [[-1, P]], 0, 1, fill=1.0, op=ALU.not_equal)
            for m, h in zip(lmask, HALVES):
                v3 = m[:, :].rearrange("p (b r) -> p b r", r=h)
                nb = 64 // h
                done(pool.memset(m[:, :], 1.0))
                keep(v3, [[-2 * h, nb], [0, h]], 0, 1)
                keep(v3, [[2 * h, nb], [0, h]], h - 1, -1)
            v3 = leafmask[:, :].rearrange("p (b r) -> p b r", r=LEAF)
            nb = T // LEAF
            done(pool.memset(leafmask[:, :], 1.0))
            keep(v3, [[-LEAF, nb], [0, LEAF]], 0, 1)
            keep(v3, [[LEAF, nb], [1, LEAF]], 0, -1)
            setup_steps["masks"] = n

            done(pool.memset(ones16[:, :], 1.0))
            done(pool.memset(ident16[:, :], 0.0))
            keep(ident16[:, :], [[-1, P]], 0, 1, fill=1.0, op=ALU.not_equal)
            done(pool.memset(thr[:, :], 0.5))
            done(pool.memset(thr[96:96 + QD, :], 1e9))
            done(pool.memset(mult[:, :], MASKED / (P - 96 - QD)))
            done(pool.memset(mult[96:96 + QD, :], -1.0))
            done(pool.memset(bmask[:, :], 1.0))
            keep(bmask[96:96 + QD, :], [[-1, QD]], 0, 1, op=ALU.is_equal)
            for blk in range(3):
                rows = bmask[32 * blk:32 * blk + 32, :]
                keep(rows, [[-DX, QD]], 0, 1)
                keep(rows, [[DX, QD]], DX - 1, -1)
            done(pool.iota(iotaC[:, :], pattern=[[1, C]], base=0, channel_multiplier=0, allow_small_or_imprecise_dtypes=True))
            done(pool.memset(upper16[:, :], 1.0))
            keep(upper16[:, :], [[1, P]], -1, -1)
            done(pool.iota(results[:, :, :], pattern=[[P * TOP, B], [1, TOP]], base=0, channel_multiplier=TOP))
            done(pool.iota(capE[:, :], pattern=[[CAP, NE]], base=0, channel_multiplier=0, allow_small_or_imprecise_dtypes=True))
            done(pool.iota(steps128[:, :], pattern=[[P, JT]], base=0, channel_multiplier=0, allow_small_or_imprecise_dtypes=True))
            done(pool.iota(tile_no[:, :], pattern=[[1, NL_]], base=0, channel_multiplier=0, allow_small_or_imprecise_dtypes=True))
            done(pool.memset(ones_e[:, :], 1.0))
            done(pool.memset(pad[:, 0:E], 0.0))
            done(pool.iota(pad[:, E:RW].bitcast(U32), pattern=[[1, 1]], base=NOWHERE, channel_multiplier=0))
            done(pool.iota(iotaE[:, :], pattern=[[1, NE]], base=0, channel_multiplier=0, allow_small_or_imprecise_dtypes=True))
            for p in range(4):
                done(pool.memset(qs[p][96:128, :, :], 1.0))
                done(pool.memset(mv9[p][:, DX:KV], 1.0))
                done(pool.memset(w9[p][:, :], 0.0))
            done(pool.memset(picks[:, :, :], 0.0))
            keep(picks[:, :, :], [[-32, NQ], [-1, KV]], 0, 1, fill=1.0, op=ALU.not_equal)
            setup_steps["cross"] = n

            words = xs.rearrange("n w -> (n w)").unsqueeze(1)

            def keys(i, c):
                b, p = 4 * i + c, c % 4
                mk = Fs[p][:, E + C:E + 2 * C]
                pool.wait_ge(s("F_ready"), b + 1)
                free(pool, "bd_ready", b)
                pause(pool)
                pool.tensor_copy(src[p % 2][0:96, :], mk[0:96, :]).then_inc(s("src_steps"), 1)
                pool.wait_ge(s("src_steps"), 2 * b + 1)
                pool.tensor_tensor(src[p % 2][0:32, :], mk[0:32, :], src[p % 2][0:32, :], ALU.subtract).then_inc(s("src_steps"), 1)
                pool.wait_ge(s("src_steps"), 2 * b + 2)
                pool.wait_ge(s("aux_ready"), b + 1)
                free(pool, "L2_ps", NQ * (b - 3))
                pool.tensor_tensor(bd[p][:, :, :], src[p % 2][:, :].unsqueeze(1).to_broadcast([P, QD, C]),
                                   bmask[:, :].unsqueeze(2).to_broadcast([P, QD, C]), ALU.mult).then_inc(s("bd_ready"), 1)

            def scatter(i, c):
                b, p = 4 * i + c, c % 4
                pool.wait_ge(s("slots_ready"), b + 1)
                pause(pool)
                for r in range(TOP):
                    pool.indirect_dma_start(words, bass.IndirectOffsetOnAxis(ap=slots[p][:, r:r + 1], axis=0),
                                            xrow[p][:, r, 0:RW], None).then_inc(s(f"scattered{p}"), 16)

            def step(i, c):
                if there(i, c + 1):
                    keys(i, c + 1)
                if there(i, c - 5):
                    scatter(i, c - 5)

            steps(pool, step)

            with pool.Fori(0, NT // UNROLL) as i:
                for p in range(UNROLL):
                    pool.wait_ge(s("y_ready"), UNROLL * i + p + 1 + 3)
                    pause(pool)
                    pool.indirect_dma_start(ys, bass.IndirectOffsetOnAxis(ap=xin[p][:, :].bitcast(U32)[:, E:RW], axis=0), yout[p][:, :], None,
                                            bounds_check=N_TOK * TOP - 1, oob_is_err=False).then_inc(s(f"y_out{p}"), 16)

        @block.tensor
        def _(pe):
            psU, psQ, psV, psG = banks[0], banks[1], banks[2], banks[3]
            psZ = banks[3]
            psA = banks[4:6]
            psO, psT, psY = banks[6], banks[7], banks[7]

            def project(g, p, n16, first=False):
                pe.wait_ge(s(f"xT_in{p}"), n16)
                if not first:
                    pe.wait_ge(s("u_ready"), g)
                pe.matmul(psU[:, :], wk[:, :], xTg[p][:, :], start=True, stop=True).then_inc(s("u_ps"), 1)
                if not first:
                    pe.wait_ge(s("qc_ready"), g)
                pe.matmul(psQ[:, :], wq[:, :], xTg[p][:, :], start=True, stop=True).then_inc(s("q_ps"), 1)
                if not first:
                    pe.wait_ge(s("gc_ready"), g)
                pe.matmul(psZ[0:DH, :], g1[:, :], xTg[p][:, :], start=True, stop=True).then_inc(s("z_ps"), 1)
                if not first:
                    pe.wait_ge(s("v_ready"), g)
                for b in range(GB):
                    mm = pe.matmul(psV[:, b * E:(b + 1) * E], xTg[p][:, b * T:(b + 1) * T], wv[:, :], start=True, stop=True)
                mm.then_inc(s("v_ps"), 1)
                pe.wait_ge(s("zT_ready"), g + 1)
                for b in range(GB):
                    mm = pe.matmul(psG[:, b * E:(b + 1) * E], zT[:, b * T:(b + 1) * T], g2[:, :], start=True, stop=True)
                mm.then_inc(s("g_ps"), 1)

            def attend(g, p):
                for l in range(NL):
                    pe.wait_ge(s("LR_ready"), (NL + 1) * g + l + 1)
                    if l >= 2:
                        pe.wait_ge(s("A_taken"), (NL + 2) * g + l - 1)
                    for b in range(GB):
                        mm = pe.matmul(psA[l % 2][:, b * T:(b + 1) * T], Lk[l][:, b * T:(b + 1) * T], Rq[l][:, b, :, :], start=True, stop=True)
                    mm.then_inc(s("A_ps"), 1)
                pe.wait_ge(s("LR_ready"), (NL + 1) * g + NL + 1)
                for j in range(2):
                    pe.wait_ge(s("A_taken"), (NL + 2) * g + NL + j - 1)
                    for b in range(2):
                        bb = 2 * j + b
                        mm = pe.matmul(psA[j][:, b * 2 * T:(b + 1) * 2 * T], Lk[NL][:, bb * T:(bb + 1) * T], Rleaf[:, bb, :, :], start=True, stop=True)
                    mm.then_inc(s("A_ps"), 1)
                pe.wait_ge(s("A_taken"), (NL + 2) * (g + 1))
                for b in range(GB):
                    for h in range(H):
                        c = b * E + h * DH
                        mm = pe.matmul(psO[:, c:c + DH], AT[:, b, h, :], v[p][:, c:c + DH], start=True, stop=True)
                mm.then_inc(s("o_ps"), 1)
                pe.wait_ge(s("on_ready"), g + 1)
                for b in range(GB):
                    mm = pe.transpose(psT[:, b * T:(b + 1) * T], on[:, b * E:(b + 1) * E], ident[:, :])
                mm.then_inc(s("oT_ps"), 1)
                pe.wait_ge(s("oT_ready"), g + 1)
                for b in range(GB):
                    mm = pe.matmul(psY[:, b * E:(b + 1) * E], oT[:, b * T:(b + 1) * T], won[:, :], start=True, stop=True)
                mm.then_inc(s("y_ps"), 1)

            pe.wait_ge(s("weights_in"), WN)
            pe.wait_ge(s("pool_setup"), setup_steps["masks"])
            pe.wait_ge(s("won_ready"), 1)
            project(0, 0, 16, first=True)

            def step(i, last=False):
                project(2 * i + 1, 1, 16 * i + 16)
                attend(2 * i, 0)
                if not last:
                    project(2 * i + 2, 0, 16 * i + 32)
                attend(2 * i + 1, 1)

            with pe.Fori(0, NG // 2 - 1) as i:
                step(i)
            step(NG // 2 - 1, last=True)

            psF, psQx, psD, psL1, psV, psL2, psT = banks[0], banks[1], banks[2], banks[3], banks[4], banks[5:7], banks[7]
            pe.wait_ge(s("pool_setup"), setup_steps["cross"])
            pe.wait_ge(s("wqs_ready"), 2)
            pe.wait_ge(s("x1_ready"), NG)

            def front(i, c):
                b, p = 4 * i + c, c % 4
                pe.wait_ge(s(f"cross_in{p}"), 32 * (i + c // 4) + 32)
                free(pe, "F_ready", b)
                pe.transpose(psF[:, 0:E], x1s[p][:, :], ident[:, :])
                pe.matmul(psF[:, E:E + C], cwq[:, :], ctxs[p][:, :], start=True, stop=True)
                pe.matmul(psF[:, E + C:E + 2 * C], wks[:, :, :].rearrange("p r d -> p (r d)"), ctxs[p][:, :], start=True, stop=True)
                pe.matmul(psF[0:C, FW:FW + DX], ctxs[p][:, :], cwkvT[:, DX:2 * DX], start=True, stop=True).then_inc(s("F_ps"), 1)

            def queries(i, c):
                b, p = 4 * i + c, c % 4
                pe.wait_ge(s("F_ready"), b + 1)
                free(pe, "qlo_ready", b)
                for j in range(NQ):
                    mm = pe.matmul(psQx[0:96, j * T:(j + 1) * T], wqs[:, j, :, :].rearrange("p r d -> p (r d)"), Fs[p][:, 0:E], start=True, stop=True)
                mm.then_inc(s("Qx_ps"), 1)

            def greatest(i, c, j):
                b, p = 4 * i + c, c % 4
                pe.wait_ge(s("bd_ready"), b + 1)
                pe.wait_ge(s("qlo_ready"), b + 1)
                free(pe, "mx_ready", NQ * b + j)
                pe.matmul(psL1[:, 0:QD * C], qs[p][:, j, :], bd[p][:, :, :].rearrange("p h c -> p (h c)"), start=True, stop=True).then_inc(s("L1_ps"), 1)

            def maxrows(i, c):
                b, p = 4 * i + c, c % 4
                pe.wait_ge(s("mx_ready"), NQ * b + NQ)
                free(pe, "E_ready", NQ * b - 1)
                for j in range(NQ):
                    mm = pe.matmul(psL2[0][96:96 + QD, j * T:(j + 1) * T], mx16[p % 2][:, QD * j:QD * j + QD], ident16[:, :], start=True, stop=True)
                mm.then_inc(s("M_ps"), 1)

            def logits(i, c, j):
                b, p = 4 * i + c, c % 4
                pe.wait_ge(s("qmax_ready"), b + 1)
                free(pe, "E_ready", NQ * b + j - 1)
                for h in range(QD):
                    mm = pe.matmul(psL2[j % 2][0:C, h * T:(h + 1) * T], bd[p][:, h, :], qs[p][:, j, :], start=True, stop=True)
                mm.then_inc(s("L2_ps"), 1)

            def values(i, c, half):
                b, p = 4 * i + c, c % 4
                pe.wait_ge(s("E_ready"), NQ * b + NQ)
                free(pe, "outT_ready", b)
                for j in range(2 * half, 2 * half + 2):
                    mm = pe.matmul(psV[32 * j:32 * j + 32, :], w9[p][:, :], Ex[p % 2][:, j, :], start=True, stop=True)
                if half:
                    mm.then_inc(s("V_ps"), 1)

            def back(i, c):
                b = 4 * i + c
                pe.wait_ge(s("outT_ready"), b + 1)
                for h in range(QD):
                    mm = pe.matmul(psD[:, c_av + h * NQ * KV:c_av + (h + 1) * NQ * KV], outT[:, h * T:(h + 1) * T], picks[:, :, :].rearrange("p j v -> p (j v)"), start=True, stop=True)
                return mm

            def selection(i, c):
                b, p = 4 * i + c, c % 4
                pe.wait_ge(s("onehot_ready"), b + 1)
                pe.matmul(psD[:, c_n:c_n + C], ones16[:, :], onehot[p % 2][:, :], start=True, stop=True)
                return pe.matmul(psD[0:C, c_n1:c_n1 + 1], onehot[p % 2][:, :], ones16[:, 0:1], start=True, stop=True)

            def bank_left(i, c):
                t = 4 * i + c
                if there(i, c - 2):
                    pe.wait_ge(s("at_ready"), t - 1)
                elif there(i, c - 3):
                    pe.wait_ge(s("tail_steps"), 2 * (t - 3) + 1)
                elif there(i, c + 2):
                    pe.wait_ge(s("select_steps"), 3 * (t + 2) + 2)
                elif there(i, c - 5):
                    pe.wait_ge(s("slot_e_ready"), t - 4)

            def turn(i, c):
                b, p = 4 * i + c, c % 4
                pe.wait_ge(s("at_ready"), b + 1)
                free(pe, "aT_ready", b)
                pe.transpose(psT[:, 0:E], at[p % 2][:, :], ident[:, :]).then_inc(s("aT_ps"), 1)

            def route_turn(i, c):
                b, p = 4 * i + c, c % 4
                pe.wait_ge(s("x2_ready"), b + 1)
                free(pe, "x2T_ready", b)
                if there(i, c + 1):
                    pe.wait_ge(s("aT_ready"), b + 2)
                pe.transpose(psT[:, E:E + T], xrow[p][:, 0, 0:E], ident[:, :]).then_inc(s("x2T_ps"), 1)

            def step(i, c):
                t = 4 * i + c
                if there(i, c - 1):
                    maxrows(i, c - 1)
                if there(i, c + 3):
                    front(i, c + 3)
                if there(i, c - 1):
                    logits(i, c - 1, 0)
                if there(i, c):
                    greatest(i, c, 0)
                if there(i, c - 3):
                    turn(i, c - 3)
                if there(i, c - 1):
                    logits(i, c - 1, 1)
                if there(i, c + 2):
                    queries(i, c + 2)
                if there(i, c):
                    greatest(i, c, 1)
                if there(i, c - 2):
                    values(i, c - 2, 0)
                if there(i, c):
                    greatest(i, c, 2)
                if there(i, c - 1):
                    logits(i, c - 1, 2)
                if there(i, c - 4):
                    route_turn(i, c - 4)
                if there(i, c - 2):
                    values(i, c - 2, 1)
                if there(i, c):
                    greatest(i, c, 3)
                if there(i, c - 1):
                    logits(i, c - 1, 3)
                last = None
                bank_left(i, c - 1)
                if there(i, c + 2):
                    pe.wait_ge(s("F_ready"), t + 3)
                    p = (c + 2) % 4
                    last = pe.matmul(psD[:, c_s:c_s + C], Fs[p][:, 0:E], Fs[p][:, E:E + C], start=True, stop=True)
                if there(i, c + 1):
                    last = selection(i, c + 1)
                if there(i, c - 3):
                    pe.wait_ge(s("aT_ready"), t - 2)
                    last = pe.matmul(psD[:, c_y2:c_y2 + E], aT[:, :], cwcT[:, :], start=True, stop=True)
                if there(i, c - 5):
                    pe.wait_ge(s("chosen_ready"), t - 4)
                    pe.matmul(psD[:, c_rk:c_rk + NE], upper16[:, :], chosen[:, :], start=True, stop=False)
                    last = pe.matmul(psD[:, c_rk:c_rk + NE], ones16[:, :], before[:, :], start=False, stop=True)
                if there(i, c - 4):
                    pe.wait_ge(s("x2T_ready"), t - 3)
                    last = pe.matmul(psD[:, c_lg:c_lg + NE], x2Tb[:, :], rw[:, :], start=True, stop=True)
                if there(i, c - 2):
                    last = back(i, c - 2)
                if last:
                    last.then_inc(s("bank_ps"), 1)
                else:
                    pe.sem_inc(s("bank_ps"), 1)

            steps(pe, step)

            psC = banks[0]
            pe.wait_ge(s("before_ready"), B + 1)
            pe.matmul(psC[:, 0:NE], ones16[:, :], before[:, :], start=True, stop=True).then_inc(s("count_ps"), 1)

            psX, psH, psY3 = banks[0:2], banks[2:5], banks[5:8]
            pe.wait_ge(s("E_ready"), NQ * B)
            pe.wait_ge(s("tables"), 1)

            def turn_in(i, loaded, p):
                pe.wait_ge(s(f"x_row_in{p}"), loaded)
                if not (isinstance(i, int) and i < 2):
                    pe.wait_ge(s("xinT_ready"), i - 1)
                pe.transpose(psX[p % 2][:, 0:P], xin[p][:, 0:E], ident[:, :]).then_inc(s("xinT_ps"), 1)

            def hidden(i, p):
                pe.wait_ge(s("xinT_ready"), i + 1)
                pe.wait_ge(s("w_ready"), i + 1)
                if not (isinstance(i, int) and i < 3):
                    pe.wait_ge(s("hid_ready"), NI * (i - 2))
                for c in range(NI):
                    mm = pe.matmul(psH[p % 3][:, c * P:(c + 1) * P], wcur[p % QUAD][:, c * P:(c + 1) * P], xinT[p % 4][:, :], start=True, stop=True)
                mm.then_inc(s("hid_ps"), 1)

            def outputs(i, p):
                pe.wait_ge(s("hid_ready"), NI * (i + 1))
                pe.wait_ge(s("y_ready"), i + 1)
                for c in range(NI):
                    mm = pe.matmul(psY3[p % 3][:, 0:E], hid[p % 3][:, c, :], wcur[p % QUAD][:, I + c * E:I + (c + 1) * E], start=(c == 0), stop=(c == NI - 1))
                mm.then_inc(s("result_ps"), 1)

            for i in range(LEAD_T):
                turn_in(i, 16, i)
            for i in range(LEAD_H):
                hidden(i, i)
            with pe.Fori(0, NT // UNROLL) as i:
                for d in range(UNROLL):
                    turn_in(UNROLL * i + d + LEAD_T, 16 * (i + (d + LEAD_T) // UNROLL) + 16, (d + LEAD_T) % UNROLL)
                    hidden(UNROLL * i + d + LEAD_H, (d + LEAD_H) % UNROLL)
                    outputs(UNROLL * i + d, d)

        @block.scalar
        def _(act):
            psQ, psV, psG, psZ, psT = banks[1], banks[2], banks[3], banks[3], banks[7]
            act.preload_act_table_set("natural_log_exp_and_others")
            act.wait_ge(s("weights_in"), WN)

            def project(g, p):
                act.wait_ge(s("z_ps"), g + 1)
                act.activation(zT[:, :], psZ[0:DH, :], ACT.Copy).then_inc(s("zT_ready"), 1)
                act.wait_ge(s("u_ready"), g + 1)
                act.activation(soft[:, :], uS[:, :], ACT.Exp, scale=-1.0).then_inc(s("act_chain"), 1)
                act.wait_ge(s("act_chain"), 6 * g + 1)
                act.activation(soft[:, :], soft[:, :], ACT.Ln, bias=1.0).then_inc(s("soft_ready"), 1)
                act.wait_ge(s("v_ps"), g + 1)
                act.activation(v[p][:, :], psV[:, :], ACT.Copy).then_inc(s("v_ready"), 1)
                act.wait_ge(s("kk_ready"), g + 1)
                act.activation(k[:, :], kk[:, :], ACT.Exp, scale=-1.0).then_inc(s("k_ready"), 1)
                for src, dst, ready, done, n in ((qc, sq_, "qc_ready", "sigq_ready", 0), (gc, sg_, "gc_ready", "gate_ready", 2)):
                    act.wait_ge(s(ready), g + 1)
                    act.activation(dst[:, :], src[:, :], ACT.Exp, scale=-1.0).then_inc(s("act_chain"), 1)
                    act.wait_ge(s("act_chain"), 6 * g + n + 2)
                    act.activation(dst[:, :], dst[:, :], ACT.Ln, bias=1.0).then_inc(s("act_chain"), 1)
                    act.wait_ge(s("act_chain"), 6 * g + n + 3)
                    o = gate[p] if n else dst
                    act.activation(o[:, :], dst[:, :], ACT.Exp, scale=-1.0).then_inc(s(done), 1)
                act.sem_inc(s("act_chain"), 1)

            def decays(g):
                for l in range(NL + 1):
                    act.wait_ge(s("dec_ready"), (NL + 1) * g + l + 1)
                    if l == NL:
                        act.activation(decK[:, :], dec[l][:, :], ACT.Exp).then_inc(s("decK_exp"), 1)
                    act.activation(dec[l][:, :], dec[l][:, :], ACT.Exp, scale=-1.0).then_inc(s("dec_exp"), 1)

            def finish(g, p):
                act.wait_ge(s("og_ready"), g + 1)
                act.activation(osq[:, :], og[:, :], ACT.Square).then_inc(s("osq_ready"), 1)
                act.wait_ge(s("ss_ready"), g + 1)
                act.activation(lss[:, :], ss[:, :], ACT.Ln, bias=EPS, scale=1.0 / DH).then_inc(s("log_steps"), 1)
                act.wait_ge(s("log_steps"), 2 * g + 1)
                act.activation(rss[:, :], lss[:, :], ACT.Exp, scale=-0.5).then_inc(s("rss_ready"), 1)
                act.wait_ge(s("oT_ps"), g + 1)
                act.activation(oT[:, :], psT[:, :], ACT.Copy).then_inc(s("oT_ready"), 1)
                act.wait_ge(s("mv1_ready"), g + 1)
                act.activation(ln1[:, :], mv1[:, :, 1], ACT.Ln, bias=EPS).then_inc(s("log_steps"), 1)
                act.wait_ge(s("log_steps"), 2 * g + 2)
                act.activation(rs1[:, :], ln1[:, :], ACT.Exp, scale=-0.5).then_inc(s("rs1_ready"), 1)

            project(0, 0)

            def step(i, last=False):
                decays(2 * i)
                project(2 * i + 1, 1)
                finish(2 * i, 0)
                decays(2 * i + 1)
                if not last:
                    project(2 * i + 2, 0)
                finish(2 * i + 1, 1)

            with act.Fori(0, NG // 2 - 1) as i:
                step(i)
            step(NG // 2 - 1, last=True)

            psF, psQx, psV, psL2, psT = banks[0], banks[1], banks[4], banks[5:7], banks[7]

            def scales(i, c):
                b, p = 4 * i + c, c % 4
                act.wait_ge(s("mv2_ready"), b + 1)
                free(act, "rs2_ready", b)
                act.activation(ln2[:, :], mv2[p % 2][:, 1:2], ACT.Ln, bias=EPS).then_inc(s("ln2_ready"), 1)
                act.wait_ge(s("ln2_ready"), b + 1)
                act.activation(rs2[p % 2][:, :], ln2[:, :], ACT.Exp, scale=-0.5).then_inc(s("rs2_ready"), 1)

            def front(i, c):
                b, p = 4 * i + c, c % 4
                act.wait_ge(s("F_ps"), b + 1)
                free(act, "bd_ready", b - 3)
                free(act, "bank_ps", b - 4)
                act.activation(mv9[p][:, 0:DX], psF[0:C, FW:FW + DX], ACT.Copy)
                act.activation(Fs[p][:, :], psF[:, 0:FW], ACT.Copy).then_inc(s("F_ready"), 1)

            def queries(i, c):
                b, p = 4 * i + c, c % 4
                act.wait_ge(s("Qx_ps"), b + 1)
                free(act, "L2_ps", NQ * (b - 3))
                act.activation(qs[p][0:96, :, :].rearrange("p j t -> p (j t)"), psQx[0:96, :], ACT.Copy).then_inc(s("qhi_ready"), 1)

            def maxrows(i, c):
                b, p = 4 * i + c, c % 4
                act.wait_ge(s("M_ps"), b + 1)
                act.activation(qs[p][96:96 + QD, :, :].rearrange("p j t -> p (j t)"), psL2[0][96:96 + QD, :], ACT.Copy).then_inc(s("qmax_ready"), 1)

            def weights(i, c, j):
                b, p = 4 * i + c, c % 4
                act.wait_ge(s("L2_ps"), NQ * b + j + 1)
                free(act, "at_ready", b - 1)
                act.activation(Ex[p % 2][:, j, :], psL2[j % 2][0:C, :], ACT.Exp).then_inc(s("E_ready"), 1)

            def values(i, c):
                b = 4 * i + c
                act.wait_ge(s("V_ps"), b + 1)
                free(act, "bank_ps", b - 1 + 3 - FIRST)
                act.activation(outT[:, :], psV[:, :], ACT.Copy).then_inc(s("outT_ready"), 1)

            def turned(i, c):
                b, p = 4 * i + c, c % 4
                act.wait_ge(s("aT_ps"), b + 1)
                free(act, "mv2_ready", b)
                act.activation(aT[:, :], psT[:, 0:E], ACT.Copy).then_inc(s("aT_ready"), 1)

            def route(i, c):
                b, p = 4 * i + c, c % 4
                act.wait_ge(s("x2T_ps"), b + 1)
                free(act, "chosen_ready", b)
                act.activation(x2Tb[:, :], psT[:, E:E + T], ACT.Copy).then_inc(s("x2T_ready"), 1)

            def step(i, c):
                if there(i, c - 1):
                    maxrows(i, c - 1)
                if there(i, c + 3):
                    front(i, c + 3)
                if there(i, c - 1):
                    weights(i, c - 1, 0)
                if there(i, c - 4):
                    scales(i, c - 4)
                if there(i, c - 3):
                    turned(i, c - 3)
                if there(i, c - 1):
                    weights(i, c - 1, 1)
                if there(i, c + 2):
                    queries(i, c + 2)
                if there(i, c - 4):
                    route(i, c - 4)
                if there(i, c - 1):
                    weights(i, c - 1, 2)
                if there(i, c - 2):
                    values(i, c - 2)
                if there(i, c - 1):
                    weights(i, c - 1, 3)

            steps(act, step)

            psX, psH = banks[0:2], banks[2:5]
            act.wait_ge(s("gates0"), 1)
            act.activation(gates[:, :, :].rearrange("p b k -> p (b k)"), gates[:, :, :].rearrange("p b k -> p (b k)"), ACT.Exp).then_inc(s("gates1"), 1)
            act.wait_ge(s("tables"), 1)
            pad_rows(act, 1)
            act.preload_act_table_set("gelu_and_others")

            def turned(i, p):
                act.wait_ge(s("xinT_ps"), i + 1)
                if not (isinstance(i, int) and i < 4):
                    act.wait_ge(s("hid_ps"), i - 3)
                act.activation(xinT[p % 4][:, :], psX[p % 2][:, 0:P], ACT.Copy).then_inc(s("xinT_ready"), 1)

            def hidden(i, p):
                act.wait_ge(s("hid_ps"), i + 1)
                if not (isinstance(i, int) and i < 3):
                    act.wait_ge(s("result_ps"), i - 2)
                for c in range(NI):
                    act.activation(hid[p % 3][:, c, :], psH[p % 3][:, c * P:(c + 1) * P], ACT.Gelu,
                                   bias=wcur[p % QUAD][:, 2 * I + c:2 * I + c + 1]).then_inc(s("hid_ready"), 1)

            for i in range(LEAD_T):
                turned(i, i)
            for i in range(LEAD_H):
                hidden(i, i)
            with act.Fori(0, NT // UNROLL) as i:
                for d in range(UNROLL):
                    turned(UNROLL * i + d + LEAD_T, (d + LEAD_T) % UNROLL)
                    hidden(UNROLL * i + d + LEAD_H, (d + LEAD_H) % UNROLL)
            act.preload_act_table_set("natural_log_exp_and_others")

            def finish3(b, p):
                act.wait_ge(s("mv3_ready"), b + 1)
                if not (isinstance(b, int) and b < 1):
                    act.wait_ge(s("rs3_ready"), b)
                act.activation(ln3[:, :], mv3[p][:, 1:2], ACT.Ln, bias=EPS).then_inc(s("ln3_ready"), 1)
                act.wait_ge(s("ln3_ready"), b + 1)
                if not (isinstance(b, int) and b < 2):
                    act.wait_ge(s("x3_ready"), b - 1)
                act.activation(rs3[p][:, :], ln3[:, :], ACT.Exp, scale=-0.5).then_inc(s("rs3_ready"), 1)

            finish3(0, 0)
            finish3(1, 1)
            with act.Fori(1, B // 2) as i:
                for p in range(2):
                    finish3(2 * i + p, p)

        @block.vector
        def _(dve):
            psU, psQ, psG = banks[0], banks[1], banks[3]
            psA = banks[4:6]
            psO, psY = banks[6], banks[7]
            dve.memset(before[:, :], 0.0).then_inc(s("before_ready"), 1)
            dve.memset(restart[:, :], 1.0).then_inc(s("dve_init"), 1)
            dve.memset(AT[:, :, :, :], 0.0).then_inc(s("dve_init"), 1)
            n = 2
            for t in Lk:
                dve.memset(t[:, :], 0.0).then_inc(s("dve_init"), 1)
                n += 1
            for t in [*Rq, Rleaf]:
                dve.memset(t[:, :, :, :], 0.0).then_inc(s("dve_init"), 1)
                n += 1
            dve.wait_ge(s("dve_init"), n)
            dve.memset(restart[:, :].rearrange("p (b t) -> p b t", t=T)[:, :, 0:1], 0.0).then_inc(s("dve_init"), 1)
            dve.wait_ge(s("weights_in"), WN)
            dve.tensor_scalar(won[:, :], wo[:, :], norm_w[:, 0:1], None, ALU.mult).then_inc(s("won_ready"), 1)
            dve.wait_ge(s("dve_init"), n + 1)
            dve.wait_ge(s("pool_setup"), setup_steps["masks"])
            dve.wait_ge(s("x_in"), 16)

            def project(g, p):
                dve.wait_ge(s("u_ps"), g + 1)
                dve.tensor_scalar(uS[:, :], psU[:, :], delta[:, 0:1], -FLOOR, ALU.add, ALU.max).then_inc(s("u_ready"), 1)
                dve.wait_ge(s("q_ps"), g + 1)
                dve.tensor_scalar(qc[:, :], psQ[:, :], -40.0, None, ALU.max).then_inc(s("qc_ready"), 1)
                dve.wait_ge(s("g_ps"), g + 1)
                dve.tensor_scalar(gc[:, :], psG[:, :], -40.0, None, ALU.max).then_inc(s("gc_ready"), 1)
                dve.wait_ge(s("soft_ready"), g + 1)
                dve.tensor_tensor(kk[:, :], uS[:, :], soft[:, :], ALU.add).then_inc(s("kk_ready"), 1)
                dve.tensor_tensor_scan(N[:, :], restart[:, :], soft[:, :], 0.0, ALU.mult, ALU.add).then_inc(s("scan_steps"), 1)
                dve.wait_ge(s("sigq_ready"), g + 1)
                dve.tensor_tensor(q[:, :], qc[:, :], sq_[:, :], ALU.mult).then_inc(s("scan_steps"), 1)

            def attend(g):
                dve.wait_ge(s("scan_steps"), 2 * g + 1)
                for l, h in enumerate(HALVES):
                    nb = GC // (2 * h)
                    n4 = N[:, :].rearrange("p (b s r) -> p b s r", s=2, r=h)
                    d4 = dec[l][:, :].rearrange("p (b s r) -> p b s r", s=2, r=h)
                    anchor = n4[:, :, 0, h - 1:h].to_broadcast([P, nb, h])
                    dve.tensor_tensor(d4[:, :, 1, :], n4[:, :, 1, :], anchor, ALU.subtract)
                    dve.tensor_tensor(d4[:, :, 0, :], anchor, n4[:, :, 0, :], ALU.subtract).then_inc(s("dec_ready"), 1)
                n3 = N[:, :].rearrange("p (b r) -> p b r", r=LEAF)
                mid = n3[:, :, LEAF // 2 - 1:LEAF // 2].to_broadcast([P, GC // LEAF, LEAF])
                dve.tensor_tensor(dec[NL][:, :].rearrange("p (b r) -> p b r", r=LEAF), n3, mid, ALU.subtract).then_inc(s("dec_ready"), 1)
                dve.wait_ge(s("k_ready"), g + 1)
                dve.wait_ge(s("scan_steps"), 2 * g + 2)
                for l, h in enumerate(HALVES):
                    dve.wait_ge(s("dec_exp"), (NL + 1) * g + l + 1)
                    k4, q4, d4, L4 = (t[:, :].rearrange("p (b s r) -> p b s r", s=2, r=h) for t in (k, q, dec[l], Lk[l]))
                    dve.tensor_tensor(L4[:, :, 0, :], k4[:, :, 0, :], d4[:, :, 0, :], ALU.mult)
                    for hd in range(H):
                        hp = slice(hd * DH, (hd + 1) * DH)
                        out_ = Rq[l][hp, :, hd, :].rearrange("p b (n r) -> p b n r", r=h)
                        qv, dv = (t[hp, :].rearrange("p (b n s r) -> p b n s r", b=GB, s=2, r=h)[:, :, :, 1, :] for t in (q, dec[l]))
                        ins = dve.tensor_tensor(out_, qv, dv, ALU.mult)
                    ins.then_inc(s("LR_ready"), 1)
                dve.wait_ge(s("decK_exp"), g + 1)
                dve.wait_ge(s("dec_exp"), (NL + 1) * (g + 1))
                dve.tensor_tensor(Lk[NL][:, :], k[:, :], decK[:, :], ALU.mult)
                for hd in range(H):
                    hp = slice(hd * DH, (hd + 1) * DH)
                    qv, dv = (t[hp, :].rearrange("p (b t) -> p b t", b=GB) for t in (q, dec[NL]))
                    ins = dve.tensor_tensor(Rleaf[hp, :, hd, :], qv, dv, ALU.mult)
                ins.then_inc(s("LR_ready"), 1)
                for l, h in enumerate(HALVES):
                    nb = T // (2 * h)
                    dve.wait_ge(s("A_ps"), (NL + 2) * g + l + 1)
                    if l:
                        dve.wait_ge(s("A_taken"), (NL + 2) * g + l)
                    dst = AT[:, :, :, :].rearrange("p b d (n s r) -> p (b d) n s r", s=2, r=h)[:, :, :, 1, :]
                    src = psA[l % 2][:, :].rearrange("p (m n r) -> p m n r", n=nb, r=h)
                    msk = lmask[l][:, :].bitcast(U32).rearrange("p (n r) -> p n r", r=h).unsqueeze(1).to_broadcast([P, GB * H, nb, h])
                    pause(dve)
                    dve.copy_predicated(dst, msk, src).then_inc(s("A_taken"), 1)
                for j in range(2):
                    dve.wait_ge(s("A_ps"), (NL + 2) * g + NL + j + 1)
                    dve.wait_ge(s("A_taken"), (NL + 2) * g + NL + j)
                    dst = AT[:, 2 * j:2 * j + 2, :, :].rearrange("p b d t -> p (b d) t")
                    src = psA[j][:, :].rearrange("p (m t) -> p m t", t=T)
                    msk = leafmask[:, :].bitcast(U32).unsqueeze(1).to_broadcast([P, 4, T])
                    pause(dve)
                    dve.copy_predicated(dst, msk, src).then_inc(s("A_taken"), 1)

            def finish(g, p):
                dve.wait_ge(s("o_ps"), g + 1)
                dve.wait_ge(s("gate_ready"), g + 1)
                dve.tensor_tensor(og[:, :], psO[:, :], gate[p][:, :], ALU.mult).then_inc(s("og_ready"), 1)
                dve.wait_ge(s("osq_ready"), g + 1)
                dve.tensor_reduce(ss[:, :], osq[:, :].rearrange("p (m d) -> p m d", d=DH), AX.X, ALU.add).then_inc(s("ss_ready"), 1)
                dve.wait_ge(s("rss_ready"), g + 1)
                dve.tensor_tensor(on[:, :].rearrange("p (m d) -> p m d", d=DH), og[:, :].rearrange("p (m d) -> p m d", d=DH),
                                  rss[:, :].unsqueeze(2).to_broadcast([P, GB * H, DH]), ALU.mult).then_inc(s("on_ready"), 1)
                dve.wait_ge(s("y_ps"), g + 1)
                xg = X[:, :, :].rearrange("p b e -> p (b e)")[:, bass.ds(g * GC, GC)]
                dve.tensor_tensor(r1[:, :], psY[:, :], xg, ALU.add).then_inc(s("norm_steps"), 1)
                dve.wait_ge(s("norm_steps"), 2 * g + 1)
                for b in range(GB):
                    ins = dve.bn_stats(st1[:, b, :], r1[:, b * E:(b + 1) * E])
                ins.then_inc(s("norm_steps"), 1)
                dve.wait_ge(s("norm_steps"), 2 * g + 2)
                pause(dve)
                for b in range(GB):
                    ins = dve.bn_aggr(mv1[:, b, :], st1[:, b, :])
                ins.then_inc(s("mv1_ready"), 1)
                dve.wait_ge(s("rs1_ready"), g + 1)
                for b in range(GB):
                    dst = X[:, :, :].rearrange("p b e -> p (b e)")[:, bass.ds(g * GC + b * E, E)]
                    ins = dve.tensor_scalar(dst, r1[:, b * E:(b + 1) * E], mv1[:, b, 0:1], rs1[:, b:b + 1], ALU.subtract, ALU.mult)
                ins.then_inc(s("x1_ready"), 1)

            project(0, 0)

            def step(i, last=False):
                attend(2 * i)
                project(2 * i + 1, 1)
                finish(2 * i, 0)
                attend(2 * i + 1)
                if not last:
                    project(2 * i + 2, 0)
                finish(2 * i + 1, 1)

            with dve.Fori(0, NG // 2 - 1) as i:
                step(i)
            step(NG // 2 - 1, last=True)


            psQx, psD, psL1 = banks[1], banks[2], banks[3]
            for r in range(3):
                ins = dve.tensor_copy(wqs[:, :, r, :], cwqT[:, :].rearrange("p (j d) -> p j d", j=NQ))
            ins.then_inc(s("wqs_ready"), 1)
            dve.tensor_scalar(wks[:, :, :], cwkvT[:, 0:DX].unsqueeze(1).to_broadcast([P, P // DX, DX]), SCALE, None, ALU.mult).then_inc(s("wqs_ready"), 1)
            dve.wait_ge(s("pool_setup"), setup_steps["cross"])
            dve.tensor_scalar(baseE[:, :], capE[:, :], float(ROW), None, ALU.mult).then_inc(s("baseE_ready"), 1)
            dve.wait_ge(s("baseE_ready"), 1)

            def normal(i, c):
                b, p, q = 4 * i + c, c % 4, i + c // 4
                dve.wait_ge(s("rs2_ready"), b + 1)
                if not (isinstance(q, int) and q < 1):
                    dve.wait_ge(s(f"x2_saved{p}"), 16 * q)
                    dve.wait_ge(s(f"scattered{p}"), 16 * TOP * q)
                dve.tensor_scalar(xrow[p][:, :, 0:E], r2[p % 2][:, :].unsqueeze(1).to_broadcast([P, TOP, E]), mv2[p % 2][:, 0:1], rs2[p % 2][:, 0:1],
                                  ALU.subtract, ALU.mult).then_inc(s("x2_ready"), 1)
                dve.tensor_copy(xrow[p][:, :, E:RW].bitcast(U32), results[:, bass.ds(b, 1), :].rearrange("p b k -> p k b")).then_inc(s("row_to"), 1)

            def queries(i, c):
                b, p = 4 * i + c, c % 4
                dve.wait_ge(s("qhi_ready"), b + 1)
                dve.memset(qs[p][96:96 + QD, :, :], 0.0)
                lo = qs[p][64:96, :, :].rearrange("p j t -> p (j t)")
                dve.tensor_tensor(lo, psQx[64:96, :], lo, ALU.subtract).then_inc(s("qlo_ready"), 1)

            def maxima(i, c, j):
                b, p = 4 * i + c, c % 4
                dve.wait_ge(s("L1_ps"), NQ * b + j + 1)
                if j == 0:
                    free(dve, "M_ps", b - 1)
                dve.tensor_reduce(mx16[p % 2][:, QD * j:QD * j + QD], psL1[:, 0:QD * C].rearrange("p (h c) -> p h c", c=C), AX.X, ALU.max).then_inc(s("mx_ready"), 1)

            def step(i, c):
                t = 4 * i + c
                if there(i, c):
                    maxima(i, c, 0)
                if there(i, c - 4):
                    normal(i, c - 4)
                if there(i, c):
                    maxima(i, c, 1)
                if there(i, c + 2):
                    queries(i, c + 2)
                if there(i, c):
                    maxima(i, c, 2)
                    maxima(i, c, 3)

                dve.wait_ge(s("bank_ps"), t - FIRST + 1)
                pause(dve)
                select, select_n, select_p = there(i, c + 2), t + 2, (c + 2) % 4
                count, count_n, count_p = there(i, c + 1), t + 1, (c + 1) % 4
                value, value_n, value_p = there(i, c - 2), t - 2, (c - 2) % 4
                tail, tail_n, tail_p = there(i, c - 3), t - 3, (c - 3) % 4
                route, route_n = there(i, c - 4), t - 4
                place, place_n, place_p = there(i, c - 5), t - 5, (c - 5) % 4
                av = psD[:, c_av:c_av + NH * KV].rearrange("p (h j v) -> p h j v", h=QD, v=KV)
                scores = psD[:, c_s:c_s + C]
                if count:
                    free(dve, "bd_ready", count_n - 1)
                    dve.tensor_scalar(src[count_p % 2][96:128, :], psD[96:128, c_n:c_n + C], thr[96:128, 0:1], mult[96:128, 0:1], ALU.is_le, ALU.mult)
                    dve.tensor_scalar(w9[count_p][:, 0:KV], mv9[count_p][:, :], psD[0:C, c_n1:c_n1 + 1], None, ALU.mult).then_inc(s("aux_ready"), 1)
                if select:
                    free(dve, "select_steps", 3 * select_n)
                    pause(dve)
                    dve.max(top8[:, :], scores).then_inc(s("select_steps"), 1)
                if value:
                    free(dve, "at_ready", value_n)
                    dve.reciprocal(rden[:, :].rearrange("p (h j) -> p h j", h=QD), av[:, :, :, DX]).then_inc(s("rden_ready"), 1)
                if route:
                    free(dve, "route_steps", 4 * route_n)
                    dve.tensor_tensor(lgs[:, :], psD[:, c_lg:c_lg + NE], rb[:, :], ALU.add).then_inc(s("lgs_ready"), 1)
                if place:
                    free(dve, "place_steps", 2 * place_n)
                    dve.scalar_tensor_tensor(slot_e[:, :], psD[:, c_rk:c_rk + NE], float(ROW), baseE[:, :], ALU.mult, ALU.add).then_inc(s("slot_e_ready"), 1)
                if select:
                    dve.wait_ge(s("select_steps"), 3 * select_n + 1)
                    pause(dve)
                    dve.max_index(idx8[:, :], top8[:, :], scores).then_inc(s("select_steps"), 1)
                if tail:
                    free(dve, "x2_ready", tail_n - 1)
                    xb = X[:, :, :].rearrange("p b e -> p (b e)")[:, bass.ds(tail_n * E, E)]
                    dve.tensor_tensor(r2[tail_p % 2][:, :], psD[:, c_y2:c_y2 + E], xb, ALU.add).then_inc(s("tail_steps"), 1)
                if value:
                    dve.wait_ge(s("rden_ready"), value_n + 1)
                    free(dve, "aT_ps", value_n - 1)
                    dve.tensor_tensor(at[value_p % 2][:, :].rearrange("p (j h d) -> p h j d", h=QD, d=DX), av[:, :, :, 0:DX],
                                      rden[:, :].rearrange("p (h j) -> p h j", h=QD).unsqueeze(3).to_broadcast([P, QD, NQ, DX]),
                                      ALU.mult).then_inc(s("at_ready"), 1)
                if place:
                    dve.wait_ge(s("before_ready"), place_n + 1)
                    dve.tensor_tensor(before[:, :], before[:, :], chosen[:, :], ALU.add).then_inc(s("before_ready"), 1)
                    dve.wait_ge(s("slot_e_ready"), place_n + 1)
                    dve.tensor_tensor(slotsel[:, :, :], onehots[:, :, :], slot_e[:, :].unsqueeze(1).to_broadcast([P, TOP, NE]), ALU.mult).then_inc(s("place_steps"), 1)
                if select:
                    dve.wait_ge(s("select_steps"), 3 * select_n + 2)
                    dve.tensor_copy(idxf[:, :], idx8[:, 0:1]).then_inc(s("select_steps"), 1)
                if tail:
                    dve.wait_ge(s("tail_steps"), 2 * tail_n + 1)
                    dve.bn_stats(st2[:, :], r2[tail_p % 2][:, :]).then_inc(s("tail_steps"), 1)
                if route:
                    dve.wait_ge(s("lgs_ready"), route_n + 1)
                    pause(dve)
                    dve.max(rtop[:, :], lgs[:, :]).then_inc(s("route_steps"), 1)
                if place:
                    dve.wait_ge(s("place_steps"), 2 * place_n + 1)
                    dve.tensor_reduce(slotf[:, :], slotsel[:, :, :], AX.X, ALU.add).then_inc(s("place_steps"), 1)
                if select:
                    dve.wait_ge(s("select_steps"), 3 * select_n + 3)
                    dve.tensor_scalar(onehot[select_p % 2][:, :], iotaC[:, :], idxf[:, 0:1], None, ALU.is_equal).then_inc(s("onehot_ready"), 1)
                if tail:
                    dve.wait_ge(s("tail_steps"), 2 * tail_n + 2)
                    pause(dve)
                    dve.bn_aggr(mv2[tail_p % 2][:, :], st2[:, :]).then_inc(s("mv2_ready"), 1)
                if route:
                    dve.wait_ge(s("route_steps"), 4 * route_n + 1)
                    pause(dve)
                    dve.max_index(ridx[:, :], rtop[:, :], lgs[:, :]).then_inc(s("route_steps"), 1)
                    dve.tensor_copy(topl[:, bass.ds(route_n, 1), :], rtop[:, 0:TOP].unsqueeze(1)).then_inc(s("top_saved"), 1)
                if place:
                    dve.wait_ge(s("place_steps"), 2 * place_n + 2)
                    dve.wait_ge(s("row_to"), place_n + 1)
                    dve.tensor_copy(slots[place_p][:, :], slotf[:, :]).then_inc(s("slots_ready"), 1)
                if route:
                    dve.wait_ge(s("route_steps"), 4 * route_n + 2)
                    dve.tensor_copy(topi[:, :], ridx[:, 0:TOP]).then_inc(s("route_steps"), 1)
                    dve.wait_ge(s("route_steps"), 4 * route_n + 3)
                    dve.tensor_tensor(onehots[:, :, :], iotaE[:, :].unsqueeze(1).to_broadcast([P, TOP, NE]), topi[:, :].unsqueeze(2).to_broadcast([P, TOP, NE]),
                                      ALU.is_equal).then_inc(s("route_steps"), 1)
                    dve.wait_ge(s("route_steps"), 4 * route_n + 4)
                    with nc.allow_low_precision(reason="a sum of one at most"):
                        dve.tensor_reduce(chosen[:, :], onehots[:, :, :].rearrange("p k e -> p e k"), AX.X, ALU.add).then_inc(s("chosen_ready"), 1)

            steps(dve, step)

            psC = banks[0]
            chain = 0

            def then(ins):
                nonlocal chain
                chain += 1
                ins.then_inc(s("table_steps"), 1)
                dve.wait_ge(s("table_steps"), chain)

            dve.wait_ge(s("count_ps"), 1)
            then(dve.tensor_copy(count[:, :], psC[0:1, 0:NE]))
            then(dve.tensor_tensor(over[:, :, :], count[:, :].unsqueeze(2).to_broadcast([1, NE, JT]), steps128[:, :].unsqueeze(1).to_broadcast([1, NE, JT]), ALU.is_gt))
            then(dve.tensor_reduce(ntile[:, :], over[:, :, :], AX.X, ALU.add))
            then(dve.tensor_tensor_scan(last_tile[:, :], ones_e[:, :], ntile[:, :], 0.0, ALU.mult, ALU.add))
            then(dve.tensor_tensor(padf[:, :], count[:, :], capE[0:1, :], ALU.add))
            then(dve.tensor_copy(pad_at[:, :], padf[:, :]))
            then(dve.tensor_tensor(past[:, :, :], tile_no[:, :].unsqueeze(2).to_broadcast([1, NL_, NE]), last_tile[:, :].unsqueeze(1).to_broadcast([1, NL_, NE]), ALU.is_ge))
            then(dve.tensor_reduce(expert[:, :], past[:, :, :], AX.X, ALU.add))
            then(dve.tensor_tensor(past[:, :, :], past[:, :, :], ntile[:, :].unsqueeze(1).to_broadcast([1, NL_, NE]), ALU.mult))
            then(dve.tensor_reduce(done_t[:, :], past[:, :, :], AX.X, ALU.add))
            then(dve.tensor_tensor(rowf[:, :], tile_no[:, :], done_t[:, :], ALU.subtract))
            then(dve.tensor_scalar(rowf[:, :], rowf[:, :], float(P), None, ALU.mult))
            then(dve.tensor_scalar(colf[:, :], expert[:, :], float(CAP), None, ALU.mult))
            then(dve.tensor_tensor(rowf[:, :], rowf[:, :], colf[:, :], ALU.add))
            then(dve.tensor_scalar(tile_row[:, :], rowf[:, :], float(LAST), None, ALU.min))
            then(dve.tensor_scalar(tile_col[:, :], expert[:, :], float(NE - 1), float(WROW), ALU.min, ALU.mult))
            dve.sem_inc(s("tables"), 1)
            dve.wait_ge(s("top_saved"), B)
            dve.tensor_tensor(gates[:, :, :], topl[:, :, :], topl[:, :, 0:1].to_broadcast([P, B, TOP]), ALU.subtract).then_inc(s("gates0"), 1)
            dve.wait_ge(s("gates1"), 1)
            then(dve.tensor_reduce(gsum[:, :], gates[:, :, :], AX.X, ALU.add))
            then(dve.reciprocal(grec[:, :], gsum[:, :]))
            then(dve.tensor_tensor(gates[:, :, :], gates[:, :, :], grec[:, :].unsqueeze(2).to_broadcast([P, B, TOP]), ALU.mult))

            psY3 = banks[5:8]
            wrow = wall[:, :, :].rearrange("p e w -> p (e w)")
            dve.wait_ge(s("wall_in"), 16 * (NI + 3))
            dve.sem_inc(s("y_ready"), 3)

            def expert_weights(i, p, col):
                dve.tensor_copy(wcur[p % QUAD][:, :], wrow[:, bass.ds(dve.snap(col, min_val=0, max_val=(NE - 1) * WROW), WROW)]).then_inc(s("w_ready"), 1)

            def results_out(i, written, p):
                dve.wait_ge(s("result_ps"), i + 1)
                if written is not None:
                    dve.wait_ge(s(f"y_out{p}"), written)
                dve.wait_ge(s("w_ready"), i + 1)
                dve.tensor_tensor(yout[p][:, :], psY3[p % 3][:, 0:E], wcur[p % QUAD][:, 2 * I + NI:WROW], ALU.add).then_inc(s("y_ready"), 1)

            with ExitStack() as regs:
                col = [regs.enter_context(dve.register(f"col{j}")) for j in range(QUAD)]
                dve.reg_load(col, tile_col[0:1, 0:QUAD])
                for d in range(QUAD):
                    expert_weights(d, d, col[d])

                def tiles(i, written):
                    for d in range(UNROLL):
                        if d % QUAD == 0:
                            dve.reg_load(col, tile_col[0:1, bass.ds(UNROLL * i + d + QUAD, QUAD)])
                        results_out(UNROLL * i + d, written, d)
                        dve.wait_ge(s("y_ready"), UNROLL * i + d + 1 + 3)
                        expert_weights(UNROLL * i + d + QUAD, d, col[d % QUAD])

                tiles(0, None)
                with dve.Fori(1, NT // UNROLL) as i:
                    tiles(i, 16 * i)

            for p in range(4):
                dve.wait_ge(s(f"x2_saved{p}"), 16 * (B // 4))
            Xf = X[:, :, :].rearrange("p b e -> p (b e)")
            gf = gates[:, :, :].rearrange("p b k -> p (b k)")

            def gather(b, d, loaded):
                dve.wait_ge(s(f"y_in{d % 4}"), loaded)
                r = r3[d % 2]
                if not (isinstance(b, int) and b < 2):
                    dve.wait_ge(s("x3_ready"), b - 1)
                for j in range(TOP):
                    if j:
                        dve.wait_ge(s("r3_steps"), TOP * b + j)
                    prev = r[:, :] if j else Xf[:, bass.ds(b * E, E)]
                    dve.scalar_tensor_tensor(r[:, :], yin[d % 4][:, j, :], gf[:, bass.ds(b * TOP + j, 1)], prev, ALU.mult, ALU.add).then_inc(s("r3_steps"), 1)
                dve.wait_ge(s("r3_steps"), TOP * b + TOP)
                dve.sem_inc(s("r3_ready"), 1)
                dve.bn_stats(st3[d % 2][:, :], r[:, :]).then_inc(s("st3_ready"), 1)

            def stats(b, d):
                dve.wait_ge(s("st3_ready"), b + 1)
                pause(dve)
                dve.bn_aggr(mv3[d % 2][:, :], st3[d % 2][:, :]).then_inc(s("mv3_ready"), 1)

            def norm(b, d, stored):
                dve.wait_ge(s("rs3_ready"), b + 1)
                if stored is not None:
                    dve.wait_ge(s(f"out{d % 2}"), stored)
                dve.tensor_scalar(o3[d % 2][:, :], r3[d % 2][:, :], mv3[d % 2][:, 0:1], rs3[d % 2][:, 0:1], ALU.subtract, ALU.mult).then_inc(s("x3_ready"), 1)

            gather(0, 0, 16)
            stats(0, 0)
            for b in (1, 2):
                gather(b, b, 16)
                stats(b, b)
                norm(b - 1, b - 1, None)
            with dve.Fori(0, B // 4 - 1) as i:
                for d in range(4):
                    gather(4 * i + 3 + d, 3 + d, 16 * (i + (3 + d) // 4) + 16)
                    stats(4 * i + 3 + d, 3 + d)
                    norm(4 * i + 2 + d, 2 + d, 16 * (2 * i + (2 + d) // 2))
            gather(B - 1, 3, 16 * (B // 4))
            stats(B - 1, 1)
            norm(B - 2, 0, 16 * (B // 2 - 1))
            norm(B - 1, 1, 16 * (B // 2 - 1))


def layout(I):
    f = lambda a: np.ascontiguousarray(a)
    x = np.asarray(I["x"])
    B, T, E = x.shape
    return {
        "x": f(x.transpose(1, 0, 2)),
        "xT": f(x.reshape(B * T, E).T),
        "wk": f(I["L0_attn_Wk"]), "wq": f(I["L0_attn_Wq"]), "wv": f(I["L0_attn_Wv"]), "wo": f(I["L0_attn_Wo"]),
        "g1": f(I["L0_attn_G1"]), "g2": f(I["L0_attn_G2"]),
        "ctxT": f(np.asarray(I["ctx_1024"]).transpose(0, 2, 1)),
        "cwq": f(I["L0_xattn_Wq"]), "cwqT": f(np.asarray(I["L0_xattn_Wq"]).T), "cwkvT": f(np.asarray(I["L0_xattn_Wkv"]).T), "cwcT": f(np.asarray(I["L0_xattn_Wc"]).T),
        "rw": f(I["L0_ffn_router_w"]), "rb": f(np.broadcast_to(np.asarray(I["L0_ffn_router_b"]), (T, I["L0_ffn_router_b"].shape[0]))),
        "w1": f(I["L0_ffn_w1"]), "w2": f(I["L0_ffn_w2"]), 
        "b1T": f(np.asarray(I["L0_ffn_b1"]).reshape(I["L0_ffn_b1"].shape[0], -1, E).transpose(2, 0, 1)),
        "b2rep": f(np.broadcast_to(np.asarray(I["L0_ffn_b2"]), (E, *I["L0_ffn_b2"].shape))),
        "delta": f(I["L0_attn_delta"]).reshape(E, 1), "norm_w": f(I["L0_attn_norm_w"]).reshape(E, 1),
    }


def kernel(**inputs):
    laid = layout(inputs)
    B, T, E = np.asarray(inputs["x"]).shape
    nc = _bacc.Bacc("TRN2", target_bir_lowering=False, num_devices=1)
    A = {name: nc.dram_tensor(name + "_dram", a.shape, _mybir.dt.from_np(a.dtype), kind="ExternalInput").ap() for name, a in laid.items()}
    out = nc.dram_tensor("out_dram", (T, B, E), _mybir.dt.float32, kind="ExternalOutput").ap()
    build(nc, A, out)
    nc.compile()
    r = _run(nc, [{name + "_dram": a for name, a in laid.items()}], core_ids=[0])
    return np.ascontiguousarray(np.asarray(r.results[0]["out_dram"]).transpose(1, 0, 2))
```

```python
from contextlib import ExitStack

import concourse.bacc as _bacc
import concourse.mybir as _mybir
import numpy as np
from concourse.bass_utils import run_bass_kernel_spmd as _run


def build(nc, A, out):
    import concourse.bass as bass
    from concourse import mybir

    ALU = mybir.AluOpType
    ACT = mybir.ActivationFunctionType
    AX = mybir.AxisListType
    F32 = mybir.dt.float32
    U32 = mybir.dt.uint32
    F16 = mybir.dt.float16

    P = 128
    E = 128
    B = A["x"].shape[1]
    T = 128
    GB = 4
    GC = GB * T
    NG = B // GB
    H = 2
    DH = E // H
    HALVES = [64, 32, 16, 8]
    NL = len(HALVES)
    LEAF = 8
    FLOOR = 20.0
    EPS = 1e-5

    with ExitStack() as ctx:
        def sb(name, shape, dt=F32):
            return ctx.enter_context(nc.sbuf_tensor(name, shape, dt))

        def sem(name):
            return ctx.enter_context(nc.semaphore(name))

        banks = [ctx.enter_context(nc.psum_tensor(f"bank{i}", [P, 512], F32)) for i in range(8)]

        X = sb("X", [P, B, E])
        wk, wq, wv, wo = (sb(n, [P, E]) for n in ("wk", "wq", "wv", "wo"))
        g1 = sb("g1", [P, DH])
        g2 = sb("g2", [DH, E])
        delta = sb("delta", [P, 1])
        norm_w = sb("norm_w", [P, 1])
        won = sb("won", [P, E])
        ident = sb("ident", [P, P])
        restart = sb("restart", [P, GC])
        lmask = [sb(f"lmask{h}", [P, 64]) for h in HALVES]
        leafmask = sb("leafmask", [P, P])

        C = A["ctxT"].shape[2]
        NH = 16
        DX = E // NH
        QD = 4
        NQ = NH // QD
        KV = DX + 1
        cwq = sb("cwq", [P, E])
        cwqT = sb("cwqT", [P, E])
        cwkvT = sb("cwkvT", [P, 2 * DX])
        cwcT = sb("cwcT", [P, E])
        wqs = sb("wqs", [P, NQ, 3, QD * DX])
        wks = sb("wks", [P, P // DX, DX])
        ident16, ones16 = sb("ident16", [P, P], F16), sb("ones16", [P, P], F16)
        iotaC = sb("iotaC", [P, C])
        thr, mult = sb("thr", [P, 1]), sb("mult", [P, 1])
        bmask = sb("bmask", [P, QD], F16)
        x1s = [sb(f"x1s{p}", [P, E]) for p in range(4)]
        ctxs = [sb(f"ctxs{p}", [P, C]) for p in range(4)]
        FW = E + 2 * C
        Fs = [sb(f"Fs{p}", [P, FW]) for p in range(4)]
        mv9 = [sb(f"mv9{p}", [C, KV]) for p in range(4)]
        qs = [sb(f"qs{p}", [P, NQ, T], F16) for p in range(4)]
        top8 = sb("top8", [P, 8])
        idx8 = sb("idx8", [P, 8], U32)
        idxf = sb("idxf", [P, 1])
        onehot = [sb(f"onehot{p}", [P, C], F16) for p in range(2)]
        src = [sb(f"src{p}", [P, C], F16) for p in range(2)]
        bd = [sb(f"bd{p}", [P, QD, C], F16) for p in range(4)]
        w9 = [sb(f"w9{p}", [C, 32]) for p in range(4)]
        picks = sb("picks", [P, NQ, KV])
        outT = sb("outT", [P, QD * T])
        mx16 = [sb(f"mx16{p}", [P, NH], F16) for p in range(2)]
        Ex = [sb(f"Ex{p}", [C, NQ, QD * T]) for p in range(2)]
        rden = sb("rden", [P, NH])
        at = [sb(f"at{p}", [P, E]) for p in range(2)]
        aT = sb("aT", [P, E])
        r2 = [sb(f"r2{p}", [P, E]) for p in range(2)]
        st2 = sb("st2", [P, 6])
        mv2 = [sb(f"mv2{p}", [P, 2]) for p in range(2)]
        ln2 = sb("ln2", [P, 1])
        rs2 = [sb(f"rs2{p}", [P, 1]) for p in range(2)]
        c_av, c_y2, c_s, c_n, c_n1, c_lg, c_rk = 0, 144, 272, 352, 430, 432, 448

        NE = A["rw"].shape[1]
        TOP = 4
        I = A["w1"].shape[2]
        NI = I // P
        N_TOK = B * T
        CAP = N_TOK + P
        LAST = NE * CAP
        NT = N_TOK * TOP // P + NE
        UNROLL = 12
        FIRST_TILES = 2 * UNROLL
        PAD_STEPS = 6
        QUAD = 4
        LEAD_T, LEAD_H = 3, 2
        NL_ = NT + UNROLL
        ROW = 192
        RW = E + 1
        NOWHERE = 1 << 20
        WROW = I + NI * E + NI + E
        xs = nc.dram_tensor("xs", [LAST + P, ROW], F32).ap()
        ys = nc.dram_tensor("ys", [N_TOK * TOP, E], F32).ap()
        rw = sb("rw", [P, NE])
        rb = sb("rb", [P, NE])
        xrow = [sb(f"xrow{p}", [P, TOP, E + 4]) for p in range(4)]
        x2Tb = sb("x2Tb", [P, T])
        lgs = sb("lgs", [P, NE])
        rtop = sb("rtop", [P, 8])
        ridx = sb("ridx", [P, 8], U32)
        topi = sb("topi", [P, TOP])
        onehots = sb("onehots", [P, TOP, NE])
        slotsel = sb("slotsel", [P, TOP, NE])
        chosen = sb("chosen", [P, NE], F16)
        before = sb("before", [P, NE], F16)
        slot_e = sb("slot_e", [P, NE])
        slotf = sb("slotf", [P, TOP])
        slots = [sb(f"slots{p}", [P, TOP], U32) for p in range(4)]
        results = sb("results", [P, B, TOP], U32)
        topl, gates = (sb(n, [P, B, TOP]) for n in ("topl", "gates"))
        gsum, grec = sb("gsum", [P, B]), sb("grec", [P, B])
        iotaE, baseE = sb("iotaE", [P, NE]), sb("baseE", [P, NE])
        upper16 = sb("upper16", [P, P], F16)
        pad = sb("pad", [P, RW])
        JT = N_TOK // P + 1
        steps128 = sb("steps128", [1, JT])
        tile_no = sb("tile_no", [1, NL_])
        ones_e, capE = sb("ones_e", [1, NE]), sb("capE", [P, NE])
        first_part = ExitStack()

        def passing(name, shape, dt=F32):
            return first_part.enter_context(nc.sbuf_tensor(name, shape, dt))

        xTg = [passing(f"xTg{p}", [P, GC]) for p in range(2)]
        uS, soft, kk, k, qc, sq_, q, N, gc, sg_ = (passing(n, [P, GC]) for n in ("uS", "soft", "kk", "k", "qc", "sigq", "q", "N", "gc", "lgate"))
        gate = [passing(f"gate{p}", [P, GC]) for p in range(2)]
        v = [passing(f"v{p}", [P, GC]) for p in range(2)]
        zT = passing("zT", [DH, GC])
        dec = [passing(f"dec{l}", [P, GC]) for l in range(NL + 1)]
        decK = passing("decK", [P, GC])
        Lk = [passing(f"Lk{l}", [P, GC]) for l in range(NL + 1)]
        Rq = [passing(f"Rq{l}", [P, GB, H, T // 2]) for l in range(NL)]
        Rleaf = passing("Rleaf", [P, GB, H, T])
        AT = passing("AT", [P, GB, H, T])
        og, osq, on, oT, r1 = (passing(n, [P, GC]) for n in ("og", "osq", "on", "oT", "r1"))
        ss, lss, rss = (passing(n, [P, GB * H]) for n in ("ss", "lss", "rss"))
        st1 = passing("st1", [P, GB, 6])
        mv1 = passing("mv1", [P, GB, 2])
        ln1, rs1, nm1 = (passing(n, [P, GB]) for n in ("ln1", "rs1", "nm1"))
        first_part.close()

        count = sb("count", [1, NE])
        over = sb("over", [1, NE, JT])
        ntile, last_tile = sb("ntile", [1, NE]), sb("last_tile", [1, NE])
        padf, pad_at = sb("padf", [1, NE]), sb("pad_at", [1, NE], U32)
        past = sb("past", [1, NL_, NE])
        expert, done_t, rowf, colf = (sb(n, [1, NL_]) for n in ("expert", "done_t", "rowf", "colf"))
        tile_row, tile_col = sb("tile_row", [1, NL_], U32), sb("tile_col", [1, NL_], U32)
        wall = sb("wall", [P, NE, WROW])
        wcur = [sb(f"wcur{p}", [P, WROW]) for p in range(QUAD)]
        xin = [sb(f"xin{p}", [P, RW]) for p in range(UNROLL)]
        xinT = [sb(f"xinT{p}", [P, P]) for p in range(4)]
        hid = [sb(f"hid{p}", [P, NI, P]) for p in range(3)]
        yout = [sb(f"yout{p}", [P, E]) for p in range(UNROLL)]
        FB = 2
        NF = B // FB
        yin = [sb(f"yin{p}", [P, FB, TOP * E]) for p in range(4)]
        r3 = [sb(f"r3{p}", [P, FB, E]) for p in range(2)]
        o3 = [sb(f"o3{p}", [P, FB, E]) for p in range(2)]
        st3 = [sb(f"st3{p}", [P, FB, 6]) for p in range(2)]
        mv3 = [sb(f"mv3{p}", [P, FB, 2]) for p in range(2)]
        ln3 = sb("ln3", [P, FB])
        rs3 = [sb(f"rs3{p}", [P, FB]) for p in range(2)]

        S = {}

        def s(name):
            if name not in S:
                S[name] = sem(name)
            return S[name]

        def pause(eng):
            eng.sem_inc(s("waits_over"), 1)

        block = ctx.enter_context(nc.Block())

        weights_dma = ["wk", "wq", "wv", "wo", "g1", "g2", "delta", "norm_w", "cwq", "cwqT", "cwkvT", "cwcT", "rw", "rb"]
        WN = 16 * len(weights_dma)
        MASKED = -30000.0
        SCALE = float(1.0 / np.sqrt(np.float32(DX)))

        FIRST, FULL, REST = -3, 9, B - 3

        def steps(eng, step):
            for c in range(FIRST, FULL):
                step(0, c)
            with eng.Fori(0, (REST - FULL) // 4) as i:
                for d in range(4):
                    step(i, FULL + d)
            for c in range(REST, B + 5):
                step(0, c)

        def there(i, c):
            return not isinstance(i, int) or 0 <= c < B

        def free(eng, name, n):
            if not (isinstance(n, int) and n < 1):
                eng.wait_ge(s(name), n)

        setup_steps = {}

        def pad_rows(eng, half):
            with ExitStack() as regs:
                at = [regs.enter_context(eng.register(f"pad_at{half}_{j}")) for j in range(4)]
                for e in range(half * NE // 2, (half + 1) * NE // 2):
                    if e % 4 == 0:
                        eng.reg_load(at, pad_at[0:1, e:e + 4])
                    eng.dma_start(xs[bass.ds(eng.snap(at[e % 4], min_val=0, max_val=LAST - P), P), 0:RW], pad[:, :]).then_inc(s(f"pads{half}"), 16)

        def groups(eng, step):
            step(0, 0, 0, finish=False)
            with eng.Fori(0, NG // 2 - 1) as i:
                for d in range(2):
                    step(2 * i + 1 + d, 1 - d, i + d)
            step(NG - 1, 1, NG // 2 - 1, project=False)
            step(NG, 0, NG // 2, attend=False, project=False)

        @block.sync
        def _(sp):
            sp.dma_start(xTg[0][:, :], A["xT"][:, 0:GC]).then_inc(s("xT_in0"), 16)
            for name, t in zip(weights_dma, (wk, wq, wv, wo, g1, g2, delta, norm_w, cwq, cwqT, cwkvT, cwcT, rw, rb)):
                sp.dma_start(t[:, :], A[name]).then_inc(s("weights_in"), 16)
            sp.dma_start(xTg[1][:, :], A["xT"][:, GC:2 * GC]).then_inc(s("xT_in1"), 16)
            sp.dma_start(X[:, :, :], A["x"]).then_inc(s("x_in"), 16)
            with sp.Fori(0, NG // 2 - 1) as i:
                for p in range(2):
                    g = 2 * i + p
                    sp.wait_ge(s("v_ps"), g + 1)
                    sp.dma_start(xTg[p][:, :], A["xT"][:, bass.ds((g + 2) * GC, GC)]).then_inc(s(f"xT_in{p}"), 16)

            def fetch(b, p):
                sp.dma_start(x1s[p][:, :], X[:, :, :].rearrange("p b e -> p (b e)")[:, bass.ds(b * E, E)]).then_inc(s(f"cross_in{p}"), 16)
                sp.dma_start(ctxs[p][:, :], A["ctxT"].rearrange("b p c -> p b c")[:, bass.ds(b, 1), :]).then_inc(s(f"cross_in{p}"), 16)

            def refetch(b, p):
                sp.wait_ge(s("F_ps"), b + 1)
                pause(sp)
                fetch(b + 4, p)

            def save(b, p):
                sp.wait_ge(s("x2_ready"), b + 1)
                pause(sp)
                sp.dma_start(X[:, :, :].rearrange("p b e -> p (b e)")[:, bass.ds(b * E, E)], xrow[p][:, 0, 0:E]).then_inc(s(f"x2_saved{p}"), 16)

            sp.wait_ge(s("x1_ready"), 1)
            for b in range(GB):
                fetch(b, b)
            sp.wait_ge(s("x1_ready"), NG)
            sp.dma_start(wall[:, :, 0:I], A["w1"].rearrange("e p i -> p e i")).then_inc(s("wall_in"), 16)
            for c in range(NI):
                sp.dma_start(wall[:, :, I + c * E:I + (c + 1) * E], A["w2"].rearrange("e (c p) d -> c p e d", p=P)[c]).then_inc(s("wall_in"), 16)
            sp.dma_start(wall[:, :, 2 * I:2 * I + NI], A["b1T"]).then_inc(s("wall_in"), 16)
            sp.dma_start(wall[:, :, 2 * I + NI:WROW], A["b2rep"]).then_inc(s("wall_in"), 16)
            for b in range(8):
                refetch(b, b % 4)
            with sp.Fori(0, B // 4 - 3) as i:
                for p in range(4):
                    refetch(4 * i + 8 + p, p)
                    save(4 * i + p, p)
            for b in range(B - 12, B):
                save(b, b % 4)
            sp.wait_ge(s("table_steps"), PAD_STEPS)
            pad_rows(sp, 0)
            sp.dma_start(xs[LAST:LAST + P, 0:RW], pad[:, :]).then_inc(s("pads0"), 16)
            sp.wait_ge(s("pads0"), 16 * (NE // 2 + 1))
            sp.wait_ge(s("pads1"), 16 * (NE // 2))
            for p in range(4):
                sp.wait_ge(s(f"scattered{p}"), 16 * TOP * (B // 4))
            sp.wait_ge(s("tables"), 1)
            with ExitStack() as regs:
                row = [regs.enter_context(sp.register(f"row{j}")) for j in range(QUAD)]

                def load(i, written):
                    for p in range(UNROLL):
                        if p % QUAD == 0:
                            sp.reg_load(row, tile_row[0:1, bass.ds(i + p, QUAD)])
                        if written is not None:
                            sp.wait_ge(s(f"y_out{p}"), written)
                            pause(sp)
                        sp.dma_start(xin[p][:, :], xs[bass.ds(sp.snap(row[p % QUAD], min_val=0, max_val=LAST), P), 0:RW]).then_inc(s(f"x_row_in{p}"), 16)

                load(0, None)
                with sp.Fori(0, NT // UNROLL) as i:
                    load(i * UNROLL + UNROLL, 16 * i + 16)
            for p in range(UNROLL):
                sp.wait_ge(s(f"y_out{p}"), 16 * (NT // UNROLL))
            y4 = ys.rearrange("(b p k) e -> p b (k e)", p=P, k=TOP)

            def load_y(f, p):
                if not (isinstance(f, int) and f < 4):
                    sp.wait_ge(s("r3_ready"), f - 3)
                    pause(sp)
                sp.dma_start(yin[p][:, :, :], y4[:, bass.ds(FB * f, FB), :]).then_inc(s(f"y_in{p}"), 16)

            def store(f, p):
                sp.wait_ge(s("x3_ready"), FB * f + FB)
                pause(sp)
                sp.dma_start(out[:, bass.ds(FB * f, FB), :], o3[p][:, :, :]).then_inc(s(f"out{p}"), 16)

            for f in range(4):
                load_y(f, f)
            with sp.Fori(0, NF // 4 - 1) as i:
                for p in range(4):
                    load_y(4 * i + 4 + p, p)
                    store(4 * i + p, p % 2)
            for f in range(NF - 4, NF):
                store(f, f % 2)
            for p in range(2):
                sp.wait_ge(s(f"out{p}"), 16 * (NF // 2))

        @block.gpsimd
        def _(pool):
            n = 0

            def done(ins):
                nonlocal n
                n += 1
                ins.then_inc(s("pool_setup"), 1)
                pool.wait_ge(s("pool_setup"), n)

            def keep(v, pattern, base, channel, fill=0.0, op=ALU.is_ge):
                done(pool.affine_select(out=v, in_=v, compare_op=op, fill=fill, base=base, pattern=pattern, channel_multiplier=channel))

            done(pool.memset(ident[:, :], 0.0))
            keep(ident[:, :], [[-1, P]], 0, 1, fill=1.0, op=ALU.not_equal)
            for m, h in zip(lmask, HALVES):
                v3 = m[:, :].rearrange("p (b r) -> p b r", r=h)
                nb = 64 // h
                done(pool.memset(m[:, :], 1.0))
                keep(v3, [[-2 * h, nb], [0, h]], 0, 1)
                keep(v3, [[2 * h, nb], [0, h]], h - 1, -1)
            v3 = leafmask[:, :].rearrange("p (b r) -> p b r", r=LEAF)
            nb = T // LEAF
            done(pool.memset(leafmask[:, :], 1.0))
            keep(v3, [[-LEAF, nb], [0, LEAF]], 0, 1)
            keep(v3, [[LEAF, nb], [1, LEAF]], 0, -1)
            setup_steps["masks"] = n

            def key_logs(g):
                pool.wait_ge(s("soft_ready"), g + 1)
                if not (isinstance(g, int) and g == 0):
                    pool.wait_ge(s("k_ready"), g)
                pool.tensor_tensor(kk[:, :], uS[:, :], soft[:, :], ALU.add).then_inc(s("kk_ready"), 1)

            def leaf_decay(g):
                pool.wait_ge(s("scan_steps"), 2 * g + 1)
                n3 = N[:, :].rearrange("p (b r) -> p b r", r=LEAF)
                mid = n3[:, :, LEAF // 2 - 1:LEAF // 2].to_broadcast([P, GC // LEAF, LEAF])
                pool.tensor_tensor(dec[NL][:, :].rearrange("p (b r) -> p b r", r=LEAF), n3, mid, ALU.subtract).then_inc(s("kk_ready"), 1)

            key_logs(0)
            leaf_decay(0)

            done(pool.memset(ones16[:, :], 1.0))
            done(pool.memset(ident16[:, :], 0.0))
            keep(ident16[:, :], [[-1, P]], 0, 1, fill=1.0, op=ALU.not_equal)
            done(pool.memset(thr[:, :], 0.5))
            done(pool.memset(thr[96:96 + QD, :], 1e9))
            done(pool.memset(mult[:, :], MASKED / (P - 96 - QD)))
            done(pool.memset(mult[96:96 + QD, :], -1.0))
            done(pool.memset(bmask[:, :], 1.0))
            keep(bmask[96:96 + QD, :], [[-1, QD]], 0, 1, op=ALU.is_equal)
            for blk in range(3):
                rows = bmask[32 * blk:32 * blk + 32, :]
                keep(rows, [[-DX, QD]], 0, 1)
                keep(rows, [[DX, QD]], DX - 1, -1)
            done(pool.iota(iotaC[:, :], pattern=[[1, C]], base=0, channel_multiplier=0, allow_small_or_imprecise_dtypes=True))
            done(pool.memset(upper16[:, :], 1.0))
            keep(upper16[:, :], [[1, P]], -1, -1)
            done(pool.iota(results[:, :, :], pattern=[[P * TOP, B], [1, TOP]], base=0, channel_multiplier=TOP))
            done(pool.iota(capE[:, :], pattern=[[CAP, NE]], base=0, channel_multiplier=0, allow_small_or_imprecise_dtypes=True))
            done(pool.iota(steps128[:, :], pattern=[[P, JT]], base=0, channel_multiplier=0, allow_small_or_imprecise_dtypes=True))
            done(pool.iota(tile_no[:, :], pattern=[[1, NL_]], base=0, channel_multiplier=0, allow_small_or_imprecise_dtypes=True))
            done(pool.memset(ones_e[:, :], 1.0))
            done(pool.memset(pad[:, 0:E], 0.0))
            done(pool.iota(pad[:, E:RW].bitcast(U32), pattern=[[1, 1]], base=NOWHERE, channel_multiplier=0))
            done(pool.iota(iotaE[:, :], pattern=[[1, NE]], base=0, channel_multiplier=0, allow_small_or_imprecise_dtypes=True))
            for p in range(4):
                done(pool.memset(qs[p][96:128, :, :], 1.0))
                done(pool.memset(mv9[p][:, DX:KV], 1.0))
                done(pool.memset(w9[p][:, :], 0.0))
            done(pool.memset(picks[:, :, :], 0.0))
            keep(picks[:, :, :], [[-32, NQ], [-1, KV]], 0, 1, fill=1.0, op=ALU.not_equal)
            setup_steps["cross"] = n

            with pool.Fori(1, NG) as g:
                key_logs(g)
                leaf_decay(g)

            words = xs.rearrange("n w -> (n w)").unsqueeze(1)

            def key_halves(i, c):
                b, p = 4 * i + c, c % 4
                mk = Fs[p][:, E + C:E + 2 * C]
                pool.wait_ge(s("F_ready"), b + 1)
                free(pool, "bd_ready", b - 1)
                pause(pool)
                pool.tensor_copy(src[p % 2][0:96, :], mk[0:96, :]).then_inc(s("src_steps"), 1)
                pool.wait_ge(s("src_steps"), 2 * b + 1)
                pool.tensor_tensor(src[p % 2][0:32, :], mk[0:32, :], src[p % 2][0:32, :], ALU.subtract).then_inc(s("src_steps"), 1)

            def keys(i, c):
                b, p = 4 * i + c, c % 4
                pool.wait_ge(s("src_steps"), 2 * b + 2)
                pool.wait_ge(s("aux_ready"), b + 1)
                free(pool, "L2_ps", NQ * (b - 3))
                pool.tensor_tensor(bd[p][:, :, :], src[p % 2][:, :].unsqueeze(1).to_broadcast([P, QD, C]),
                                   bmask[:, :].unsqueeze(2).to_broadcast([P, QD, C]), ALU.mult).then_inc(s("bd_ready"), 1)

            def scatter(i, c):
                b, p = 4 * i + c, c % 4
                pool.wait_ge(s("slots_ready"), b + 1)
                pause(pool)
                for r in range(TOP):
                    pool.indirect_dma_start(words, bass.IndirectOffsetOnAxis(ap=slots[p][:, r:r + 1], axis=0),
                                            xrow[p][:, r, 0:RW], None).then_inc(s(f"scattered{p}"), 16)

            def step(i, c):
                if there(i, c + 1):
                    keys(i, c + 1)
                if there(i, c + 2):
                    key_halves(i, c + 2)
                if there(i, c - 6):
                    scatter(i, c - 6)

            steps(pool, step)
            scatter(0, B - 1)

            with pool.Fori(0, NT // UNROLL) as i:
                for p in range(UNROLL):
                    pool.wait_ge(s("y_ready"), UNROLL * i + p + 1 + 3)
                    pause(pool)
                    pool.indirect_dma_start(ys, bass.IndirectOffsetOnAxis(ap=xin[p][:, :].bitcast(U32)[:, E:RW], axis=0), yout[p][:, :], None,
                                            bounds_check=N_TOK * TOP - 1, oob_is_err=False).then_inc(s(f"y_out{p}"), 16)

        @block.tensor
        def _(pe):
            psU, psQ, psV, psG = banks[0], banks[1], banks[2], banks[3]
            psZ = banks[3]
            psA = banks[4:6]
            psO, psT, psY = banks[6], banks[7], banks[7]

            def project_in(g, p, n16, first=False):
                pe.wait_ge(s(f"xT_in{p}"), n16)
                if not first:
                    pe.wait_ge(s("u_ready"), g)
                pe.matmul(psU[:, :], wk[:, :], xTg[p][:, :], start=True, stop=True).then_inc(s("u_ps"), 1)
                if not first:
                    pe.wait_ge(s("qc_ready"), g)
                pe.matmul(psQ[:, :], wq[:, :], xTg[p][:, :], start=True, stop=True).then_inc(s("q_ps"), 1)
                if not first:
                    pe.wait_ge(s("gc_ready"), g)
                pe.matmul(psZ[0:DH, :], g1[:, :], xTg[p][:, :], start=True, stop=True).then_inc(s("z_ps"), 1)
                if not first:
                    pe.wait_ge(s("v_ready"), g)
                for b in range(GB):
                    mm = pe.matmul(psV[:, b * E:(b + 1) * E], xTg[p][:, b * T:(b + 1) * T], wv[:, :], start=True, stop=True)
                mm.then_inc(s("v_ps"), 1)

            def gates(g):
                pe.wait_ge(s("zT_ready"), g + 1)
                for b in range(GB):
                    mm = pe.matmul(psG[:, b * E:(b + 1) * E], zT[:, b * T:(b + 1) * T], g2[:, :], start=True, stop=True)
                mm.then_inc(s("g_ps"), 1)

            def level(g, l):
                pe.wait_ge(s("LR_ready"), (NL + 1) * g + l + 1)
                if l >= 2:
                    pe.wait_ge(s("A_taken"), (NL + 2) * g + l - 1)
                for b in range(GB):
                    mm = pe.matmul(psA[l % 2][:, b * T:(b + 1) * T], Lk[l][:, b * T:(b + 1) * T], Rq[l][:, b, :, :], start=True, stop=True)
                mm.then_inc(s("A_ps"), 1)

            def leaves(g):
                pe.wait_ge(s("LR_ready"), (NL + 1) * g + NL + 1)
                for j in range(2):
                    pe.wait_ge(s("A_taken"), (NL + 2) * g + NL + j - 1)
                    for b in range(2):
                        bb = 2 * j + b
                        mm = pe.matmul(psA[j][:, b * 2 * T:(b + 1) * 2 * T], Lk[NL][:, bb * T:(bb + 1) * T], Rleaf[:, bb, :, :], start=True, stop=True)
                    mm.then_inc(s("A_ps"), 1)

            def values(g, p):
                pe.wait_ge(s("A_taken"), (NL + 2) * (g + 1))
                for b in range(GB):
                    for h in range(H):
                        c = b * E + h * DH
                        mm = pe.matmul(psO[:, c:c + DH], AT[:, b, h, :], v[p][:, c:c + DH], start=True, stop=True)
                mm.then_inc(s("o_ps"), 1)

            def turn(g):
                pe.wait_ge(s("on_ready"), g + 1)
                for b in range(GB):
                    mm = pe.transpose(psT[:, b * T:(b + 1) * T], on[:, b * E:(b + 1) * E], ident[:, :])
                mm.then_inc(s("oT_ps"), 1)

            def project_out(g):
                pe.wait_ge(s("oT_ready"), g + 1)
                for b in range(GB):
                    mm = pe.matmul(psY[:, b * E:(b + 1) * E], oT[:, b * T:(b + 1) * T], won[:, :], start=True, stop=True)
                mm.then_inc(s("y_ps"), 1)

            pe.wait_ge(s("weights_in"), WN)
            pe.wait_ge(s("pool_setup"), setup_steps["masks"])
            pe.wait_ge(s("won_ready"), 1)
            project_in(0, 0, 16, first=True)
            gates(0)

            def step(g, p, half, attend=True, project=True, finish=True):
                if attend:
                    level(g, 0)
                    level(g, 1)
                if finish:
                    turn(g - 1)
                if attend:
                    level(g, 2)
                if project:
                    project_in(g + 1, 1 - p, 16 * (half + p) + 16)
                if finish:
                    project_out(g - 1)
                if attend:
                    level(g, 3)
                if attend:
                    leaves(g)
                if project:
                    gates(g + 1)
                if attend:
                    values(g, p)

            groups(pe, step)

            psF, psQx, psD, psL1, psV, psL2, psT = banks[0], banks[1], banks[2], banks[3], banks[4], banks[5:7], banks[7]
            pe.wait_ge(s("pool_setup"), setup_steps["cross"])
            pe.wait_ge(s("wqs_ready"), 2)
            pe.wait_ge(s("x1_ready"), NG)

            def front(i, c):
                b, p = 4 * i + c, c % 4
                pe.wait_ge(s(f"cross_in{p}"), 32 * (i + c // 4) + 32)
                free(pe, "F_ready", b)
                pe.transpose(psF[:, 0:E], x1s[p][:, :], ident[:, :])
                pe.matmul(psF[:, E:E + C], cwq[:, :], ctxs[p][:, :], start=True, stop=True)
                pe.matmul(psF[:, E + C:E + 2 * C], wks[:, :, :].rearrange("p r d -> p (r d)"), ctxs[p][:, :], start=True, stop=True)
                pe.matmul(psF[0:C, FW:FW + DX], ctxs[p][:, :], cwkvT[:, DX:2 * DX], start=True, stop=True).then_inc(s("F_ps"), 1)

            def queries(i, c):
                b, p = 4 * i + c, c % 4
                pe.wait_ge(s("F_ready"), b + 1)
                free(pe, "qlo_ready", b)
                for j in range(NQ):
                    mm = pe.matmul(psQx[0:96, j * T:(j + 1) * T], wqs[:, j, :, :].rearrange("p r d -> p (r d)"), Fs[p][:, 0:E], start=True, stop=True)
                mm.then_inc(s("Qx_ps"), 1)

            def greatest(i, c, j):
                b, p = 4 * i + c, c % 4
                pe.wait_ge(s("bd_ready"), b + 1)
                pe.wait_ge(s("qlo_ready"), b + 1)
                free(pe, "mx_ready", NQ * b + j)
                pe.matmul(psL1[:, 0:QD * C], qs[p][:, j, :], bd[p][:, :, :].rearrange("p h c -> p (h c)"), start=True, stop=True).then_inc(s("L1_ps"), 1)

            def maxrows(i, c):
                b, p = 4 * i + c, c % 4
                pe.wait_ge(s("mx_ready"), NQ * b + NQ)
                free(pe, "E_ready", NQ * b - 1)
                for j in range(NQ):
                    mm = pe.matmul(psL2[0][96:96 + QD, j * T:(j + 1) * T], mx16[p % 2][:, QD * j:QD * j + QD], ident16[:, :], start=True, stop=True)
                mm.then_inc(s("M_ps"), 1)

            def logits(i, c, j):
                b, p = 4 * i + c, c % 4
                pe.wait_ge(s("qmax_ready"), b + 1)
                free(pe, "E_ready", NQ * b + j - 1)
                for h in range(QD):
                    mm = pe.matmul(psL2[j % 2][0:C, h * T:(h + 1) * T], bd[p][:, h, :], qs[p][:, j, :], start=True, stop=True)
                mm.then_inc(s("L2_ps"), 1)

            def values(i, c, half):
                b, p = 4 * i + c, c % 4
                pe.wait_ge(s("E_ready"), NQ * b + NQ)
                free(pe, "outT_ready", b)
                for j in range(2 * half, 2 * half + 2):
                    mm = pe.matmul(psV[32 * j:32 * j + 32, :], w9[p][:, :], Ex[p % 2][:, j, :], start=True, stop=True)
                if half:
                    mm.then_inc(s("V_ps"), 1)

            def back(i, c):
                b = 4 * i + c
                pe.wait_ge(s("outT_ready"), b + 1)
                for h in range(QD):
                    mm = pe.matmul(psD[:, c_av + h * NQ * KV:c_av + (h + 1) * NQ * KV], outT[:, h * T:(h + 1) * T], picks[:, :, :].rearrange("p j v -> p (j v)"), start=True, stop=True)
                return mm

            def selection(i, c):
                b, p = 4 * i + c, c % 4
                pe.wait_ge(s("onehot_ready"), b + 1)
                pe.matmul(psD[:, c_n:c_n + C], ones16[:, :], onehot[p % 2][:, :], start=True, stop=True)
                return pe.matmul(psD[0:C, c_n1:c_n1 + 1], onehot[p % 2][:, :], ones16[:, 0:1], start=True, stop=True)

            def bank_left(i, c):
                t = 4 * i + c
                if there(i, c - 2):
                    pe.wait_ge(s("at_ready"), t - 1)
                elif there(i, c - 3):
                    pe.wait_ge(s("tail_steps"), 2 * (t - 3) + 1)
                elif there(i, c + 2):
                    pe.wait_ge(s("select_steps"), 3 * (t + 2) + 2)
                elif there(i, c - 5):
                    pe.wait_ge(s("slot_e_ready"), t - 4)

            def turn(i, c):
                b, p = 4 * i + c, c % 4
                pe.wait_ge(s("at_ready"), b + 1)
                free(pe, "aT_ready", b)
                pe.transpose(psT[:, 0:E], at[p % 2][:, :], ident[:, :]).then_inc(s("aT_ps"), 1)

            def route_turn(i, c):
                b, p = 4 * i + c, c % 4
                pe.wait_ge(s("x2_ready"), b + 1)
                free(pe, "x2T_ready", b)
                if there(i, c + 1):
                    pe.wait_ge(s("aT_ready"), b + 2)
                pe.transpose(psT[:, E:E + T], xrow[p][:, 0, 0:E], ident[:, :]).then_inc(s("x2T_ps"), 1)

            def step(i, c):
                t = 4 * i + c
                if there(i, c - 1):
                    maxrows(i, c - 1)
                if there(i, c + 3):
                    front(i, c + 3)
                if there(i, c - 1):
                    logits(i, c - 1, 0)
                if there(i, c - 2):
                    values(i, c - 2, 0)
                    values(i, c - 2, 1)
                if there(i, c):
                    greatest(i, c, 0)
                if there(i, c - 3):
                    turn(i, c - 3)
                if there(i, c - 1):
                    logits(i, c - 1, 1)
                if there(i, c):
                    greatest(i, c, 1)
                last = None
                bank_left(i, c - 1)
                if there(i, c + 2):
                    pe.wait_ge(s("F_ready"), t + 3)
                    p = (c + 2) % 4
                    last = pe.matmul(psD[:, c_s:c_s + C], Fs[p][:, 0:E], Fs[p][:, E:E + C], start=True, stop=True)
                    queries(i, c + 2)
                if there(i, c):
                    greatest(i, c, 2)
                if there(i, c - 1):
                    logits(i, c - 1, 2)
                if there(i, c + 1):
                    last = selection(i, c + 1)
                if there(i, c - 3):
                    pe.wait_ge(s("aT_ready"), t - 2)
                    last = pe.matmul(psD[:, c_y2:c_y2 + E], aT[:, :], cwcT[:, :], start=True, stop=True)
                if there(i, c - 2):
                    last = back(i, c - 2)
                if there(i, c):
                    greatest(i, c, 3)
                if there(i, c - 4):
                    route_turn(i, c - 4)
                if there(i, c - 1):
                    logits(i, c - 1, 3)
                if there(i, c - 5):
                    pe.wait_ge(s("chosen_ready"), t - 4)
                    pe.matmul(psD[:, c_rk:c_rk + NE], upper16[:, :], chosen[:, :], start=True, stop=False)
                    last = pe.matmul(psD[:, c_rk:c_rk + NE], ones16[:, :], before[:, :], start=False, stop=True)
                if there(i, c - 4):
                    pe.wait_ge(s("x2T_ready"), t - 3)
                    last = pe.matmul(psD[:, c_lg:c_lg + NE], x2Tb[:, :], rw[:, :], start=True, stop=True)
                if last:
                    last.then_inc(s("bank_ps"), 1)
                else:
                    pe.sem_inc(s("bank_ps"), 1)

            steps(pe, step)

            psC = banks[0]
            pe.wait_ge(s("before_ready"), B + 1)
            pe.matmul(psC[:, 0:NE], ones16[:, :], before[:, :], start=True, stop=True).then_inc(s("count_ps"), 1)

            psX, psH, psY3 = banks[0:2], banks[2:5], banks[5:8]
            pe.wait_ge(s("E_ready"), NQ * B)
            pe.wait_ge(s("tables"), 1)

            def turn_in(i, loaded, p):
                pe.wait_ge(s(f"x_row_in{p}"), loaded)
                if not (isinstance(i, int) and i < 2):
                    pe.wait_ge(s("xinT_ready"), i - 1)
                pe.transpose(psX[p % 2][:, 0:P], xin[p][:, 0:E], ident[:, :]).then_inc(s("xinT_ps"), 1)

            def hidden(i, p):
                pe.wait_ge(s("xinT_ready"), i + 1)
                pe.wait_ge(s("w_ready"), i + 1)
                if not (isinstance(i, int) and i < 3):
                    pe.wait_ge(s("hid_ready"), NI * (i - 2))
                for c in range(NI):
                    mm = pe.matmul(psH[p % 3][:, c * P:(c + 1) * P], wcur[p % QUAD][:, c * P:(c + 1) * P], xinT[p % 4][:, :], start=True, stop=True)
                mm.then_inc(s("hid_ps"), 1)

            def outputs(i, p):
                pe.wait_ge(s("hid_ready"), NI * (i + 1))
                pe.wait_ge(s("y_ready"), i + 1)
                for c in range(NI):
                    mm = pe.matmul(psY3[p % 3][:, 0:E], hid[p % 3][:, c, :], wcur[p % QUAD][:, I + c * E:I + (c + 1) * E], start=(c == 0), stop=(c == NI - 1))
                mm.then_inc(s("result_ps"), 1)

            for i in range(LEAD_T):
                turn_in(i, 16, i)
            for i in range(LEAD_H):
                hidden(i, i)
            with pe.Fori(0, NT // UNROLL) as i:
                for d in range(UNROLL):
                    turn_in(UNROLL * i + d + LEAD_T, 16 * (i + (d + LEAD_T) // UNROLL) + 16, (d + LEAD_T) % UNROLL)
                    hidden(UNROLL * i + d + LEAD_H, (d + LEAD_H) % UNROLL)
                    outputs(UNROLL * i + d, d)

        @block.scalar
        def _(act):
            psQ, psV, psG, psZ, psT = banks[1], banks[2], banks[3], banks[3], banks[7]
            act.preload_act_table_set("natural_log_exp_and_others")
            act.wait_ge(s("weights_in"), WN)

            def project_in(g, p):
                act.wait_ge(s("z_ps"), g + 1)
                act.activation(zT[:, :], psZ[0:DH, :], ACT.Copy).then_inc(s("zT_ready"), 1)
                act.wait_ge(s("u_ready"), g + 1)
                act.activation(soft[:, :], uS[:, :], ACT.Exp, scale=-1.0).then_inc(s("act_chain"), 1)
                act.wait_ge(s("qc_ready"), g + 1)
                act.activation(sq_[:, :], qc[:, :], ACT.Exp, scale=-1.0).then_inc(s("act_chain"), 1)
                act.wait_ge(s("act_chain"), 6 * g + 1)
                act.activation(soft[:, :], soft[:, :], ACT.Ln, bias=1.0).then_inc(s("soft_ready"), 1)
                act.wait_ge(s("act_chain"), 6 * g + 2)
                act.activation(sq_[:, :], sq_[:, :], ACT.Ln, bias=1.0).then_inc(s("act_chain"), 1)
                act.wait_ge(s("v_ps"), g + 1)
                act.activation(v[p][:, :], psV[:, :], ACT.Copy).then_inc(s("v_ready"), 1)
                act.wait_ge(s("act_chain"), 6 * g + 3)
                act.activation(sq_[:, :], sq_[:, :], ACT.Exp, scale=-1.0).then_inc(s("sigq_ready"), 1)
                act.wait_ge(s("kk_ready"), 2 * g + 1)
                act.activation(k[:, :], kk[:, :], ACT.Exp, scale=-1.0).then_inc(s("k_ready"), 1)

            def value_gates(g, p):
                act.wait_ge(s("gc_ready"), g + 1)
                act.activation(sg_[:, :], gc[:, :], ACT.Exp, scale=-1.0).then_inc(s("act_chain"), 1)
                act.wait_ge(s("act_chain"), 6 * g + 4)
                act.activation(sg_[:, :], sg_[:, :], ACT.Ln, bias=1.0).then_inc(s("act_chain"), 1)
                act.wait_ge(s("act_chain"), 6 * g + 5)
                act.activation(gate[p][:, :], sg_[:, :], ACT.Exp, scale=-1.0).then_inc(s("gate_ready"), 1)
                act.sem_inc(s("act_chain"), 1)

            def decay(g, l):
                if l == NL:
                    act.wait_ge(s("kk_ready"), 2 * g + 2)
                else:
                    act.wait_ge(s("dec_ready"), NL * g + l + 1)
                if l == NL:
                    act.activation(decK[:, :], dec[l][:, :], ACT.Exp).then_inc(s("decK_exp"), 1)
                act.activation(dec[l][:, :], dec[l][:, :], ACT.Exp, scale=-1.0).then_inc(s("dec_exp"), 1)

            def squares(g):
                act.wait_ge(s("og_ready"), g + 1)
                act.activation(osq[:, :], og[:, :], ACT.Square).then_inc(s("osq_ready"), 1)

            def head_scales(g):
                act.wait_ge(s("ss_ready"), g + 1)
                act.activation(lss[:, :], ss[:, :], ACT.Ln, bias=EPS, scale=1.0 / DH).then_inc(s("log_steps"), 1)
                act.wait_ge(s("log_steps"), 2 * g + 1)
                act.activation(rss[:, :], lss[:, :], ACT.Exp, scale=-0.5).then_inc(s("rss_ready"), 1)

            def turned(g):
                act.wait_ge(s("oT_ps"), g + 1)
                act.activation(oT[:, :], psT[:, :], ACT.Copy).then_inc(s("oT_ready"), 1)

            def scales(g):
                act.wait_ge(s("mv1_ready"), g + 1)
                act.activation(ln1[:, :], mv1[:, :, 1], ACT.Ln, bias=EPS).then_inc(s("log_steps"), 1)
                act.wait_ge(s("log_steps"), 2 * g + 2)
                act.activation(rs1[:, :], ln1[:, :], ACT.Exp, scale=-0.5).then_inc(s("rs1_ready"), 1)

            def step(g, p, half, attend=True, project=True, finish=True):
                if attend:
                    for l in range(NL):
                        decay(g, l)
                if finish:
                    squares(g - 1)
                if attend:
                    decay(g, NL)
                if finish:
                    head_scales(g - 1)
                    turned(g - 1)
                if project:
                    project_in(g + 1, 1 - p)
                if finish:
                    scales(g - 1)
                if project:
                    value_gates(g + 1, 1 - p)
                if finish:
                    normal(g - 1)

            def normal(g):
                act.wait_ge(s("nm1_ready"), g + 1)
                pause(act)
                for b in range(GB):
                    dst = X[:, :, :].rearrange("p b e -> p (b e)")[:, bass.ds(g * GC + b * E, E)]
                    ins = act.activation(dst, r1[:, b * E:(b + 1) * E], ACT.Identity, scale=rs1[:, b:b + 1], bias=nm1[:, b:b + 1])
                ins.then_inc(s("x1_ready"), 1)

            project_in(0, 0)
            value_gates(0, 0)
            groups(act, step)

            psF, psQx, psV, psL2, psT = banks[0], banks[1], banks[4], banks[5:7], banks[7]

            def scales(i, c):
                b, p = 4 * i + c, c % 4
                act.wait_ge(s("mv2_ready"), b + 1)
                free(act, "rs2_ready", b)
                act.activation(ln2[:, :], mv2[p % 2][:, 1:2], ACT.Ln, bias=EPS).then_inc(s("ln2_ready"), 1)
                act.wait_ge(s("ln2_ready"), b + 1)
                act.activation(rs2[p % 2][:, :], ln2[:, :], ACT.Exp, scale=-0.5).then_inc(s("rs2_ready"), 1)

            def front(i, c):
                b, p = 4 * i + c, c % 4
                act.wait_ge(s("F_ps"), b + 1)
                free(act, "bd_ready", b - 3)
                free(act, "bank_ps", b - 4)
                act.activation(mv9[p][:, 0:DX], psF[0:C, FW:FW + DX], ACT.Copy)
                act.activation(Fs[p][:, :], psF[:, 0:FW], ACT.Copy).then_inc(s("F_ready"), 1)

            def queries(i, c):
                b, p = 4 * i + c, c % 4
                act.wait_ge(s("Qx_ps"), b + 1)
                free(act, "L2_ps", NQ * (b - 3))
                act.activation(qs[p][0:96, :, :].rearrange("p j t -> p (j t)"), psQx[0:96, :], ACT.Copy).then_inc(s("qhi_ready"), 1)

            def maxrows(i, c):
                b, p = 4 * i + c, c % 4
                act.wait_ge(s("M_ps"), b + 1)
                act.activation(qs[p][96:96 + QD, :, :].rearrange("p j t -> p (j t)"), psL2[0][96:96 + QD, :], ACT.Copy).then_inc(s("qmax_ready"), 1)

            def weights(i, c, j):
                b, p = 4 * i + c, c % 4
                act.wait_ge(s("L2_ps"), NQ * b + j + 1)
                free(act, "V_ps", b - 1)
                act.activation(Ex[p % 2][:, j, :], psL2[j % 2][0:C, :], ACT.Exp).then_inc(s("E_ready"), 1)

            def values(i, c):
                b = 4 * i + c
                act.wait_ge(s("V_ps"), b + 1)
                free(act, "bank_ps", b - 1 + 3 - FIRST)
                act.activation(outT[:, :], psV[:, :], ACT.Copy).then_inc(s("outT_ready"), 1)

            def turned(i, c):
                b, p = 4 * i + c, c % 4
                act.wait_ge(s("aT_ps"), b + 1)
                free(act, "mv2_ready", b)
                act.activation(aT[:, :], psT[:, 0:E], ACT.Copy).then_inc(s("aT_ready"), 1)

            def route(i, c):
                b, p = 4 * i + c, c % 4
                act.wait_ge(s("x2T_ps"), b + 1)
                free(act, "chosen_ready", b)
                act.activation(x2Tb[:, :], psT[:, E:E + T], ACT.Copy).then_inc(s("x2T_ready"), 1)

            def step(i, c):
                if there(i, c - 1):
                    maxrows(i, c - 1)
                if there(i, c + 3):
                    front(i, c + 3)
                if there(i, c - 1):
                    weights(i, c - 1, 0)
                if there(i, c - 2):
                    values(i, c - 2)
                if there(i, c - 3):
                    turned(i, c - 3)
                if there(i, c - 1):
                    weights(i, c - 1, 1)
                if there(i, c - 4):
                    scales(i, c - 4)
                if there(i, c + 2):
                    queries(i, c + 2)
                if there(i, c - 1):
                    weights(i, c - 1, 2)
                if there(i, c - 4):
                    route(i, c - 4)
                if there(i, c - 1):
                    weights(i, c - 1, 3)

            steps(act, step)

            psX, psH = banks[0:2], banks[2:5]
            act.wait_ge(s("table_steps"), PAD_STEPS)
            pad_rows(act, 1)
            act.wait_ge(s("gates0"), 1)
            act.activation(gates[:, :, :].rearrange("p b k -> p (b k)"), gates[:, :, :].rearrange("p b k -> p (b k)"), ACT.Exp).then_inc(s("gates1"), 1)
            act.preload_act_table_set("gelu_and_others")

            def turned(i, p):
                act.wait_ge(s("xinT_ps"), i + 1)
                if not (isinstance(i, int) and i < 4):
                    act.wait_ge(s("hid_ps"), i - 3)
                act.activation(xinT[p % 4][:, :], psX[p % 2][:, 0:P], ACT.Copy).then_inc(s("xinT_ready"), 1)

            def hidden(i, p):
                act.wait_ge(s("hid_ps"), i + 1)
                if not (isinstance(i, int) and i < 3):
                    act.wait_ge(s("result_ps"), i - 2)
                for c in range(NI):
                    act.activation(hid[p % 3][:, c, :], psH[p % 3][:, c * P:(c + 1) * P], ACT.Gelu,
                                   bias=wcur[p % QUAD][:, 2 * I + c:2 * I + c + 1]).then_inc(s("hid_ready"), 1)

            for i in range(LEAD_T):
                turned(i, i)
            for i in range(LEAD_H):
                hidden(i, i)
            with act.Fori(0, NT // UNROLL) as i:
                for d in range(UNROLL):
                    turned(UNROLL * i + d + LEAD_T, (d + LEAD_T) % UNROLL)
                    hidden(UNROLL * i + d + LEAD_H, (d + LEAD_H) % UNROLL)
            act.preload_act_table_set("natural_log_exp_and_others")

            def finish3(f, p):
                act.wait_ge(s("mv3_ready"), FB * f + FB)
                if not (isinstance(f, int) and f < 1):
                    act.wait_ge(s("rs3_ready"), f)
                act.activation(ln3[:, :], mv3[p][:, :, 1], ACT.Ln, bias=EPS).then_inc(s("ln3_ready"), 1)
                act.wait_ge(s("ln3_ready"), f + 1)
                if not (isinstance(f, int) and f < 2):
                    act.wait_ge(s("x3_ready"), FB * (f - 1))
                act.activation(rs3[p][:, :], ln3[:, :], ACT.Exp, scale=-0.5).then_inc(s("rs3_ready"), 1)

            finish3(0, 0)
            finish3(1, 1)
            with act.Fori(1, NF // 2) as i:
                for p in range(2):
                    finish3(2 * i + p, p)

        @block.vector
        def _(dve):
            psU, psQ, psG = banks[0], banks[1], banks[3]
            psA = banks[4:6]
            psO, psY = banks[6], banks[7]
            dve.memset(before[:, :], 0.0).then_inc(s("before_ready"), 1)
            dve.memset(restart[:, :], 1.0).then_inc(s("dve_init"), 1)
            dve.memset(AT[:, :, :, :], 0.0).then_inc(s("dve_init"), 1)
            n = 2
            for t in Lk:
                dve.memset(t[:, :], 0.0).then_inc(s("dve_init"), 1)
                n += 1
            for t in [*Rq, Rleaf]:
                dve.memset(t[:, :, :, :], 0.0).then_inc(s("dve_init"), 1)
                n += 1
            dve.wait_ge(s("dve_init"), n)
            dve.memset(restart[:, :].rearrange("p (b t) -> p b t", t=T)[:, :, 0:1], 0.0).then_inc(s("dve_init"), 1)
            dve.wait_ge(s("weights_in"), WN)
            dve.tensor_scalar(won[:, :], wo[:, :], norm_w[:, 0:1], None, ALU.mult).then_inc(s("won_ready"), 1)
            dve.wait_ge(s("dve_init"), n + 1)
            dve.wait_ge(s("pool_setup"), setup_steps["masks"])
            dve.wait_ge(s("x_in"), 16)

            def project_1(g):
                dve.wait_ge(s("u_ps"), g + 1)
                if not (isinstance(g, int) and g == 0):
                    dve.wait_ge(s("kk_ready"), 2 * g - 1)
                dve.tensor_scalar(uS[:, :], psU[:, :], delta[:, 0:1], -FLOOR, ALU.add, ALU.max).then_inc(s("u_ready"), 1)
                dve.wait_ge(s("q_ps"), g + 1)
                dve.tensor_scalar(qc[:, :], psQ[:, :], -40.0, None, ALU.max).then_inc(s("qc_ready"), 1)

            def project_2(g):
                dve.wait_ge(s("soft_ready"), g + 1)
                if not (isinstance(g, int) and g == 0):
                    dve.wait_ge(s("kk_ready"), 2 * g)
                dve.tensor_tensor_scan(N[:, :], restart[:, :], soft[:, :], 0.0, ALU.mult, ALU.add).then_inc(s("scan_steps"), 1)

            def project_3(g):
                dve.wait_ge(s("g_ps"), g + 1)
                dve.tensor_scalar(gc[:, :], psG[:, :], -40.0, None, ALU.max).then_inc(s("gc_ready"), 1)

            def project_4(g):
                dve.wait_ge(s("sigq_ready"), g + 1)
                dve.tensor_tensor(q[:, :], qc[:, :], sq_[:, :], ALU.mult).then_inc(s("scan_steps"), 1)

            def decay(g, l):
                h = HALVES[l]
                nb = GC // (2 * h)
                n4 = N[:, :].rearrange("p (b s r) -> p b s r", s=2, r=h)
                d4 = dec[l][:, :].rearrange("p (b s r) -> p b s r", s=2, r=h)
                anchor = n4[:, :, 0, h - 1:h].to_broadcast([P, nb, h])
                dve.tensor_tensor(d4[:, :, 1, :], n4[:, :, 1, :], anchor, ALU.subtract)
                dve.tensor_tensor(d4[:, :, 0, :], anchor, n4[:, :, 0, :], ALU.subtract).then_inc(s("dec_ready"), 1)

            def weigh(g, l):
                dve.wait_ge(s("dec_exp"), (NL + 1) * g + l + 1)
                if l == NL:
                    dve.wait_ge(s("decK_exp"), g + 1)
                    dve.tensor_tensor(Lk[NL][:, :], k[:, :], decK[:, :], ALU.mult)
                    for hd in range(H):
                        hp = slice(hd * DH, (hd + 1) * DH)
                        qv, dv = (t[hp, :].rearrange("p (b t) -> p b t", b=GB) for t in (q, dec[NL]))
                        ins = dve.tensor_tensor(Rleaf[hp, :, hd, :], qv, dv, ALU.mult)
                    ins.then_inc(s("LR_ready"), 1)
                    return
                h = HALVES[l]
                k4, d4, L4 = (t[:, :].rearrange("p (b s r) -> p b s r", s=2, r=h) for t in (k, dec[l], Lk[l]))
                dve.tensor_tensor(L4[:, :, 0, :], k4[:, :, 0, :], d4[:, :, 0, :], ALU.mult)
                for hd in range(H):
                    hp = slice(hd * DH, (hd + 1) * DH)
                    out_ = Rq[l][hp, :, hd, :].rearrange("p b (n r) -> p b n r", r=h)
                    qv, dv = (t[hp, :].rearrange("p (b n s r) -> p b n s r", b=GB, s=2, r=h)[:, :, :, 1, :] for t in (q, dec[l]))
                    ins = dve.tensor_tensor(out_, qv, dv, ALU.mult)
                ins.then_inc(s("LR_ready"), 1)

            def take(g, l):
                dve.wait_ge(s("A_ps"), (NL + 2) * g + l + 1)
                if l:
                    dve.wait_ge(s("A_taken"), (NL + 2) * g + l)
                if l < NL:
                    h = HALVES[l]
                    nb = T // (2 * h)
                    dst = AT[:, :, :, :].rearrange("p b d (n s r) -> p (b d) n s r", s=2, r=h)[:, :, :, 1, :]
                    src = psA[l % 2][:, :].rearrange("p (m n r) -> p m n r", n=nb, r=h)
                    msk = lmask[l][:, :].bitcast(U32).rearrange("p (n r) -> p n r", r=h).unsqueeze(1).to_broadcast([P, GB * H, nb, h])
                else:
                    j = l - NL
                    dst = AT[:, 2 * j:2 * j + 2, :, :].rearrange("p b d t -> p (b d) t")
                    src = psA[j][:, :].rearrange("p (m t) -> p m t", t=T)
                    msk = leafmask[:, :].bitcast(U32).unsqueeze(1).to_broadcast([P, 4, T])
                pause(dve)
                dve.copy_predicated(dst, msk, src).then_inc(s("A_taken"), 1)

            def gated(g, p):
                dve.wait_ge(s("o_ps"), g + 1)
                dve.wait_ge(s("gate_ready"), g + 1)
                dve.tensor_tensor(og[:, :], psO[:, :], gate[p][:, :], ALU.mult).then_inc(s("og_ready"), 1)

            def square_sums(g):
                dve.wait_ge(s("osq_ready"), g + 1)
                dve.tensor_reduce(ss[:, :], osq[:, :].rearrange("p (m d) -> p m d", d=DH), AX.X, ALU.add).then_inc(s("ss_ready"), 1)

            def head_norm(g):
                dve.wait_ge(s("rss_ready"), g + 1)
                dve.tensor_tensor(on[:, :].rearrange("p (m d) -> p m d", d=DH), og[:, :].rearrange("p (m d) -> p m d", d=DH),
                                  rss[:, :].unsqueeze(2).to_broadcast([P, GB * H, DH]), ALU.mult).then_inc(s("on_ready"), 1)

            def residual(g):
                dve.wait_ge(s("y_ps"), g + 1)
                if not (isinstance(g, int) and g == 0):
                    dve.wait_ge(s("x1_ready"), g)
                xg = X[:, :, :].rearrange("p b e -> p (b e)")[:, bass.ds(g * GC, GC)]
                dve.tensor_tensor(r1[:, :], psY[:, :], xg, ALU.add).then_inc(s("norm_steps"), 1)

            def moments(g):
                dve.wait_ge(s("norm_steps"), 2 * g + 1)
                for b in range(GB):
                    ins = dve.bn_stats(st1[:, b, :], r1[:, b * E:(b + 1) * E])
                ins.then_inc(s("norm_steps"), 1)

            def combined(g):
                dve.wait_ge(s("norm_steps"), 2 * g + 2)
                pause(dve)
                for b in range(GB):
                    ins = dve.bn_aggr(mv1[:, b, :], st1[:, b, :])
                ins.then_inc(s("mv1_ready"), 1)

            def shift(g):
                dve.wait_ge(s("rs1_ready"), g + 1)
                dve.scalar_tensor_tensor(nm1[:, :], mv1[:, :, 0], -1.0, rs1[:, :], ALU.mult, ALU.mult).then_inc(s("nm1_ready"), 1)

            def step(g, p, half, attend=True, project=True, finish=True):
                if attend:
                    dve.wait_ge(s("scan_steps"), 2 * g + 1)
                    for l in range(NL):
                        decay(g, l)
                if finish:
                    gated(g - 1, 1 - p)
                if attend:
                    dve.wait_ge(s("k_ready"), g + 1)
                    dve.wait_ge(s("scan_steps"), 2 * g + 2)
                    weigh(g, 0)
                    weigh(g, 1)
                if finish:
                    square_sums(g - 1)
                if attend:
                    weigh(g, 2)
                    weigh(g, 3)
                if finish:
                    head_norm(g - 1)
                if attend:
                    take(g, 0)
                    weigh(g, NL)
                    take(g, 1)
                if project:
                    project_1(g + 1)
                if attend:
                    take(g, 2)
                if finish:
                    residual(g - 1)
                if attend:
                    take(g, 3)
                if finish:
                    moments(g - 1)
                if project:
                    project_2(g + 1)
                if finish:
                    combined(g - 1)
                if attend:
                    take(g, 4)
                if project:
                    project_3(g + 1)
                if attend:
                    take(g, 5)
                if project:
                    project_4(g + 1)
                if finish:
                    shift(g - 1)

            for r in range(3):
                ins = dve.tensor_copy(wqs[:, :, r, :], cwqT[:, :].rearrange("p (j d) -> p j d", j=NQ))
            ins.then_inc(s("wqs_ready"), 1)
            dve.tensor_scalar(wks[:, :, :], cwkvT[:, 0:DX].unsqueeze(1).to_broadcast([P, P // DX, DX]), SCALE, None, ALU.mult).then_inc(s("wqs_ready"), 1)
            project_1(0)
            project_2(0)
            project_3(0)
            project_4(0)
            groups(dve, step)

            psQx, psD, psL1 = banks[1], banks[2], banks[3]
            dve.wait_ge(s("pool_setup"), setup_steps["cross"])
            dve.tensor_scalar(baseE[:, :], capE[:, :], float(ROW), None, ALU.mult).then_inc(s("baseE_ready"), 1)
            dve.wait_ge(s("baseE_ready"), 1)

            def normal(i, c):
                b, p, q = 4 * i + c, c % 4, i + c // 4
                dve.wait_ge(s("rs2_ready"), b + 1)
                if not (isinstance(q, int) and q < 1):
                    dve.wait_ge(s(f"x2_saved{p}"), 16 * q)
                    dve.wait_ge(s(f"scattered{p}"), 16 * TOP * q)
                dve.tensor_scalar(xrow[p][:, :, 0:E], r2[p % 2][:, :].unsqueeze(1).to_broadcast([P, TOP, E]), mv2[p % 2][:, 0:1], rs2[p % 2][:, 0:1],
                                  ALU.subtract, ALU.mult).then_inc(s("x2_ready"), 1)
                dve.tensor_copy(xrow[p][:, :, E:RW].bitcast(U32), results[:, bass.ds(b, 1), :].rearrange("p b k -> p k b")).then_inc(s("row_to"), 1)

            def queries(i, c):
                b, p = 4 * i + c, c % 4
                dve.wait_ge(s("qhi_ready"), b + 1)
                dve.memset(qs[p][96:96 + QD, :, :], 0.0)
                lo = qs[p][64:96, :, :].rearrange("p j t -> p (j t)")
                dve.tensor_tensor(lo, psQx[64:96, :], lo, ALU.subtract).then_inc(s("qlo_ready"), 1)

            def maxima(i, c, j):
                b, p = 4 * i + c, c % 4
                dve.wait_ge(s("L1_ps"), NQ * b + j + 1)
                if j == 0:
                    free(dve, "M_ps", b - 1)
                dve.tensor_reduce(mx16[p % 2][:, QD * j:QD * j + QD], psL1[:, 0:QD * C].rearrange("p (h c) -> p h c", c=C), AX.X, ALU.max).then_inc(s("mx_ready"), 1)

            def step(i, c):
                t = 4 * i + c
                following = there(i, c + 1)
                dve.wait_ge(s("bank_ps"), t - FIRST + 1)
                pause(dve)
                select, select_n, select_p = there(i, c + 2), t + 2, (c + 2) % 4
                count, count_n, count_p = there(i, c + 1), t + 1, (c + 1) % 4
                value, value_n, value_p = there(i, c - 2), t - 2, (c - 2) % 4
                tail, tail_n, tail_p = there(i, c - 3), t - 3, (c - 3) % 4
                route, route_n = there(i, c - 4), t - 4
                place, place_n, place_p = there(i, c - 5), t - 5, (c - 5) % 4
                av = psD[:, c_av:c_av + NH * KV].rearrange("p (h j v) -> p h j v", h=QD, v=KV)
                scores = psD[:, c_s:c_s + C]
                if count:
                    free(dve, "bd_ready", count_n - 1)
                    dve.tensor_scalar(src[count_p % 2][96:128, :], psD[96:128, c_n:c_n + C], thr[96:128, 0:1], mult[96:128, 0:1], ALU.is_le, ALU.mult)
                    dve.tensor_scalar(w9[count_p][:, 0:KV], mv9[count_p][:, :], psD[0:C, c_n1:c_n1 + 1], None, ALU.mult).then_inc(s("aux_ready"), 1)
                if select:
                    free(dve, "select_steps", 3 * select_n)
                    pause(dve)
                    dve.max(top8[:, :], scores).then_inc(s("select_steps"), 1)
                if value:
                    free(dve, "at_ready", value_n)
                    dve.reciprocal(rden[:, :].rearrange("p (h j) -> p h j", h=QD), av[:, :, :, DX]).then_inc(s("rden_ready"), 1)
                if route:
                    free(dve, "route_steps", 4 * route_n)
                    dve.tensor_tensor(lgs[:, :], psD[:, c_lg:c_lg + NE], rb[:, :], ALU.add).then_inc(s("lgs_ready"), 1)
                if place:
                    free(dve, "place_steps", 2 * place_n)
                    dve.scalar_tensor_tensor(slot_e[:, :], psD[:, c_rk:c_rk + NE], float(ROW), baseE[:, :], ALU.mult, ALU.add).then_inc(s("slot_e_ready"), 1)
                if select:
                    dve.wait_ge(s("select_steps"), 3 * select_n + 1)
                    pause(dve)
                    dve.max_index(idx8[:, :], top8[:, :], scores).then_inc(s("select_steps"), 1)
                if tail:
                    free(dve, "x2_ready", tail_n - 1)
                    xb = X[:, :, :].rearrange("p b e -> p (b e)")[:, bass.ds(tail_n * E, E)]
                    dve.tensor_tensor(r2[tail_p % 2][:, :], psD[:, c_y2:c_y2 + E], xb, ALU.add).then_inc(s("tail_steps"), 1)
                if value:
                    dve.wait_ge(s("rden_ready"), value_n + 1)
                    free(dve, "aT_ps", value_n - 1)
                    dve.tensor_tensor(at[value_p % 2][:, :].rearrange("p (j h d) -> p h j d", h=QD, d=DX), av[:, :, :, 0:DX],
                                      rden[:, :].rearrange("p (h j) -> p h j", h=QD).unsqueeze(3).to_broadcast([P, QD, NQ, DX]),
                                      ALU.mult).then_inc(s("at_ready"), 1)
                if following:
                    maxima(i, c + 1, 0)
                if place:
                    dve.wait_ge(s("before_ready"), place_n + 1)
                    dve.tensor_tensor(before[:, :], before[:, :], chosen[:, :], ALU.add).then_inc(s("before_ready"), 1)
                    dve.wait_ge(s("slot_e_ready"), place_n + 1)
                    dve.tensor_tensor(slotsel[:, :, :], onehots[:, :, :], slot_e[:, :].unsqueeze(1).to_broadcast([P, TOP, NE]), ALU.mult).then_inc(s("place_steps"), 1)
                if select:
                    dve.wait_ge(s("select_steps"), 3 * select_n + 2)
                    dve.tensor_copy(idxf[:, :], idx8[:, 0:1]).then_inc(s("select_steps"), 1)
                if tail:
                    dve.wait_ge(s("tail_steps"), 2 * tail_n + 1)
                    dve.bn_stats(st2[:, :], r2[tail_p % 2][:, :]).then_inc(s("tail_steps"), 1)
                if route:
                    dve.wait_ge(s("lgs_ready"), route_n + 1)
                    pause(dve)
                    dve.max(rtop[:, :], lgs[:, :]).then_inc(s("route_steps"), 1)
                if place:
                    dve.wait_ge(s("place_steps"), 2 * place_n + 1)
                    dve.tensor_reduce(slotf[:, :], slotsel[:, :, :], AX.X, ALU.add).then_inc(s("place_steps"), 1)
                if select:
                    dve.wait_ge(s("select_steps"), 3 * select_n + 3)
                    dve.tensor_scalar(onehot[select_p % 2][:, :], iotaC[:, :], idxf[:, 0:1], None, ALU.is_equal).then_inc(s("onehot_ready"), 1)
                if tail:
                    dve.wait_ge(s("tail_steps"), 2 * tail_n + 2)
                    pause(dve)
                    dve.bn_aggr(mv2[tail_p % 2][:, :], st2[:, :]).then_inc(s("mv2_ready"), 1)
                if following:
                    maxima(i, c + 1, 1)
                if route:
                    dve.wait_ge(s("route_steps"), 4 * route_n + 1)
                    pause(dve)
                    dve.max_index(ridx[:, :], rtop[:, :], lgs[:, :]).then_inc(s("route_steps"), 1)
                    dve.tensor_copy(topl[:, bass.ds(route_n, 1), :], rtop[:, 0:TOP].unsqueeze(1)).then_inc(s("top_saved"), 1)
                if place:
                    dve.wait_ge(s("place_steps"), 2 * place_n + 2)
                    dve.wait_ge(s("row_to"), place_n + 1)
                    dve.tensor_copy(slots[place_p][:, :], slotf[:, :]).then_inc(s("slots_ready"), 1)
                if route:
                    dve.wait_ge(s("route_steps"), 4 * route_n + 2)
                    dve.tensor_copy(topi[:, :], ridx[:, 0:TOP]).then_inc(s("route_steps"), 1)
                    dve.wait_ge(s("route_steps"), 4 * route_n + 3)
                    dve.tensor_tensor(onehots[:, :, :], iotaE[:, :].unsqueeze(1).to_broadcast([P, TOP, NE]), topi[:, :].unsqueeze(2).to_broadcast([P, TOP, NE]),
                                      ALU.is_equal).then_inc(s("route_steps"), 1)
                    dve.wait_ge(s("route_steps"), 4 * route_n + 4)
                    with nc.allow_low_precision(reason="a sum of one at most"):
                        dve.tensor_reduce(chosen[:, :], onehots[:, :, :].rearrange("p k e -> p e k"), AX.X, ALU.add).then_inc(s("chosen_ready"), 1)
                if following:
                    maxima(i, c + 1, 2)
                if there(i, c - 3):
                    normal(i, c - 3)
                if following:
                    maxima(i, c + 1, 3)
                if there(i, c + 3):
                    queries(i, c + 3)

            steps(dve, step)

            psC = banks[0]
            chain = 0

            def then(ins):
                nonlocal chain
                chain += 1
                ins.then_inc(s("table_steps"), 1)
                dve.wait_ge(s("table_steps"), chain)

            dve.wait_ge(s("count_ps"), 1)
            then(dve.tensor_copy(count[:, :], psC[0:1, 0:NE]))
            then(dve.tensor_tensor(over[:, :, :], count[:, :].unsqueeze(2).to_broadcast([1, NE, JT]), steps128[:, :].unsqueeze(1).to_broadcast([1, NE, JT]), ALU.is_gt))
            then(dve.tensor_reduce(ntile[:, :], over[:, :, :], AX.X, ALU.add))
            then(dve.tensor_tensor_scan(last_tile[:, :], ones_e[:, :], ntile[:, :], 0.0, ALU.mult, ALU.add))
            then(dve.tensor_tensor(padf[:, :], count[:, :], capE[0:1, :], ALU.add))
            then(dve.tensor_copy(pad_at[:, :], padf[:, :]))
            for lo, hi in ((0, FIRST_TILES), (FIRST_TILES, NL_)):
                n, part = hi - lo, slice(lo, hi)
                then(dve.tensor_tensor(past[:, part, :], tile_no[:, part].unsqueeze(2).to_broadcast([1, n, NE]), last_tile[:, :].unsqueeze(1).to_broadcast([1, n, NE]), ALU.is_ge))
                then(dve.tensor_reduce(expert[:, part], past[:, part, :], AX.X, ALU.add))
                then(dve.tensor_tensor(past[:, part, :], past[:, part, :], ntile[:, :].unsqueeze(1).to_broadcast([1, n, NE]), ALU.mult))
                then(dve.tensor_reduce(done_t[:, part], past[:, part, :], AX.X, ALU.add))
                then(dve.tensor_tensor(rowf[:, part], tile_no[:, part], done_t[:, part], ALU.subtract))
                then(dve.tensor_scalar(rowf[:, part], rowf[:, part], float(P), None, ALU.mult))
                then(dve.tensor_scalar(colf[:, part], expert[:, part], float(CAP), None, ALU.mult))
                then(dve.tensor_tensor(rowf[:, part], rowf[:, part], colf[:, part], ALU.add))
                then(dve.tensor_scalar(tile_row[:, part], rowf[:, part], float(LAST), None, ALU.min))
                then(dve.tensor_scalar(tile_col[:, part], expert[:, part], float(NE - 1), float(WROW), ALU.min, ALU.mult))
                dve.sem_inc(s("tables"), 1)
            dve.wait_ge(s("top_saved"), B)
            dve.tensor_tensor(gates[:, :, :], topl[:, :, :], topl[:, :, 0:1].to_broadcast([P, B, TOP]), ALU.subtract).then_inc(s("gates0"), 1)
            dve.wait_ge(s("gates1"), 1)
            then(dve.tensor_reduce(gsum[:, :], gates[:, :, :], AX.X, ALU.add))
            then(dve.reciprocal(grec[:, :], gsum[:, :]))
            then(dve.tensor_tensor(gates[:, :, :], gates[:, :, :], grec[:, :].unsqueeze(2).to_broadcast([P, B, TOP]), ALU.mult))

            psY3 = banks[5:8]
            wrow = wall[:, :, :].rearrange("p e w -> p (e w)")
            dve.wait_ge(s("wall_in"), 16 * (NI + 3))
            dve.sem_inc(s("y_ready"), 3)

            def expert_weights(i, p, col):
                dve.tensor_copy(wcur[p % QUAD][:, :], wrow[:, bass.ds(dve.snap(col, min_val=0, max_val=(NE - 1) * WROW), WROW)]).then_inc(s("w_ready"), 1)

            def results_out(i, written, p):
                dve.wait_ge(s("result_ps"), i + 1)
                if written is not None:
                    dve.wait_ge(s(f"y_out{p}"), written)
                dve.wait_ge(s("w_ready"), i + 1)
                dve.tensor_tensor(yout[p][:, :], psY3[p % 3][:, 0:E], wcur[p % QUAD][:, 2 * I + NI:WROW], ALU.add).then_inc(s("y_ready"), 1)

            with ExitStack() as regs:
                col = [regs.enter_context(dve.register(f"col{j}")) for j in range(QUAD)]
                dve.reg_load(col, tile_col[0:1, 0:QUAD])
                for d in range(QUAD):
                    expert_weights(d, d, col[d])

                def tiles(i, written):
                    for d in range(UNROLL):
                        if d % QUAD == 0:
                            dve.reg_load(col, tile_col[0:1, bass.ds(UNROLL * i + d + QUAD, QUAD)])
                        results_out(UNROLL * i + d, written, d)
                        dve.wait_ge(s("y_ready"), UNROLL * i + d + 1 + 3)
                        expert_weights(UNROLL * i + d + QUAD, d, col[d % QUAD])

                tiles(0, None)
                with dve.Fori(1, NT // UNROLL) as i:
                    tiles(i, 16 * i)

            for p in range(4):
                dve.wait_ge(s(f"x2_saved{p}"), 16 * (B // 4))
            Xf = X[:, :, :].rearrange("p b e -> p (b e)")
            gf = gates[:, :, :].rearrange("p b k -> p (b k)")

            def gather(f, d, loaded):
                dve.wait_ge(s(f"y_in{d % 4}"), loaded)
                if not (isinstance(f, int) and f < 2):
                    dve.wait_ge(s("x3_ready"), FB * (f - 1))
                for j in range(TOP):
                    for c in range(FB):
                        r = r3[d % 2][:, c, :]
                        if j:
                            dve.wait_ge(s("r3_steps"), TOP * FB * f + (j - 1) * FB + c + 1)
                        prev = r if j else Xf[:, bass.ds((FB * f + c) * E, E)]
                        dve.scalar_tensor_tensor(r, yin[d % 4][:, c, j * E:(j + 1) * E], gf[:, bass.ds((FB * f + c) * TOP + j, 1)], prev,
                                                 ALU.mult, ALU.add).then_inc(s("r3_steps"), 1)

            def stats(f, d):
                for c in range(FB):
                    dve.wait_ge(s("r3_steps"), TOP * FB * f + (TOP - 1) * FB + c + 1)
                    dve.bn_stats(st3[d % 2][:, c, :], r3[d % 2][:, c, :]).then_inc(s("st3_ready"), 1)
                dve.sem_inc(s("r3_ready"), 1)

            def spread(f, d):
                for c in range(FB):
                    dve.wait_ge(s("st3_ready"), FB * f + c + 1)
                    pause(dve)
                    dve.bn_aggr(mv3[d % 2][:, c, :], st3[d % 2][:, c, :]).then_inc(s("mv3_ready"), 1)

            def norm(f, d, stored):
                dve.wait_ge(s("rs3_ready"), f + 1)
                if stored is not None:
                    dve.wait_ge(s(f"out{d % 2}"), stored)
                for c in range(FB):
                    dve.tensor_scalar(o3[d % 2][:, c, :], r3[d % 2][:, c, :], mv3[d % 2][:, c, 0:1], rs3[d % 2][:, c:c + 1],
                                      ALU.subtract, ALU.mult).then_inc(s("x3_ready"), 1)

            def end_step(f, d, loaded, stored):
                gather(f, d, loaded)
                stats(f, d)
                norm(f - 1, d - 1, stored)
                spread(f, d)

            gather(0, 0, 16)
            stats(0, 0)
            spread(0, 0)
            for f in (1, 2):
                end_step(f, f, 16, None)
            with dve.Fori(0, NF // 4 - 1) as i:
                for d in range(3, 7):
                    end_step(4 * i + d, d, 16 * (i + d // 4) + 16, 16 * (2 * i + (d - 1) // 2))
            end_step(NF - 1, 3, 16 * (NF // 4), 16 * (NF // 2 - 1))
            norm(NF - 1, 1, 16 * (NF // 2 - 1))


def layout(I):
    f = lambda a: np.ascontiguousarray(a)
    x = np.asarray(I["x"])
    B, T, E = x.shape
    return {
        "x": f(x.transpose(1, 0, 2)),
        "xT": f(x.reshape(B * T, E).T),
        "wk": f(I["L0_attn_Wk"]), "wq": f(I["L0_attn_Wq"]), "wv": f(I["L0_attn_Wv"]), "wo": f(I["L0_attn_Wo"]),
        "g1": f(I["L0_attn_G1"]), "g2": f(I["L0_attn_G2"]),
        "ctxT": f(np.asarray(I["ctx_1024"]).transpose(0, 2, 1)),
        "cwq": f(I["L0_xattn_Wq"]), "cwqT": f(np.asarray(I["L0_xattn_Wq"]).T), "cwkvT": f(np.asarray(I["L0_xattn_Wkv"]).T), "cwcT": f(np.asarray(I["L0_xattn_Wc"]).T),
        "rw": f(I["L0_ffn_router_w"]), "rb": f(np.broadcast_to(np.asarray(I["L0_ffn_router_b"]), (T, I["L0_ffn_router_b"].shape[0]))),
        "w1": f(I["L0_ffn_w1"]), "w2": f(I["L0_ffn_w2"]), 
        "b1T": f(np.asarray(I["L0_ffn_b1"]).reshape(I["L0_ffn_b1"].shape[0], -1, E).transpose(2, 0, 1)),
        "b2rep": f(np.broadcast_to(np.asarray(I["L0_ffn_b2"]), (E, *I["L0_ffn_b2"].shape))),
        "delta": f(I["L0_attn_delta"]).reshape(E, 1), "norm_w": f(I["L0_attn_norm_w"]).reshape(E, 1),
    }


def kernel(**inputs):
    laid = layout(inputs)
    B, T, E = np.asarray(inputs["x"]).shape
    nc = _bacc.Bacc("TRN2", target_bir_lowering=False, num_devices=1)
    A = {name: nc.dram_tensor(name + "_dram", a.shape, _mybir.dt.from_np(a.dtype), kind="ExternalInput").ap() for name, a in laid.items()}
    out = nc.dram_tensor("out_dram", (T, B, E), _mybir.dt.float32, kind="ExternalOutput").ap()
    build(nc, A, out)
    nc.compile()
    r = _run(nc, [{name + "_dram": a for name, a in laid.items()}], core_ids=[0])
    return np.ascontiguousarray(np.asarray(r.results[0]["out_dram"]).transpose(1, 0, 2))
```
